# Optimizing a Trainium2 kernel written in Bass

```python
import numpy as np
import jax
import jax.numpy as jnp

def _softmax(x, axis=-1):
    return jax.nn.softmax(x, axis=axis)

def _gelu(x):
    return jax.nn.gelu(x, approximate=True)

def _silu(x):
    return jax.nn.silu(x)

def _sigmoid(x):
    return jax.nn.sigmoid(x)

def _layernorm(x, axis=-1, eps=1e-05):
    m = jnp.mean(x, axis=axis, keepdims=True)
    v = jnp.var(x, axis=axis, keepdims=True)
    return (x - m) / jnp.sqrt(v + eps)

def _scatter_add(tgt, idx, src, axis=0):
    return tgt.at[idx].add(src)

def _segment_sum(src, seg, n):
    return jax.ops.segment_sum(src, seg, n)
kernel_name = 'mk_decoder_postln_d1_seqx_r4_461b4e'

def setup_inputs(seed: int=0):
    np.random.seed(seed)
    _w = jnp.asarray

    def _rec_inputs():
        import jax
        import jax.numpy as jnp
        _rk = jax.random.key(seed)
        x = 7.22e-05 + 1 * jax.random.normal(jax.random.fold_in(_rk, 1), (8, 256, 256), jnp.float32)
        _lenS = 256 - jax.random.randint(jax.random.fold_in(_rk, 7), (8,), 0, max(1, 256 // 4) + 1, jnp.int32)
        _lenS2 = 256 - jax.random.randint(jax.random.fold_in(_rk, 8), (8,), 0, max(1, 256 // 4) + 1, jnp.int32)
        _ctx_1024P = jax.random.normal(jax.random.fold_in(_rk, 11), (8, 16, 256), jnp.float32)
        _ctx_1024c = jax.random.dirichlet(jax.random.fold_in(_rk, 511), 0.3 * jnp.ones((16,), jnp.float32), (8, 256))
        _ctx_1024t = jnp.einsum('bsk,bkd->bsd', _ctx_1024c, _ctx_1024P)
        _ctx_1024t = _ctx_1024t * jax.lax.rsqrt(jnp.mean(jnp.square(_ctx_1024t)) + 1e-12) * 0.953939
        ctx_1024 = 4.13588e-05 + 0.999923 * (_ctx_1024t + 0.3 * jax.random.normal(jax.random.fold_in(_rk, 611), (8, 256, 256), jnp.float32))
        return (x, ctx_1024)
    x, ctx_1024 = _rec_inputs()

    def _L0_attn_setup():
        import jax, jax.numpy as jnp
        import numpy as np
        from jax import lax
        D_MODEL = 256
        D_STATE = 16
        D_CONV = 4
        EXPAND = 2
        D_INNER = EXPAND * D_MODEL
        DT_RANK = (D_MODEL + 15) // 16
        BATCH = 4
        SEQLEN = 256

        def _silu(x):
            return x * jax.nn.sigmoid(x)

        def _init_block(key):
            ks = jax.random.split(key, 5)
            s = 0.02
            in_proj_w = jax.random.normal(ks[0], (2 * D_INNER, D_MODEL), jnp.float32) * s
            conv_w = jax.random.normal(ks[1], (D_INNER, D_CONV), jnp.float32) * s
            conv_b = jnp.zeros((D_INNER,), jnp.float32)
            x_proj_w = jax.random.normal(ks[2], (DT_RANK + 2 * D_STATE, D_INNER), jnp.float32) * s
            dt_proj_w = jax.random.normal(ks[3], (D_INNER, DT_RANK), jnp.float32) * DT_RANK ** (-0.5)
            dt_proj_b = jnp.log(jnp.expm1(jnp.full((D_INNER,), 0.01, jnp.float32)))
            A_log = jnp.log(jnp.broadcast_to(jnp.arange(1, D_STATE + 1, dtype=jnp.float32), (D_INNER, D_STATE)))
            D_param = jnp.ones((D_INNER,), jnp.float32)
            out_proj_w = jax.random.normal(ks[4], (D_MODEL, D_INNER), jnp.float32) * s
            return (in_proj_w, conv_w, conv_b, x_proj_w, dt_proj_w, dt_proj_b, A_log, D_param, out_proj_w)

        def _mamba(x, in_proj_w, conv_w, conv_b, x_proj_w, dt_proj_w, dt_proj_b, A_log, D_param, out_proj_w):
            B, L, _ = x.shape
            xz = jnp.einsum('bld,ed->ble', x, in_proj_w)
            x_in, z = jnp.split(xz, 2, axis=-1)
            x_c = x_in.swapaxes(1, 2)
            x_c = lax.conv_general_dilated(x_c, conv_w[:, None, :], window_strides=(1,), padding=[(D_CONV - 1, 0)], feature_group_count=D_INNER, dimension_numbers=('NCH', 'OIH', 'NCH'))
            x_c = x_c + conv_b[None, :, None]
            u = _silu(x_c).swapaxes(1, 2)
            x_dbl = jnp.einsum('bld,ed->ble', u, x_proj_w)
            dt, Bm, Cm = jnp.split(x_dbl, [DT_RANK, DT_RANK + D_STATE], axis=-1)
            delta = jax.nn.softplus(jnp.einsum('blr,dr->bld', dt, dt_proj_w) + dt_proj_b)
            A = -jnp.exp(A_log)

            def step(h, inp):
                d_t, b_t, c_t, u_t = inp
                h = h * jnp.exp(d_t[:, :, None] * A) + (d_t * u_t)[:, :, None] * b_t[:, None, :]
                y = jnp.einsum('bdn,bn->bd', h, c_t)
                return (h, y)
            h0 = jnp.zeros((B, D_INNER, D_STATE), x.dtype)
            xs = (delta.swapaxes(0, 1), Bm.swapaxes(0, 1), Cm.swapaxes(0, 1), u.swapaxes(0, 1))
            _, ys = lax.scan(step, h0, xs)
            y = ys.swapaxes(0, 1) + u * D_param
            y = y * _silu(z)
            return jnp.einsum('bld,ed->ble', y, out_proj_w)

        def _reference_tuple_inner(hidden, diff, h_in_proj_w, h_conv_w, h_conv_b, h_x_proj_w, h_dt_proj_w, h_dt_proj_b, h_A_log, h_D_param, h_out_proj_w, d_in_proj_w, d_conv_w, d_conv_b, d_x_proj_w, d_dt_proj_w, d_dt_proj_b, d_A_log, d_D_param, d_out_proj_w):
            hidden_out = _mamba(hidden, h_in_proj_w, h_conv_w, h_conv_b, h_x_proj_w, h_dt_proj_w, h_dt_proj_b, h_A_log, h_D_param, h_out_proj_w)
            diff_out = _mamba(diff, d_in_proj_w, d_conv_w, d_conv_b, d_x_proj_w, d_dt_proj_w, d_dt_proj_b, d_A_log, d_D_param, d_out_proj_w)
            return (hidden_out, diff_out)
        key = jax.random.key(seed)
        k_h, k_d, k1, k2 = jax.random.split(key, 4)
        hidden = jax.random.normal(k_h, (BATCH, SEQLEN, D_MODEL), jnp.float32)
        diff = jax.random.normal(k_d, (BATCH, SEQLEN, D_MODEL), jnp.float32)
        hp = _init_block(k1)
        dp = _init_block(k2)
        names = ['in_proj_w', 'conv_w', 'conv_b', 'x_proj_w', 'dt_proj_w', 'dt_proj_b', 'A_log', 'D_param', 'out_proj_w']
        out = {'hidden': hidden, 'diff': diff}
        for n, v in zip(names, hp):
            out['h_' + n] = v
        for n, v in zip(names, dp):
            out['d_' + n] = v
        return out
    _L0_attn_all = _L0_attn_setup()
    _L0_attn_in = {k: v for k, v in _L0_attn_all.items() if k in ('diff', 'h_in_proj_w', 'h_conv_w', 'h_conv_b', 'h_x_proj_w', 'h_dt_proj_w', 'h_dt_proj_b', 'h_A_log', 'h_D_param', 'h_out_proj_w', 'd_in_proj_w', 'd_conv_w', 'd_conv_b', 'd_x_proj_w', 'd_dt_proj_w', 'd_dt_proj_b', 'd_A_log', 'd_D_param', 'd_out_proj_w')}
    del _L0_attn_all

    def _L0_xattn_setup():
        import jax, jax.numpy as jnp
        import numpy as np
        D_MODEL = 256
        D_FF = 1024
        LN_EPS = 1e-05

        def _layer_norm(x, gamma, beta):
            mu = jnp.mean(x, axis=-1, keepdims=True)
            var = jnp.var(x, axis=-1, keepdims=True)
            return (x - mu) * jax.lax.rsqrt(var + LN_EPS) * gamma + beta
        key = jax.random.key(seed)
        ks = jax.random.split(key, 16)
        B, S, D, F = (4, 512, D_MODEL, D_FF)
        s = 0.02
        return {'queries': jax.random.normal(ks[0], (B, S, D), jnp.float32), 'keys': jax.random.normal(ks[1], (B, S, D), jnp.float32), 'values': jax.random.normal(ks[2], (B, S, D), jnp.float32), 'Wq': jax.random.normal(ks[3], (D, D), jnp.float32) * s, 'bq': jnp.zeros((D,), jnp.float32), 'Wk': jax.random.normal(ks[4], (D, D), jnp.float32) * s, 'bk': jnp.zeros((D,), jnp.float32), 'Wv': jax.random.normal(ks[5], (D, D), jnp.float32) * s, 'bv': jnp.zeros((D,), jnp.float32), 'Wo': jax.random.normal(ks[6], (D, D), jnp.float32) * s, 'bo': jnp.zeros((D,), jnp.float32), 'W1': jax.random.normal(ks[7], (D, F), jnp.float32) * s, 'b1': jnp.zeros((F,), jnp.float32), 'W2': jax.random.normal(ks[8], (F, D), jnp.float32) * s, 'b2': jnp.zeros((D,), jnp.float32), 'ln1_g': jnp.ones((D,), jnp.float32), 'ln1_b': jnp.zeros((D,), jnp.float32), 'ln2_g': jnp.ones((D,), jnp.float32), 'ln2_b': jnp.zeros((D,), jnp.float32)}
    _L0_xattn_all = _L0_xattn_setup()
    _L0_xattn_in = {k: v for k, v in _L0_xattn_all.items() if k in ('Wq', 'bq', 'Wk', 'bk', 'Wv', 'bv', 'Wo', 'bo', 'W1', 'b1', 'W2', 'b2', 'ln1_g', 'ln1_b', 'ln2_g', 'ln2_b')}
    del _L0_xattn_all

    def _L0_ffn_setup():
        import jax, jax.numpy as jnp
        import numpy as np
        NUM_EXPERTS = 160
        TOP_K = 8
        ROUTED_SCALE = 2.5
        HIDDEN = 256
        INTER = 128
        key = jax.random.key(seed)
        ks = jax.random.split(key, 7)
        B, S = (1, 512)
        return {'hidden_states': jax.random.normal(ks[0], (B, S, HIDDEN), dtype=jnp.float32), 'router_w': jax.random.normal(ks[1], (NUM_EXPERTS, HIDDEN), dtype=jnp.float32) * 0.02, 'expert_bias': jnp.zeros((NUM_EXPERTS,), dtype=jnp.float32), 'w_gate': jax.random.normal(ks[2], (NUM_EXPERTS, INTER, HIDDEN), dtype=jnp.float32) * 0.02, 'w_down': jax.random.normal(ks[3], (NUM_EXPERTS, HIDDEN, INTER), dtype=jnp.float32) * 0.02, 'w_gate_shared': jax.random.normal(ks[4], (INTER, HIDDEN), dtype=jnp.float32) * 0.02, 'w_down_shared': jax.random.normal(ks[5], (HIDDEN, INTER), dtype=jnp.float32) * 0.02}
    _L0_ffn_all = _L0_ffn_setup()
    _L0_ffn_in = {k: v for k, v in _L0_ffn_all.items() if k in ('router_w', 'expert_bias', 'w_gate', 'w_down', 'w_gate_shared', 'w_down_shared')}
    del _L0_ffn_all
    return {'x': x, 'ctx_1024': ctx_1024, 'L0_attn_diff': _L0_attn_in['diff'], 'L0_attn_h_in_proj_w': _L0_attn_in['h_in_proj_w'], 'L0_attn_h_conv_w': _L0_attn_in['h_conv_w'], 'L0_attn_h_conv_b': _L0_attn_in['h_conv_b'], 'L0_attn_h_x_proj_w': _L0_attn_in['h_x_proj_w'], 'L0_attn_h_dt_proj_w': _L0_attn_in['h_dt_proj_w'], 'L0_attn_h_dt_proj_b': _L0_attn_in['h_dt_proj_b'], 'L0_attn_h_A_log': _L0_attn_in['h_A_log'], 'L0_attn_h_D_param': _L0_attn_in['h_D_param'], 'L0_attn_h_out_proj_w': _L0_attn_in['h_out_proj_w'], 'L0_attn_d_in_proj_w': _L0_attn_in['d_in_proj_w'], 'L0_attn_d_conv_w': _L0_attn_in['d_conv_w'], 'L0_attn_d_conv_b': _L0_attn_in['d_conv_b'], 'L0_attn_d_x_proj_w': _L0_attn_in['d_x_proj_w'], 'L0_attn_d_dt_proj_w': _L0_attn_in['d_dt_proj_w'], 'L0_attn_d_dt_proj_b': _L0_attn_in['d_dt_proj_b'], 'L0_attn_d_A_log': _L0_attn_in['d_A_log'], 'L0_attn_d_D_param': _L0_attn_in['d_D_param'], 'L0_attn_d_out_proj_w': _L0_attn_in['d_out_proj_w'], 'L0_xattn_Wq': _L0_xattn_in['Wq'], 'L0_xattn_bq': _L0_xattn_in['bq'], 'L0_xattn_Wk': _L0_xattn_in['Wk'], 'L0_xattn_bk': _L0_xattn_in['bk'], 'L0_xattn_Wv': _L0_xattn_in['Wv'], 'L0_xattn_bv': _L0_xattn_in['bv'], 'L0_xattn_Wo': _L0_xattn_in['Wo'], 'L0_xattn_bo': _L0_xattn_in['bo'], 'L0_xattn_W1': _L0_xattn_in['W1'], 'L0_xattn_b1': _L0_xattn_in['b1'], 'L0_xattn_W2': _L0_xattn_in['W2'], 'L0_xattn_b2': _L0_xattn_in['b2'], 'L0_xattn_ln1_g': _L0_xattn_in['ln1_g'], 'L0_xattn_ln1_b': _L0_xattn_in['ln1_b'], 'L0_xattn_ln2_g': _L0_xattn_in['ln2_g'], 'L0_xattn_ln2_b': _L0_xattn_in['ln2_b'], 'L0_ffn_router_w': _L0_ffn_in['router_w'], 'L0_ffn_expert_bias': _L0_ffn_in['expert_bias'], 'L0_ffn_w_gate': _L0_ffn_in['w_gate'], 'L0_ffn_w_down': _L0_ffn_in['w_down'], 'L0_ffn_w_gate_shared': _L0_ffn_in['w_gate_shared'], 'L0_ffn_w_down_shared': _L0_ffn_in['w_down_shared']}

def reference(x, ctx_1024, L0_attn_diff, L0_attn_h_in_proj_w, L0_attn_h_conv_w, L0_attn_h_conv_b, L0_attn_h_x_proj_w, L0_attn_h_dt_proj_w, L0_attn_h_dt_proj_b, L0_attn_h_A_log, L0_attn_h_D_param, L0_attn_h_out_proj_w, L0_attn_d_in_proj_w, L0_attn_d_conv_w, L0_attn_d_conv_b, L0_attn_d_x_proj_w, L0_attn_d_dt_proj_w, L0_attn_d_dt_proj_b, L0_attn_d_A_log, L0_attn_d_D_param, L0_attn_d_out_proj_w, L0_xattn_Wq, L0_xattn_bq, L0_xattn_Wk, L0_xattn_bk, L0_xattn_Wv, L0_xattn_bv, L0_xattn_Wo, L0_xattn_bo, L0_xattn_W1, L0_xattn_b1, L0_xattn_W2, L0_xattn_b2, L0_xattn_ln1_g, L0_xattn_ln1_b, L0_xattn_ln2_g, L0_xattn_ln2_b, L0_ffn_router_w, L0_ffn_expert_bias, L0_ffn_w_gate, L0_ffn_w_down, L0_ffn_w_gate_shared, L0_ffn_w_down_shared):
    import jax
    import jax.numpy as jnp

    def _L0_attn_ref(hidden, diff, h_in_proj_w, h_conv_w, h_conv_b, h_x_proj_w, h_dt_proj_w, h_dt_proj_b, h_A_log, h_D_param, h_out_proj_w, d_in_proj_w, d_conv_w, d_conv_b, d_x_proj_w, d_dt_proj_w, d_dt_proj_b, d_A_log, d_D_param, d_out_proj_w):
        import jax, jax.numpy as jnp
        import numpy as np
        from jax import lax
        D_MODEL = 256
        D_STATE = 16
        D_CONV = 4
        EXPAND = 2
        D_INNER = EXPAND * D_MODEL
        DT_RANK = (D_MODEL + 15) // 16
        BATCH = 4
        SEQLEN = 256

        def _silu(x):
            return x * jax.nn.sigmoid(x)

        def _init_block(key):
            ks = jax.random.split(key, 5)
            s = 0.02
            in_proj_w = jax.random.normal(ks[0], (2 * D_INNER, D_MODEL), jnp.float32) * s
            conv_w = jax.random.normal(ks[1], (D_INNER, D_CONV), jnp.float32) * s
            conv_b = jnp.zeros((D_INNER,), jnp.float32)
            x_proj_w = jax.random.normal(ks[2], (DT_RANK + 2 * D_STATE, D_INNER), jnp.float32) * s
            dt_proj_w = jax.random.normal(ks[3], (D_INNER, DT_RANK), jnp.float32) * DT_RANK ** (-0.5)
            dt_proj_b = jnp.log(jnp.expm1(jnp.full((D_INNER,), 0.01, jnp.float32)))
            A_log = jnp.log(jnp.broadcast_to(jnp.arange(1, D_STATE + 1, dtype=jnp.float32), (D_INNER, D_STATE)))
            D_param = jnp.ones((D_INNER,), jnp.float32)
            out_proj_w = jax.random.normal(ks[4], (D_MODEL, D_INNER), jnp.float32) * s
            return (in_proj_w, conv_w, conv_b, x_proj_w, dt_proj_w, dt_proj_b, A_log, D_param, out_proj_w)

        def _mamba(x, in_proj_w, conv_w, conv_b, x_proj_w, dt_proj_w, dt_proj_b, A_log, D_param, out_proj_w):
            B, L, _ = x.shape
            xz = jnp.einsum('bld,ed->ble', x, in_proj_w)
            x_in, z = jnp.split(xz, 2, axis=-1)
            x_c = x_in.swapaxes(1, 2)
            x_c = lax.conv_general_dilated(x_c, conv_w[:, None, :], window_strides=(1,), padding=[(D_CONV - 1, 0)], feature_group_count=D_INNER, dimension_numbers=('NCH', 'OIH', 'NCH'))
            x_c = x_c + conv_b[None, :, None]
            u = _silu(x_c).swapaxes(1, 2)
            x_dbl = jnp.einsum('bld,ed->ble', u, x_proj_w)
            dt, Bm, Cm = jnp.split(x_dbl, [DT_RANK, DT_RANK + D_STATE], axis=-1)
            delta = jax.nn.softplus(jnp.einsum('blr,dr->bld', dt, dt_proj_w) + dt_proj_b)
            A = -jnp.exp(A_log)

            def step(h, inp):
                d_t, b_t, c_t, u_t = inp
                h = h * jnp.exp(d_t[:, :, None] * A) + (d_t * u_t)[:, :, None] * b_t[:, None, :]
                y = jnp.einsum('bdn,bn->bd', h, c_t)
                return (h, y)
            h0 = jnp.zeros((B, D_INNER, D_STATE), x.dtype)
            xs = (delta.swapaxes(0, 1), Bm.swapaxes(0, 1), Cm.swapaxes(0, 1), u.swapaxes(0, 1))
            _, ys = lax.scan(step, h0, xs)
            y = ys.swapaxes(0, 1) + u * D_param
            y = y * _silu(z)
            return jnp.einsum('bld,ed->ble', y, out_proj_w)

        def _reference_tuple_inner(hidden, diff, h_in_proj_w, h_conv_w, h_conv_b, h_x_proj_w, h_dt_proj_w, h_dt_proj_b, h_A_log, h_D_param, h_out_proj_w, d_in_proj_w, d_conv_w, d_conv_b, d_x_proj_w, d_dt_proj_w, d_dt_proj_b, d_A_log, d_D_param, d_out_proj_w):
            hidden_out = _mamba(hidden, h_in_proj_w, h_conv_w, h_conv_b, h_x_proj_w, h_dt_proj_w, h_dt_proj_b, h_A_log, h_D_param, h_out_proj_w)
            diff_out = _mamba(diff, d_in_proj_w, d_conv_w, d_conv_b, d_x_proj_w, d_dt_proj_w, d_dt_proj_b, d_A_log, d_D_param, d_out_proj_w)
            return (hidden_out, diff_out)
        return _reference_tuple_inner(hidden, diff, h_in_proj_w, h_conv_w, h_conv_b, h_x_proj_w, h_dt_proj_w, h_dt_proj_b, h_A_log, h_D_param, h_out_proj_w, d_in_proj_w, d_conv_w, d_conv_b, d_x_proj_w, d_dt_proj_w, d_dt_proj_b, d_A_log, d_D_param, d_out_proj_w)[0]

    def _L0_xattn_ref(queries, keys, values, Wq, bq, Wk, bk, Wv, bv, Wo, bo, W1, b1, W2, b2, ln1_g, ln1_b, ln2_g, ln2_b):
        import jax, jax.numpy as jnp
        import numpy as np
        D_MODEL = 256
        D_FF = 1024
        LN_EPS = 1e-05

        def _layer_norm(x, gamma, beta):
            mu = jnp.mean(x, axis=-1, keepdims=True)
            var = jnp.var(x, axis=-1, keepdims=True)
            return (x - mu) * jax.lax.rsqrt(var + LN_EPS) * gamma + beta
        Q = queries @ Wq + bq
        K = keys @ Wk + bk
        V = values @ Wv + bv
        scale = 1.0 / jnp.sqrt(jnp.float32(Q.shape[-1]))
        scores = jnp.einsum('bqd,bkd->bqk', Q, K) * scale
        attn_w = jax.nn.softmax(scores, axis=-1)
        attn = jnp.einsum('bqk,bkd->bqd', attn_w, V)
        merged = attn @ Wo + bo
        x = queries + keys + values
        x = _layer_norm(x + merged, ln1_g, ln1_b)
        h = jax.nn.relu(x @ W1 + b1) @ W2 + b2
        return _layer_norm(x + h, ln2_g, ln2_b)

    def _L0_ffn_ref(hidden_states, router_w, expert_bias, w_gate, w_down, w_gate_shared, w_down_shared):
        import jax, jax.numpy as jnp
        import numpy as np
        NUM_EXPERTS = 160
        TOP_K = 8
        ROUTED_SCALE = 2.5
        HIDDEN = 256
        INTER = 128
        B, S, H = hidden_states.shape
        x = hidden_states.reshape(-1, H)
        T = x.shape[0]
        logits = x @ router_w.T + expert_bias[None, :]
        probs = jax.nn.sigmoid(logits)
        top_w, top_idx = jax.lax.top_k(probs, TOP_K)
        top_w = top_w / (jnp.sum(top_w, axis=-1, keepdims=True) + 1e-09)
        top_w = top_w * ROUTED_SCALE
        combine = jnp.zeros((T, NUM_EXPERTS), dtype=x.dtype)
        combine = combine.at[jnp.arange(T)[:, None], top_idx].set(top_w)
        h1 = jax.nn.silu(jnp.einsum('th,eih->eti', x, w_gate))
        h1w = h1 * combine.T[:, :, None]
        routed = jnp.einsum('eti,ehi->th', h1w, w_down)
        shared = jax.nn.silu(x @ w_gate_shared.T) @ w_down_shared.T
        return (routed + shared).reshape(B, S, H)
    x = _layernorm(x + _L0_attn_ref(x, L0_attn_diff, L0_attn_h_in_proj_w, L0_attn_h_conv_w, L0_attn_h_conv_b, L0_attn_h_x_proj_w, L0_attn_h_dt_proj_w, L0_attn_h_dt_proj_b, L0_attn_h_A_log, L0_attn_h_D_param, L0_attn_h_out_proj_w, L0_attn_d_in_proj_w, L0_attn_d_conv_w, L0_attn_d_conv_b, L0_attn_d_x_proj_w, L0_attn_d_dt_proj_w, L0_attn_d_dt_proj_b, L0_attn_d_A_log, L0_attn_d_D_param, L0_attn_d_out_proj_w), axis=-1)
    x = _layernorm(x + _L0_xattn_ref(x, ctx_1024, ctx_1024, L0_xattn_Wq, L0_xattn_bq, L0_xattn_Wk, L0_xattn_bk, L0_xattn_Wv, L0_xattn_bv, L0_xattn_Wo, L0_xattn_bo, L0_xattn_W1, L0_xattn_b1, L0_xattn_W2, L0_xattn_b2, L0_xattn_ln1_g, L0_xattn_ln1_b, L0_xattn_ln2_g, L0_xattn_ln2_b), axis=-1)
    x = _layernorm(x + _L0_ffn_ref(x, L0_ffn_router_w, L0_ffn_expert_bias, L0_ffn_w_gate, L0_ffn_w_down, L0_ffn_w_gate_shared, L0_ffn_w_down_shared), axis=-1)
    return x

_drawn_inputs = setup_inputs


def setup_inputs(seed=0):
    import zlib

    import numpy as np

    out = dict(_drawn_inputs(seed))
    spreads = {'L0_attn_h_conv_b': (0.0, 0.8),
     'L0_attn_h_dt_proj_b': (-4.600166320800781, 0.6),
     'L0_attn_h_D_param': (1.0, 0.6),
     'L0_attn_d_conv_b': (0.0, 0.1),
     'L0_attn_d_dt_proj_b': (-4.600166320800781, 0.2),
     'L0_attn_d_D_param': (1.0, 0.2),
     'L0_xattn_bq': (0.0, 0.8),
     'L0_xattn_bk': (0.0, 0.8),
     'L0_xattn_bv': (0.0, 0.8),
     'L0_xattn_bo': (0.0, 0.3),
     'L0_xattn_b1': (0.0, 0.338),
     'L0_xattn_b2': (0.0, 0.1),
     'L0_xattn_ln1_g': (1.0, 0.2),
     'L0_xattn_ln1_b': (0.0, 0.1),
     'L0_xattn_ln2_g': (1.0, 0.2),
     'L0_xattn_ln2_b': (0.0, 0.1),
     'L0_ffn_expert_bias': (0.0, 0.337)}
    factors = {'L0_attn_h_in_proj_w': 8.0,
     'L0_attn_h_conv_w': 8.0,
     'L0_attn_h_x_proj_w': 8.0,
     'L0_attn_h_dt_proj_w': 8.0,
     'L0_attn_h_A_log': 8.0,
     'L0_attn_h_out_proj_w': 8.0,
     'L0_xattn_Wq': 8.0,
     'L0_xattn_Wk': 8.0,
     'L0_xattn_Wv': 3.796,
     'L0_xattn_Wo': 3.236}
    for name, (base, spread) in spreads.items():
        noise = np.random.default_rng([zlib.crc32(name.encode()), seed]).standard_normal(out[name].shape)
        drawn = base * np.exp(spread * noise) if base else spread * noise
        out[name] = jnp.asarray(drawn.astype(out[name].dtype))
    for name, factor in factors.items():
        out[name] = (out[name] * factor).astype(out[name].dtype)
    return out
```

```python
import concourse.bass as bass
from concourse import mybir
from contextlib import ExitStack
import numpy as np

FP32 = mybir.dt.float32
BF16 = mybir.dt.bfloat16
I32 = mybir.dt.int32
U32 = mybir.dt.uint32
ACT = mybir.ActivationFunctionType
ALU = mybir.AluOpType
AX = mybir.AxisListType

P = 128
NB, T, D = 8, 256, 256
NT = NB * T
KD = D // P
QT = T // P
DI = 512
NC = DI // P
NS = 16
R = 16
TAPS = 4
XP = 64
NG = 4
SG = NS // NG
NTAU = NG * 2
FF = 1024
KF = FF // P
NE, TOPK, INTER = 160, 8, 128
CAP = NT
NTILE = NT // P
NBLK = NT * TOPK // P + NE
BJ = NBLK // 3
LN_EPS = 1e-5
SCALE = 1.0 / 16.0
UNROLL = 4
TURNS = NBLK // UNROLL
NSEL = NTILE * TOPK
ROWS = ("bv", "bo", "ln1_g", "ln1_b", "b2", "ln2_g", "ln2_b")


def whole(t):
    return t[tuple(slice(None) for _ in t.shape)]


class Sig:

    def __init__(self, sem, per, credit=0):
        self.sem, self.per, self.credit = sem, per, credit

    def at(self, b, c, due=False):
        v = b * self.per + (c + self.credit)
        return (not isinstance(v, int) or v > 0) if due else v


def decoder_kernel(nc, a, out):
    ctx = ExitStack()
    with ctx:
        def sb(name, shape, dt=FP32):
            return ctx.enter_context(nc.sbuf_tensor(name, shape, dt))

        def ps(name, shape=(P, 512), dt=FP32):
            return ctx.enter_context(nc.psum_tensor(name, list(shape), dt))

        def sig(name, per=1, credit=0):
            return Sig(ctx.enter_context(nc.semaphore(name)), per, credit)

        x2_dram = nc.dram_tensor("x2_dram", (NT, D), FP32, kind="Internal").ap()
        acc_dram = nc.dram_tensor("acc_dram", (NT, D), FP32, kind="Internal").ap()
        bc_dram = nc.dram_tensor("bc_dram", (NB, 2, NS * T), FP32, kind="Internal").ap()
        tok_dram = nc.dram_tensor("tok_dram", (NE * CAP, 1), I32, kind="Internal").ap()
        y_dram = nc.dram_tensor("y_dram", (NBLK * P, D), FP32, kind="Internal").ap()
        blk_dram = nc.dram_tensor("blk_dram", (NBLK, 2), I32, kind="Internal").ap()

        w_in = sb("w_in", [P, KD, 2 * DI])
        w_conv = sb("w_conv", [P, NC, TAPS])
        b_conv = sb("b_conv", [P, NC])
        w_xp = sb("w_xp", [P, NC, XP])
        w_dt = sb("w_dt", [R, DI])
        b_dt = sb("b_dt", [P, NC])
        a_neg = sb("a_neg", [P, NC, NS])
        d_par = sb("d_par", [P, NC])
        w_out = sb("w_out", [P, NC, D])
        w_q = sb("w_q", [P, KD, D])
        w_k = sb("w_k", [P, KD, D])
        w_v = sb("w_v", [P, KD, D])
        w_o = sb("w_o", [P, KD, D])
        b_q = sb("b_q", [P, KD])
        b_k = sb("b_k", [P, KD])
        w_1 = sb("w_1", [P, KD, FF])
        b_1 = sb("b_1", [P, KF])
        w_2 = sb("w_2", [P, KF, D])
        rows = sb("rows", [P, 7, D])
        BV, BO, G1, B1, B2, G2, BB2 = range(7)
        w_r = sb("w_r", [P, KD, NE])
        b_r = sb("b_r", [P, NE])
        ws_g = sb("ws_g", [P, KD, INTER])
        ws_d = sb("ws_d", [P, D])
        ident = sb("ident", [P, P])
        earlier = sb("earlier", [P, P], BF16)
        ones = sb("ones", [P, P], BF16)
        iota_i = sb("iota_i", [P, NE], I32)
        iota_e = sb("iota_e", [P, NE])
        ids_all = sb("ids_all", [P, NTILE], I32)
        m_half = sb("m_half", [P, QT])

        sel_e = sb("sel_e", [P, 2 * TURNS])
        sel_r = sb("sel_r", [P, 2 * TURNS])
        gate = sb("gate", [P, NSEL])
        m_sum = sb("m_sum", [P, NE], BF16)

        PB = [ps("PB0"), ps("PB1")]
        Y = [ps("Y0"), ps("Y1")]
        QB = [ps(f"QB{i}") for i in range(4)]

        w_mamba = sig("w_mamba")
        w_rest = sig("w_rest")
        k_pool = sig("k_pool")
        k_scaled = sig("k_scaled")
        zeroed = sig("zeroed")
        xt_in = sig("xt_in", 16)
        proj_f = sig("proj_f", 7)
        proj_c = sig("proj_c", 6)
        conv = sig("conv", NC * TAPS)
        z_tanh = sig("z_tanh", 2)
        gate_d = sig("gate_d")
        u_tanh = sig("u_tanh")
        u_d = sig("u_d")
        xdb_c = sig("xdb_c")
        bc_w = sig("bc_w", 16)
        bc_in = [sig(f"bc_in{i}", 8 * NG) for i in range(2)]
        softp = sig("softp", 3)
        lost = sig("lost", 3)
        dl_d = sig("dl_d")
        du_d = sig("du_d")
        decay_d = sig("decay_d", NTAU)
        inflow_d = sig("inflow_d", NTAU)
        scan_d = sig("scan_d", NTAU)
        outflow_d = sig("outflow_d", NTAU)
        sum_d = sig("sum_d", NTAU)
        y_read = sig("y_read", 2)
        y_d = sig("y_d", 2)
        q_in = sig("q_in", 48)
        v_f, v_c, kT_f, kT_c = sig("v_f", 1, 1), sig("v_c"), sig("kT_f"), sig("kT_c")
        out_f, r0_d = sig("out_f"), sig("r0_d", 1, 1)
        x1T_f, x1T_c, qT_f, qT_c = sig("x1T_f"), sig("x1T_c"), sig("qT_f"), sig("qT_c")
        sco_f, max_d, p_d = sig("sco_f"), sig("max_d", 2), sig("p_d")
        pT_f, pT_c, aT_f, aT_c = sig("pT_f"), sig("pT_c"), sig("aT_f"), sig("aT_c")
        rsum_d, mg_f, mg_c = sig("rsum_d"), sig("mg_f"), sig("mg_c")
        x2aT_f, x2aT_c, h_f, h_c = sig("x2aT_f"), sig("x2aT_c"), sig("h_f", 4), sig("h_c", 4)
        ff_f, ff_c = sig("ff_f"), sig("ff_c")
        stat1, stat2 = sig("stat1", 4 * QT), sig("stat2", 4)
        root_d = sig("root_d", 8)
        norm_d = sig("norm_d", 4)
        base_d = sig("base_d", 3, 3)
        aff1_d = sig("aff1_d", 3)
        aff2_d = sig("aff2_d", 2)
        res_d = sig("res_d")
        x2T_f, x2T_c = sig("x2T_f"), sig("x2T_c")
        lg_f, lg_c, lg_e, key_d = sig("lg_f"), sig("lg_c"), sig("lg_e"), sig("key_d")
        sh_f, sh_c, hs_d, so_f, acc_d = sig("sh_f"), sig("sh_c", 2, 2), sig("hs_d"), sig("so_f"), sig("acc_d", 1, 1)
        x2_st, acc_st = sig("x2_st", 16, 16), sig("acc_st", 16, 16)
        pick = sig("pick", 14)
        mask_d, cum_f, cum_c, msum_d = sig("mask_d"), sig("cum_f"), sig("cum_c", 1, 1), sig("msum_d", 1, 1)
        addr = sig("addr", 2)
        addr_d = sig("addr_d")
        scat = sig("scat", 16 * QT * TOPK)
        scat_d = sig("scat_d", 1, 1)
        zero_read, a_exp, k_conv = sig("zero_read"), sig("a_exp"), sig("k_conv")
        rank_s, selr_d = sig("rank_s", QT * TOPK), sig("selr_d")
        tick = sig("tick").sem
        first_units = [v_f, r0_d, base_d, sh_c, acc_d, x2_st, acc_st, cum_c, msum_d, scat_d]

        front = ExitStack()
        def sf(name, shape, dt=FP32):
            return front.enter_context(nc.sbuf_tensor(name, shape, dt))

        xt = [sf(f"xt{i}", [P, KD, T]) for i in range(2)]
        xr = sf("xr", [P, QT, D])
        ct = sf("ct", [P, KD, T])
        cr = sf("cr", [P, QT, D])
        xin = sf("xin", [P, NC, TAPS - 1 + T])
        cv = sf("cv", [P, NC, T])
        th = sf("th", [P, NC, T])
        u = [sf(f"u{i}", [P, NC, T]) for i in range(2)]
        sz = [sf(f"sz{i}", [P, NC, T]) for i in range(2)]
        dl = [sf(f"dl{i}", [P, NC, T]) for i in range(2)]
        du = [sf(f"du{i}", [P, NC, T]) for i in range(2)]
        xdb = sf("xdb", [XP, T])
        yb = [sf(f"yb{i}", [P, NC, T]) for i in range(2)]
        bc = [sf(f"bc{i}", [P, 2, SG, T]) for i in range(2)]
        da = [sf(f"da{i}", [P, 2, SG, T]) for i in range(2)]
        hb = [sf(f"hb{i}", [P, 2, SG, T]) for i in range(2)]
        x1 = sf("x1", [P, QT, D])
        fT = sf("fT", [P, KD, T])
        qT = sf("qT", [P, KD, T])
        kT = sf("kT", [P, KD, T])
        vv = sf("vv", [P, QT, D])
        pe_ = sf("pe_", [P, QT, T])
        base = sf("base", [P, QT, D])
        x2a = sf("x2a", [P, QT, D])
        hT = sf("hT", [P, KF, T])
        x2 = sf("x2", [P, QT, D])
        hs = sf("hs", [P, T])
        hth = sf("hth", [P, T])
        acc = sf("acc", [P, QT, D])
        stats = sf("stats", [P, QT, 6])
        mv = sf("mv", [P, QT, 2])
        ve = sf("ve", [P, QT])
        rs = sf("rs", [P, QT])
        nmx = sf("nmx", [P, QT])
        ssum = sf("ssum", [P, QT])
        rsum = sf("rsum", [P, QT])
        key = sf("key", [P, QT, NE])
        rep = sf("rep", [P, QT, NE])
        msk_b = sf("msk_b", [P, QT, NE], BF16)
        junk = sf("junk", [P, NE])
        top = sf("top", [P, QT, TOPK])
        ti = sf("ti", [P, QT, TOPK], U32)
        pr = sf("pr", [P, QT, TOPK])
        psm = sf("psm", [P, QT])
        e_st = sf("e_st", [P, QT, TOPK])
        r_st = sf("r_st", [P, QT, TOPK])
        ad_f = sf("ad_f", [P, QT, TOPK])
        ad_i = sf("ad_i", [P, QT, TOPK], I32)
        id_st = sf("id_st", [P, QT], I32)
        zi = th[:, :, :].rearrange("p c t -> p (c t)").bitcast(I32)

        def pair(bank):
            return bank[:, :].rearrange("p (c t) -> p c t", c=2)

        def all_batches(eng, batch):
            for b in range(2):
                batch(b, b)
            with eng.Fori(1, NB // 2) as i:
                for p in range(2):
                    batch(i * 2 + p, p)

        block = front.enter_context(nc.Block())

        @block.sync
        def _(sp):
            for g in first_units:
                sp.sem_inc(g.sem, g.credit)
            for dst, src in ((w_in, "w_in"), (w_conv, "conv_w"), (b_conv, "conv_b"), (w_xp, "w_xp"),
                             (w_dt, "w_dt"), (b_dt, "dt_b"), (a_neg, "A_log"), (d_par, "D")):
                sp.dma_start(whole(dst), a[src]).then_inc(w_mamba.sem, 16)

            def in_proj(b, p):
                if proj_f.at(b - 1, 4, True):
                    sp.wait_ge(proj_f.sem, proj_f.at(b - 1, 4))
                sp.dma_start(xt[p][:, :, :], a["xT"][:, :, bass.ts(b, T)]).then_inc(xt_in.sem, 16)
                if isinstance(b, int) and b == 0:
                    for dst, src in ((w_out, "w_out"), (w_q, "w_q"), (w_k, "w_k"), (w_v, "w_v"), (w_o, "w_o"), (b_q, "b_q"),
                                     (b_k, "b_k"), (w_1, "w_1"), (b_1, "b_1"), (w_2, "w_2"), (w_r, "w_r"),
                                     (ws_g, "ws_g"), (ws_d, "ws_d")):
                        sp.dma_start(whole(dst), a[src]).then_inc(w_rest.sem, 16)
                    for i in range(7):
                        sp.dma_start(rows[:, i, :], a[ROWS[i]].unsqueeze(0).broadcast_to([P, D])).then_inc(w_rest.sem, 16)
                    sp.dma_start(b_r[:, :], a["b_r"].unsqueeze(0).broadcast_to([P, NE])).then_inc(w_rest.sem, 16)

            def bc_out(b, p):
                sp.wait_ge(xdb_c.sem, xdb_c.at(b, 1))
                sp.dma_start(bc_dram[b].rearrange("a (n t) -> (a n) t", n=NS), xdb[2 * R:XP, :]).then_inc(bc_w.sem, 16)

            def bc_load(b, p, g):
                if g == 0:
                    sp.wait_ge(bc_w.sem, bc_w.at(b, 16))
                if outflow_d.at(b, 2 * g - 2, True):
                    sp.wait_ge(outflow_d.sem, outflow_d.at(b, 2 * g - 2))
                src = bc_dram[b][:, g * SG * T:(g + 1) * SG * T]
                sp.dma_start(bc[g % 2][:, :, :, :].rearrange("p a n t -> p a (n t)"),
                             src.unsqueeze(0).broadcast_to([P, 2, SG * T])).then_inc(bc_in[g % 2].sem, 16)

            def q_load(b, p):
                if v_f.at(b - 1, 1, True):
                    sp.wait_ge(v_f.sem, v_f.at(b - 1, 1))
                if base_d.at(b - 1, 3, True):
                    sp.wait_ge(base_d.sem, base_d.at(b - 1, 3))
                if r0_d.at(b - 1, 1, True):
                    sp.wait_ge(r0_d.sem, r0_d.at(b - 1, 1))
                sp.dma_start(ct[:, :, :], a["cT"][:, :, bass.ts(b, T)]).then_inc(q_in.sem, 16)
                sp.dma_start(cr[:, :, :], a["c"][bass.ts(b, T), :].rearrange("(q p) d -> p q d", p=P)).then_inc(q_in.sem, 16)
                sp.dma_start(xr[:, :, :], a["x"][bass.ts(b, T), :].rearrange("(q p) d -> p q d", p=P)).then_inc(q_in.sem, 16)

            def x2T(b, p):
                sp.wait_ge(norm_d.sem, norm_d.at(b, 4))
                sp.dma_start(x2_dram[bass.ts(b, T), :].rearrange("(q p) d -> p q d", p=P), x2[:, :, :]).then_inc(x2_st.sem, 16)

            def shared_out(b, p):
                sp.wait_ge(acc_d.sem, acc_d.at(b, 1))
                sp.dma_start(acc_dram[bass.ts(b, T), :].rearrange("(q p) d -> p q d", p=P), acc[:, :, :]).then_inc(acc_st.sem, 16)

            def batch(b, p):
                in_proj(b, p)
                bc_out(b, p)
                for g in range(NG):
                    bc_load(b, p, g)
                q_load(b, p)
                x2T(b, p)
                shared_out(b, p)

            all_batches(sp, batch)
            sp.wait_ge(x2_st.sem, x2_st.at(NB - 1, 16))
            sp.wait_ge(acc_st.sem, acc_st.at(NB - 1, 16))

        @block.gpsimd
        def _(pool):
            g = nc.gpsimd
            g.memset(ident[:, :], 0.0).then_inc(k_pool.sem, 1)
            g.memset(earlier[:, :], 1.0).then_inc(k_pool.sem, 1)
            g.memset(ones[:, :], 1.0).then_inc(k_pool.sem, 1)
            g.memset(xin[:, :, 0:TAPS - 1], 0.0).then_inc(k_pool.sem, 1)
            g.memset(da[0][:, :, :, 0:1], 0.0).then_inc(k_pool.sem, 1)
            g.memset(da[1][:, :, :, 0:1], 0.0).then_inc(k_pool.sem, 1)
            g.memset(m_sum[:, :], 0.0).then_inc(k_pool.sem, 1)
            g.memset(m_half[:, :], -0.5).then_inc(k_pool.sem, 1)
            g.memset(zi, 0).then_inc(k_pool.sem, 1)
            g.iota(iota_i[:, :], pattern=[[1, NE]], base=0, channel_multiplier=0).then_inc(k_pool.sem, 1)
            g.iota(ids_all[:, :], pattern=[[P, NTILE]], base=0, channel_multiplier=1).then_inc(k_pool.sem, 1)
            pool.wait_ge(k_pool.sem, 11)
            g.affine_select(out=ident[:, :], in_=ident[:, :], compare_op=ALU.not_equal, fill=1.0, base=0,
                            pattern=[[-1, P]], channel_multiplier=1).then_inc(k_pool.sem, 1)
            g.affine_select(out=earlier[:, :], in_=earlier[:, :], compare_op=ALU.is_gt, fill=0.0, base=0,
                            pattern=[[1, P]], channel_multiplier=-1).then_inc(k_pool.sem, 1)
            table = tok_dram.rearrange("(p n) o -> p (n o)", p=P)
            pieces = -(-table.shape[1] // (NC * T))
            for i in range(pieces):
                lo, hi = i * NC * T, min((i + 1) * NC * T, table.shape[1])
                pool.dma_start(table[:, lo:hi], zi[:, 0:hi - lo]).then_inc(zeroed.sem, 16)
            pool.wait_ge(zeroed.sem, 16 * pieces)
            pool.sem_inc(zero_read.sem, 1)

            def inflow(b, p, t):
                gr, cp = t // 2, t % 2
                if t == 0:
                    pool.wait_ge(du_d.sem, du_d.at(b, 1))
                if cp == 0:
                    pool.wait_ge(bc_in[gr % 2].sem, bc_in[gr % 2].at(b, 16 * (gr // 2 + 1)))
                if sum_d.at(b, t - 1, True):
                    pool.wait_ge(sum_d.sem, sum_d.at(b, t - 1))
                for ci in range(2):
                    c = 2 * cp + ci
                    ins = g.tensor_tensor(hb[t % 2][:, ci, :, :], bc[gr % 2][:, 0, :, :],
                                          du[p][:, c, :].unsqueeze(1).to_broadcast([P, SG, T]), ALU.mult)
                ins.then_inc(inflow_d.sem, 1)

            def ln_root(b, i):
                pool.wait_ge(stat2.sem, stat2.at(b, i + 1))
                pool.sem_inc(tick, 1)
                g.tensor_scalar(ve[:, :], mv[:, :, 1], LN_EPS, None, ALU.add).then_inc(root_d.sem, 1)
                pool.wait_ge(root_d.sem, root_d.at(b, 2 * i + 1))
                g.tensor_tensor(rs[:, :], ve[:, :], m_half[:, :], ALU.pow).then_inc(root_d.sem, 1)

            def row(i):
                return rows[:, i, :].unsqueeze(1).to_broadcast([P, QT, D])

            def base_(b, p):
                if isinstance(b, int) and b == 0:
                    pool.wait_ge(w_rest.sem, 16 * 21)
                pool.wait_ge(norm_d.sem, norm_d.at(b, 1))
                pool.wait_ge(q_in.sem, q_in.at(b, 48))
                g.tensor_tensor(base[:, :, :], x1[:, :, :], cr[:, :, :], ALU.add).then_inc(base_d.sem, 1)
                pool.wait_ge(base_d.sem, base_d.at(b, 1))
                g.tensor_tensor(base[:, :, :], base[:, :, :], cr[:, :, :], ALU.add).then_inc(base_d.sem, 1)
                pool.wait_ge(base_d.sem, base_d.at(b, 2))
                g.tensor_tensor(base[:, :, :], base[:, :, :], row(BO), ALU.add).then_inc(base_d.sem, 1)

            def ln1_affine(b, p):
                pool.wait_ge(norm_d.sem, norm_d.at(b, 2))
                g.tensor_tensor(x2a[:, :, :], x2a[:, :, :], row(G1), ALU.mult).then_inc(aff1_d.sem, 1)
                pool.wait_ge(aff1_d.sem, aff1_d.at(b, 1))
                g.tensor_tensor(x2a[:, :, :], x2a[:, :, :], row(B1), ALU.add).then_inc(aff1_d.sem, 1)
                pool.wait_ge(aff1_d.sem, aff1_d.at(b, 2))
                g.tensor_tensor(base[:, :, :], x2a[:, :, :], row(B2), ALU.add).then_inc(aff1_d.sem, 1)

            def ln2_affine(b, p):
                pool.wait_ge(norm_d.sem, norm_d.at(b, 3))
                g.tensor_tensor(x2[:, :, :], x2[:, :, :], row(G2), ALU.mult).then_inc(aff2_d.sem, 1)
                pool.wait_ge(aff2_d.sem, aff2_d.at(b, 1))
                g.tensor_tensor(x2[:, :, :], x2[:, :, :], row(BB2), ALU.add).then_inc(aff2_d.sem, 1)

            def scatter(b, p):
                pool.wait_ge(addr_d.sem, addr_d.at(b, 1))
                pool.sem_inc(tick, 1)
                for q in range(QT):
                    for k in range(TOPK):
                        g.indirect_dma_start(tok_dram, bass.IndirectOffsetOnAxis(ap=ad_i[:, q, k:k + 1], axis=0),
                                             id_st[:, q:q + 1], None).then_inc(scat.sem, 16)

            def settle(b, p):
                pool.wait_ge(scat.sem, scat.at(b, 16 * QT * TOPK))
                pool.sem_inc(scat_d.sem, 1)

            def batch(b, p):
                for t in range(NTAU):
                    inflow(b, p, t)
                ln_root(b, 0)
                base_(b, p)
                ln_root(b, 1)
                ln1_affine(b, p)
                ln_root(b, 2)
                ln2_affine(b, p)
                ln_root(b, 3)
                scatter(b, p)
                settle(b, p)

            all_batches(pool, batch)
            pool.wait_ge(scat.sem, scat.at(NB - 1, 16 * QT * TOPK))

        @block.scalar
        def _(act):
            s = nc.scalar

            def in_proj(b, p):
                for f in range(2):
                    act.wait_ge(proj_f.sem, proj_f.at(b, f + 1))
                    if conv.at(b - 1, NC * TAPS, True):
                        act.wait_ge(conv.sem, conv.at(b - 1, NC * TAPS))
                    if isinstance(b, int) and b == 0:
                        act.wait_ge(k_pool.sem, 13)
                    s.activation(xin[:, 2 * f:2 * f + 2, TAPS - 1:], pair(PB[f]), ACT.Copy).then_inc(proj_c.sem, 1)

            def gate_z(b, p):
                if isinstance(b, int) and b == 0:
                    act.wait_ge(w_mamba.sem, 16 * 8)
                    s.activation(a_neg[:, :, :], a_neg[:, :, :], ACT.Exp).then_inc(a_exp.sem, 1)
                    act.wait_ge(zero_read.sem, 1)
                if dl_d.at(b - 1, 1, True):
                    act.wait_ge(dl_d.sem, dl_d.at(b - 1, 1))
                if y_d.at(b - 2, 2, True):
                    act.wait_ge(y_d.sem, y_d.at(b - 2, 2))
                for f in range(2):
                    act.wait_ge(proj_f.sem, proj_f.at(b, f + 3))
                    s.activation(th[:, 2 * f:2 * f + 2, :], pair(PB[f]), ACT.Tanh, scale=0.5).then_inc(z_tanh.sem, 1)
                    s.activation(sz[p][:, 2 * f:2 * f + 2, :], pair(PB[f]), ACT.Copy, scale=0.5).then_inc(proj_c.sem, 1)

            def u_(b, p):
                act.wait_ge(conv.sem, conv.at(b, NC * TAPS))
                act.wait_ge(gate_d.sem, gate_d.at(b, 1))
                s.activation(th[:, :, :], cv[:, :, :], ACT.Tanh).then_inc(u_tanh.sem, 1)

            def x_proj(b, p):
                act.wait_ge(proj_f.sem, proj_f.at(b, 5))
                if proj_f.at(b - 1, 7, True):
                    act.wait_ge(proj_f.sem, proj_f.at(b - 1, 7))
                if bc_w.at(b - 1, 16, True):
                    act.wait_ge(bc_w.sem, bc_w.at(b - 1, 16))
                s.activation(xdb[:, :], PB[0][0:XP, 0:T], ACT.Copy).then_inc(xdb_c.sem, 1)

            def dt_proj(b, p):
                if du_d.at(b - 2, 1, True):
                    act.wait_ge(du_d.sem, du_d.at(b - 2, 1))
                act.wait_ge(u_d.sem, u_d.at(b, 1))
                for f in range(2):
                    act.wait_ge(proj_f.sem, proj_f.at(b, 6 + f))
                    for i in range(2):
                        c = 2 * f + i
                        ins = s.activation(dl[p][:, c, :], pair(PB[(f + 1) % 2])[:, i, :], ACT.Identity, bias=b_dt[:, c:c + 1])
                    ins.then_inc(proj_c.sem, 1)
                act.wait_ge(proj_c.sem, proj_c.at(b, 6))
                s.activation(th[:, :, :], dl[p][:, :, :], ACT.Abs).then_inc(softp.sem, 1)
                act.wait_ge(softp.sem, softp.at(b, 1))
                s.activation(th[:, :, :], th[:, :, :], ACT.Exp, scale=-1.0).then_inc(softp.sem, 1)
                act.wait_ge(softp.sem, softp.at(b, 2))
                s.activation(cv[:, :, :], th[:, :, :], ACT.Ln, bias=1.0).then_inc(softp.sem, 1)

            def decay(b, p, t):
                gr, cp = t // 2, t % 2
                if t == 0:
                    act.wait_ge(dl_d.sem, dl_d.at(b, 1))
                    if isinstance(b, int) and b == 0:
                        act.wait_ge(k_scaled.sem, 2)
                if scan_d.at(b, t - 1, True):
                    act.wait_ge(scan_d.sem, scan_d.at(b, t - 1))
                for ci in range(2):
                    for n in range(SG):
                        c, st = 2 * cp + ci, gr * SG + n
                        ins = s.activation(da[t % 2][:, ci, n, 1:T], dl[p][:, c, 1:T], ACT.Exp, scale=a_neg[:, c, st:st + 1])
                ins.then_inc(decay_d.sem, 1)

            def copy_out(b, filled, bank, dst, done):
                act.wait_ge(filled.sem, filled.at(b, 1))
                s.activation(dst[:, :, :], pair(bank), ACT.Copy).then_inc(done.sem, 1)

            def kv(b, p):
                act.wait_ge(kT_f.sem, kT_f.at(b, 1))
                for i in range(KD):
                    ins = s.activation(kT[:, i, :], pair(QB[3])[:, i, :], ACT.Identity, bias=b_k[:, i:i + 1])
                ins.then_inc(kT_c.sem, 1)

            def q(b, p):
                act.wait_ge(qT_f.sem, qT_f.at(b, 1))
                for i in range(KD):
                    ins = s.activation(qT[:, i, :], pair(QB[2])[:, i, :], ACT.Identity, bias=b_q[:, i:i + 1])
                ins.then_inc(qT_c.sem, 1)

            def softmax(b, p):
                act.wait_ge(max_d.sem, max_d.at(b, 2))
                for i in range(QT):
                    ins = s.activation(pe_[:, i, :], pair(QB[1])[:, i, :], ACT.Exp, bias=nmx[:, i:i + 1], scale=SCALE,
                                       accum_out=ssum[:, i:i + 1])
                ins.then_inc(p_d.sem, 1)

            def ffn1(b, p):
                for f in range(4):
                    act.wait_ge(h_f.sem, h_f.at(b, f + 1))
                    for i in range(2):
                        c = 2 * f + i
                        ins = s.activation(hT[:, c, :], pair(QB[2 + f % 2])[:, i, :], ACT.Relu, bias=b_1[:, c:c + 1])
                    ins.then_inc(h_c.sem, 1)

            def shared(b, p):
                act.wait_ge(sh_f.sem, sh_f.at(b, 1))
                s.activation(hth[:, :], QB[3][:, 0:T], ACT.Tanh, scale=0.5).then_inc(sh_c.sem, 1)
                s.activation(hs[:, :], QB[3][:, 0:T], ACT.Copy, scale=0.5).then_inc(sh_c.sem, 1)

            def router(b, p):
                act.wait_ge(lg_c.sem, lg_c.at(b, 1))
                s.activation(key[:, :, :], key[:, :, :], ACT.Exp, scale=-1.0).then_inc(lg_e.sem, 1)

            def batch(b, p):
                in_proj(b, p)
                gate_z(b, p)
                u_(b, p)
                x_proj(b, p)
                dt_proj(b, p)
                for t in range(NTAU):
                    decay(b, p, t)
                kv(b, p)
                copy_out(b, x1T_f, QB[1], fT, x1T_c)
                q(b, p)
                softmax(b, p)
                copy_out(b, pT_f, QB[2], qT, pT_c)
                copy_out(b, aT_f, QB[3], kT, aT_c)
                copy_out(b, x2aT_f, QB[1], fT, x2aT_c)
                ffn1(b, p)
                copy_out(b, x2T_f, QB[1], fT, x2T_c)
                router(b, p)
                shared(b, p)

            all_batches(act, batch)

        @block.tensor
        def _(pe):
            mm, tr = nc.tensor.matmul, nc.tensor.transpose

            def in_proj(b, p):
                if isinstance(b, int) and b == 0:
                    pe.wait_ge(w_mamba.sem, 16 * 8)
                pe.wait_ge(xt_in.sem, xt_in.at(b, 16))
                for f in range(4):
                    if f < 2:
                        if proj_c.at(b - 1, 6, True):
                            pe.wait_ge(proj_c.sem, proj_c.at(b - 1, 6))
                    else:
                        if proj_c.at(b, f - 1, True):
                            pe.wait_ge(proj_c.sem, proj_c.at(b, f - 1))
                    for i in range(2):
                        c = 2 * f + i
                        for k in range(KD):
                            ins = mm(pair(PB[f % 2])[:, i, :], w_in[:, k, c * P:(c + 1) * P], xt[p][:, k, :],
                                     start=k == 0, stop=k == KD - 1)
                    ins.then_inc(proj_f.sem, 1)

            def x_proj(b, p):
                pe.wait_ge(u_d.sem, u_d.at(b, 1))
                pe.wait_ge(proj_c.sem, proj_c.at(b, 3))
                for c in range(NC):
                    ins = mm(PB[0][0:XP, 0:T], w_xp[:, c, :], u[p][:, c, :], start=c == 0, stop=c == NC - 1)
                ins.then_inc(proj_f.sem, 1)

            def dt_proj(b, p):
                pe.wait_ge(xdb_c.sem, xdb_c.at(b, 1))
                pe.wait_ge(proj_c.sem, proj_c.at(b, 4))
                for f in range(2):
                    for i in range(2):
                        c = 2 * f + i
                        ins = mm(pair(PB[(f + 1) % 2])[:, i, :], w_dt[:, c * P:(c + 1) * P], xdb[0:R, :], start=True, stop=True)
                    ins.then_inc(proj_f.sem, 1)

            def sum_(b, p, t):
                gr, cp = t // 2, t % 2
                if gr == 0:
                    if y_read.at(b - 1, cp + 1, True):
                        pe.wait_ge(y_read.sem, y_read.at(b - 1, cp + 1))
                pe.wait_ge(outflow_d.sem, outflow_d.at(b, t + 1))
                for ci in range(2):
                    for n in range(SG):
                        ins = mm(pair(Y[cp])[:, ci, :], ident[:, :], hb[t % 2][:, ci, n, :],
                                 start=gr == 0 and ci == 0 and n == 0, stop=gr == NG - 1 and n == SG - 1,
                                 skip_group_check=True)
                ins.then_inc(sum_d.sem, 1)

            def kv(b, p):
                if isinstance(b, int) and b == 0:
                    pe.wait_ge(w_rest.sem, 16 * 21)
                pe.wait_ge(q_in.sem, q_in.at(b, 48))
                if sh_c.at(b - 1, 2, True):
                    pe.wait_ge(sh_c.sem, sh_c.at(b - 1, 2))
                for i in range(KD):
                    for k in range(KD):
                        ins = mm(pair(QB[3])[:, i, :], w_k[:, k, i * P:(i + 1) * P], ct[:, k, :], start=k == 0, stop=k == KD - 1)
                ins.then_inc(kT_f.sem, 1)
                if acc_d.at(b - 1, 1, True):
                    pe.wait_ge(acc_d.sem, acc_d.at(b - 1, 1))
                for q in range(QT):
                    for k in range(KD):
                        ins = mm(pair(QB[0])[:, q, :], ct[:, k, q * P:(q + 1) * P], w_v[:, k, :], start=k == 0, stop=k == KD - 1)
                ins.then_inc(v_f.sem, 1)

            def out_proj(b, p):
                pe.wait_ge(y_d.sem, y_d.at(b, 2))
                pe.wait_ge(v_c.sem, v_c.at(b, 1))
                for q in range(QT):
                    for c in range(NC):
                        ins = mm(pair(QB[0])[:, q, :], yb[p][:, c, q * P:(q + 1) * P], w_out[:, c, :], start=c == 0, stop=c == NC - 1)
                ins.then_inc(out_f.sem, 1)

            def turned(src, bank, filled):
                for q in range(QT):
                    for k in range(KD):
                        ins = tr(pair(bank)[:, k, q * P:(q + 1) * P], src[:, q, k * P:(k + 1) * P], ident[:, :])
                ins.then_inc(filled.sem, 1)

            def q_(b, p):
                pe.wait_ge(x1T_c.sem, x1T_c.at(b, 1))
                for i in range(KD):
                    for k in range(KD):
                        ins = mm(pair(QB[2])[:, i, :], w_q[:, k, i * P:(i + 1) * P], fT[:, k, :], start=k == 0, stop=k == KD - 1)
                ins.then_inc(qT_f.sem, 1)

            def scores(b, p):
                pe.wait_ge(qT_c.sem, qT_c.at(b, 1))
                pe.wait_ge(kT_c.sem, kT_c.at(b, 1))
                for q in range(QT):
                    for k in range(KD):
                        ins = mm(pair(QB[1])[:, q, :], qT[:, k, q * P:(q + 1) * P], kT[:, k, :], start=k == 0, stop=k == KD - 1)
                ins.then_inc(sco_f.sem, 1)

            def pv(b, p):
                pe.wait_ge(pT_c.sem, pT_c.at(b, 1))
                for i in range(KD):
                    for k in range(QT):
                        ins = mm(pair(QB[3])[:, i, :], vv[:, k, i * P:(i + 1) * P], qT[:, k, :], start=k == 0, stop=k == QT - 1)
                ins.then_inc(aT_f.sem, 1)

            def merge(b, p):
                pe.wait_ge(aT_c.sem, aT_c.at(b, 1))
                pe.wait_ge(r0_d.sem, r0_d.at(b, 1))
                for q in range(QT):
                    for k in range(KD):
                        ins = mm(pair(QB[0])[:, q, :], kT[:, k, q * P:(q + 1) * P], w_o[:, k, :], start=k == 0, stop=k == KD - 1)
                ins.then_inc(mg_f.sem, 1)

            def ffn1(b, p):
                pe.wait_ge(x2aT_c.sem, x2aT_c.at(b, 1))
                for f in range(4):
                    if f >= 2:
                        if h_c.at(b, f - 1, True):
                            pe.wait_ge(h_c.sem, h_c.at(b, f - 1))
                    for i in range(2):
                        c = 2 * f + i
                        for k in range(KD):
                            ins = mm(pair(QB[2 + f % 2])[:, i, :], w_1[:, k, c * P:(c + 1) * P], fT[:, k, :], start=k == 0, stop=k == KD - 1)
                    ins.then_inc(h_f.sem, 1)

            def ffn2(b, p):
                pe.wait_ge(h_c.sem, h_c.at(b, 4))
                for q in range(QT):
                    for k in range(KF):
                        ins = mm(pair(QB[0])[:, q, :], hT[:, k, q * P:(q + 1) * P], w_2[:, k, :], start=k == 0, stop=k == KF - 1)
                ins.then_inc(ff_f.sem, 1)

            def router(b, p):
                pe.wait_ge(x2T_c.sem, x2T_c.at(b, 1))
                for q in range(QT):
                    for k in range(KD):
                        ins = mm(QB[2][:, q * NE:(q + 1) * NE], fT[:, k, q * P:(q + 1) * P], w_r[:, k, :], start=k == 0, stop=k == KD - 1)
                ins.then_inc(lg_f.sem, 1)

            def shared(b, p):
                for k in range(KD):
                    ins = mm(QB[3][:, 0:T], ws_g[:, k, :], fT[:, k, :], start=k == 0, stop=k == KD - 1)
                ins.then_inc(sh_f.sem, 1)

            def shared_out(b, p):
                pe.wait_ge(hs_d.sem, hs_d.at(b, 1))
                for q in range(QT):
                    ins = mm(pair(QB[0])[:, q, :], hs[:, q * P:(q + 1) * P], ws_d[:, :], start=True, stop=True)
                ins.then_inc(so_f.sem, 1)

            def rank(b, p):
                pe.wait_ge(mask_d.sem, mask_d.at(b, 1))
                if msum_d.at(b - 1, 1, True):
                    pe.wait_ge(msum_d.sem, msum_d.at(b - 1, 1))
                mm(QB[1][:, 0:NE], earlier[:, :], msk_b[:, 0, :], start=True, stop=False)
                mm(QB[1][:, 0:NE], ones[:, :], m_sum[:, :], start=False, stop=True)
                mm(QB[1][:, NE:2 * NE], earlier[:, :], msk_b[:, 1, :], start=True, stop=False)
                mm(QB[1][:, NE:2 * NE], ones[:, :], msk_b[:, 0, :], start=False, stop=False)
                mm(QB[1][:, NE:2 * NE], ones[:, :], m_sum[:, :], start=False, stop=True).then_inc(cum_f.sem, 1)

            def batch(b, p):
                in_proj(b, p)
                x_proj(b, p)
                dt_proj(b, p)
                for t in range(NTAU):
                    sum_(b, p, t)
                kv(b, p)
                out_proj(b, p)
                pe.wait_ge(norm_d.sem, norm_d.at(b, 1))
                if cum_c.at(b - 1, 1, True):
                    pe.wait_ge(cum_c.sem, cum_c.at(b - 1, 1))
                turned(x1, QB[1], x1T_f)
                q_(b, p)
                scores(b, p)
                pe.wait_ge(p_d.sem, p_d.at(b, 1))
                turned(pe_, QB[2], pT_f)
                pv(b, p)
                merge(b, p)
                pe.wait_ge(aff1_d.sem, aff1_d.at(b, 2))
                turned(x2a, QB[1], x2aT_f)
                ffn1(b, p)
                ffn2(b, p)
                pe.wait_ge(norm_d.sem, norm_d.at(b, 4))
                turned(x2, QB[1], x2T_f)
                router(b, p)
                shared(b, p)
                shared_out(b, p)
                rank(b, p)

            all_batches(pe, batch)

        @block.vector
        def _(dve):
            v = nc.vector
            dve.wait_ge(w_mamba.sem, 16 * 8)
            dve.wait_ge(k_pool.sem, 13)
            v.tensor_scalar(w_conv[:, :, :], w_conv[:, :, :], 0.5, None, ALU.mult).then_inc(k_conv.sem, 1)
            v.tensor_scalar(b_conv[:, :], b_conv[:, :], 0.5, None, ALU.mult).then_inc(k_conv.sem, 1)
            v.tensor_copy(iota_e[:, :], iota_i[:, :]).then_inc(k_conv.sem, 1)
            v.memset(sel_e[:, NSEL:], 0.0).then_inc(k_conv.sem, 1)
            v.memset(sel_r[:, NSEL:], 0.0).then_inc(k_conv.sem, 1)
            dve.wait_ge(k_conv.sem, 5)

            def conv_(b, p):
                dve.wait_ge(proj_c.sem, proj_c.at(b, 2))
                for k in range(TAPS):
                    for c in range(NC):
                        if k == 0:
                            ins = v.tensor_scalar(cv[:, c, :], xin[:, c, 0:T], w_conv[:, c, 0:1], b_conv[:, c:c + 1], ALU.mult, ALU.add)
                        else:
                            if conv.at(b, (k - 1) * NC + c + 1, True):
                                dve.wait_ge(conv.sem, conv.at(b, (k - 1) * NC + c + 1))
                            ins = v.scalar_tensor_tensor(cv[:, c, :], xin[:, c, k:k + T], w_conv[:, c, k:k + 1], cv[:, c, :], ALU.mult, ALU.add)
                        ins.then_inc(conv.sem, 1)

            def gate_z(b, p):
                dve.wait_ge(z_tanh.sem, z_tanh.at(b, 2))
                dve.wait_ge(proj_c.sem, proj_c.at(b, 4))
                v.scalar_tensor_tensor(sz[p][:, :, :], th[:, :, :], 1.0, sz[p][:, :, :], ALU.add, ALU.mult).then_inc(gate_d.sem, 1)

            def u_(b, p):
                dve.wait_ge(u_tanh.sem, u_tanh.at(b, 1))
                v.scalar_tensor_tensor(u[p][:, :, :], th[:, :, :], 1.0, cv[:, :, :], ALU.add, ALU.mult).then_inc(u_d.sem, 1)

            def delta(b, p):
                dve.wait_ge(softp.sem, softp.at(b, 3))
                v.tensor_scalar(du[p][:, :, :], th[:, :, :], 1.0, -1.0, ALU.add, ALU.add).then_inc(lost.sem, 1)
                v.scalar_tensor_tensor(dl[p][:, :, :], dl[p][:, :, :], 0.0, cv[:, :, :], ALU.max, ALU.add).then_inc(lost.sem, 1)
                dve.wait_ge(lost.sem, lost.at(b, 1))
                v.tensor_tensor(th[:, :, :], th[:, :, :], du[p][:, :, :], ALU.subtract).then_inc(lost.sem, 1)
                dve.wait_ge(lost.sem, lost.at(b, 3))
                v.tensor_tensor(dl[p][:, :, :], dl[p][:, :, :], th[:, :, :], ALU.add).then_inc(dl_d.sem, 1)
                dve.wait_ge(dl_d.sem, dl_d.at(b, 1))
                v.tensor_tensor(du[p][:, :, :], dl[p][:, :, :], u[p][:, :, :], ALU.mult).then_inc(du_d.sem, 1)
                if isinstance(b, int) and b == 0:
                    dve.wait_ge(a_exp.sem, 1)
                    v.tensor_scalar(a_neg[:, :, :], a_neg[:, :, :], -1.0, None, ALU.mult).then_inc(k_scaled.sem, 2)

            def scan(b, p, t):
                dve.wait_ge(decay_d.sem, decay_d.at(b, t + 1))
                dve.wait_ge(inflow_d.sem, inflow_d.at(b, t + 1))
                flat = hb[t % 2][:, :, :, :].rearrange("p c n t -> p (c n t)")
                v.tensor_tensor_scan(flat, da[t % 2][:, :, :, :].rearrange("p c n t -> p (c n t)"), flat, 0.0,
                                     ALU.mult, ALU.add).then_inc(scan_d.sem, 1)

            def outflow(b, p, t):
                dve.wait_ge(scan_d.sem, scan_d.at(b, t + 1))
                gr = t // 2
                for ci in range(2):
                    ins = v.tensor_tensor(hb[t % 2][:, ci, :, :], hb[t % 2][:, ci, :, :], bc[gr % 2][:, 1, :, :], ALU.mult)
                ins.then_inc(outflow_d.sem, 1)

            def y(b, p, cp):
                dve.wait_ge(sum_d.sem, sum_d.at(b, NTAU - 1 + cp))
                for ci in range(2):
                    c = 2 * cp + ci
                    ins = v.scalar_tensor_tensor(yb[p][:, c, :], u[p][:, c, :], d_par[:, c:c + 1], pair(Y[cp])[:, ci, :], ALU.mult, ALU.add)
                ins.then_inc(y_read.sem, 1)
                dve.wait_ge(y_read.sem, y_read.at(b, cp + 1))
                cs = slice(2 * cp, 2 * cp + 2)
                v.tensor_tensor(yb[p][:, cs, :], yb[p][:, cs, :], sz[p][:, cs, :], ALU.mult).then_inc(y_d.sem, 1)

            def kv(b, p):
                dve.wait_ge(v_f.sem, v_f.at(b, 1))
                v.tensor_tensor(vv[:, :, :], pair(QB[0]), rows[:, BV, :].unsqueeze(1).to_broadcast([P, QT, D]), ALU.add).then_inc(v_c.sem, 1)

            def moments(i, src, b):
                for q in range(QT):
                    v.bn_stats(stats[:, q, :], src[:, q, :]).then_inc(stat1.sem, 1)
                dve.wait_ge(stat1.sem, stat1.at(b, QT * (i + 1)))
                dve.sem_inc(tick, 1)
                for q in range(QT):
                    ins = v.bn_aggr(mv[:, q, :], stats[:, q, :])
                ins.then_inc(stat2.sem, 1)

            def normalise(b, i, src):
                dve.wait_ge(root_d.sem, root_d.at(b, 2 * i + 2))
                for q in range(QT):
                    ins = v.tensor_scalar(src[:, q, :], src[:, q, :], mv[:, q, 0:1], rs[:, q:q + 1], ALU.subtract, ALU.mult)
                ins.then_inc(norm_d.sem, 1)

            def ln0(b, p):
                dve.wait_ge(out_f.sem, out_f.at(b, 1))
                dve.wait_ge(q_in.sem, q_in.at(b, 48))
                v.tensor_tensor(x1[:, :, :], pair(QB[0]), xr[:, :, :], ALU.add).then_inc(r0_d.sem, 1)
                dve.wait_ge(r0_d.sem, r0_d.at(b, 1))
                moments(0, x1, b)

            def softmax(b, p):
                dve.wait_ge(sco_f.sem, sco_f.at(b, 1))
                v.tensor_reduce(nmx[:, :], pair(QB[1]), AX.X, ALU.max).then_inc(max_d.sem, 1)
                dve.wait_ge(max_d.sem, max_d.at(b, 1))
                v.tensor_scalar(nmx[:, :], nmx[:, :], -SCALE, None, ALU.mult).then_inc(max_d.sem, 1)

            def ln1(b, p):
                dve.wait_ge(p_d.sem, p_d.at(b, 1))
                v.reciprocal(rsum[:, :], ssum[:, :]).then_inc(rsum_d.sem, 1)
                dve.wait_ge(rsum_d.sem, rsum_d.at(b, 1))
                dve.wait_ge(mg_f.sem, mg_f.at(b, 1))
                dve.wait_ge(base_d.sem, base_d.at(b, 3))
                for q in range(QT):
                    ins = v.scalar_tensor_tensor(x2a[:, q, :], pair(QB[0])[:, q, :], rsum[:, q:q + 1], base[:, q, :], ALU.mult, ALU.add)
                ins.then_inc(mg_c.sem, 1)
                dve.wait_ge(mg_c.sem, mg_c.at(b, 1))
                moments(1, x2a, b)

            def ln2(b, p):
                dve.wait_ge(ff_f.sem, ff_f.at(b, 1))
                dve.wait_ge(aff1_d.sem, aff1_d.at(b, 3))
                if x2_st.at(b - 1, 16, True):
                    dve.wait_ge(x2_st.sem, x2_st.at(b - 1, 16))
                v.tensor_tensor(x2[:, :, :], pair(QB[0]), base[:, :, :], ALU.add).then_inc(ff_c.sem, 1)
                dve.wait_ge(ff_c.sem, ff_c.at(b, 1))
                moments(2, x2, b)

            def ln3(b, p):
                dve.wait_ge(aff2_d.sem, aff2_d.at(b, 2))
                v.tensor_tensor(x2[:, :, :], x2[:, :, :], x1[:, :, :], ALU.add).then_inc(res_d.sem, 1)
                dve.wait_ge(res_d.sem, res_d.at(b, 1))
                moments(3, x2, b)

            def router(b, p):
                dve.wait_ge(lg_f.sem, lg_f.at(b, 1))
                v.tensor_tensor(key[:, :, :], QB[2][:, 0:QT * NE].rearrange("p (q e) -> p q e", q=QT),
                                b_r[:, :].unsqueeze(1).to_broadcast([P, QT, NE]), ALU.add).then_inc(lg_c.sem, 1)

            def shared(b, p):
                dve.wait_ge(sh_c.sem, sh_c.at(b, 2))
                v.scalar_tensor_tensor(hs[:, :], hth[:, :], 1.0, hs[:, :], ALU.add, ALU.mult).then_inc(hs_d.sem, 1)

            def shared_out(b, p):
                dve.wait_ge(so_f.sem, so_f.at(b, 1))
                if acc_st.at(b - 1, 16, True):
                    dve.wait_ge(acc_st.sem, acc_st.at(b - 1, 16))
                dve.wait_ge(norm_d.sem, norm_d.at(b, 4))
                v.tensor_tensor(acc[:, :, :], pair(QB[0]), x2[:, :, :], ALU.add).then_inc(acc_d.sem, 1)

            def choose(b, p):
                dve.wait_ge(lg_e.sem, lg_e.at(b, 1))
                v.tensor_scalar(key[:, :, :], key[:, :, :], -1.0, -1.0, ALU.mult, ALU.add).then_inc(key_d.sem, 1)
                dve.wait_ge(key_d.sem, key_d.at(b, 1))
                dve.sem_inc(tick, 1)
                for q in range(QT):
                    v.max(top[:, q, :], key[:, q, :]).then_inc(pick.sem, 1)
                for q in range(QT):
                    dve.wait_ge(pick.sem, pick.at(b, q + 1))
                    dve.sem_inc(tick, 1)
                    v.match_replace(rep[:, q, :], top[:, q, :], key[:, q, :], 1.0).then_inc(pick.sem, 1)
                dve.wait_ge(pick.sem, pick.at(b, 4))
                v.tensor_scalar(msk_b[:, :, :], rep[:, :, :], 0.0, None, ALU.is_gt).then_inc(mask_d.sem, 1)
                for q in range(QT):
                    v.max_index(ti[:, q, :], top[:, q, :], key[:, q, :]).then_inc(pick.sem, 1)
                dve.wait_ge(pick.sem, pick.at(b, 6))
                if scat_d.at(b - 1, 1, True):
                    dve.wait_ge(scat_d.sem, scat_d.at(b - 1, 1))
                v.tensor_copy(e_st[:, :, :], ti[:, :, :]).then_inc(pick.sem, 1)
                v.reciprocal(pr[:, :, :], top[:, :, :]).then_inc(pick.sem, 1)
                dve.wait_ge(pick.sem, pick.at(b, 8))
                v.tensor_reduce(psm[:, :], pr[:, :, :], AX.X, ALU.add).then_inc(pick.sem, 1)
                dve.wait_ge(pick.sem, pick.at(b, 9))
                v.tensor_scalar(psm[:, :], psm[:, :], -1.0, 1e-9, ALU.mult, ALU.add).then_inc(pick.sem, 1)
                dve.wait_ge(pick.sem, pick.at(b, 10))
                v.reciprocal(psm[:, :], psm[:, :]).then_inc(pick.sem, 1)
                v.tensor_scalar(pr[:, :, :], pr[:, :, :], -2.5, None, ALU.mult).then_inc(pick.sem, 1)
                dve.wait_ge(pick.sem, pick.at(b, 12))
                w8 = QT * TOPK
                v.tensor_tensor(gate[:, bass.ds(b * w8, w8)].rearrange("p (q k) -> p q k", q=QT), pr[:, :, :],
                                psm[:, :].unsqueeze(2).to_broadcast([P, QT, TOPK]), ALU.mult).then_inc(pick.sem, 1)
                v.tensor_copy(sel_e[:, bass.ds(b * w8, w8)], e_st[:, :, :].rearrange("p q k -> p (q k)")).then_inc(pick.sem, 1)

            def rank(b, p):
                dve.wait_ge(cum_f.sem, cum_f.at(b, 1))
                for q in range(QT):
                    for k in range(TOPK):
                        v.scalar_tensor_tensor(junk[:, :], iota_e[:, :], e_st[:, q, k:k + 1], QB[1][:, q * NE:(q + 1) * NE],
                                               ALU.is_equal, ALU.mult, accum_out=r_st[:, q, k:k + 1]).then_inc(rank_s.sem, 1)
                        dve.wait_ge(rank_s.sem, rank_s.at(b, q * TOPK + k + 1))
                dve.sem_inc(cum_c.sem, 1)
                v.tensor_tensor(m_sum[:, :], m_sum[:, :], msk_b[:, 0, :], ALU.add).then_inc(addr.sem, 1)
                v.scalar_tensor_tensor(ad_f[:, :, :], e_st[:, :, :], float(CAP), r_st[:, :, :], ALU.mult, ALU.add).then_inc(addr.sem, 1)
                dve.wait_ge(addr.sem, addr.at(b, 2))
                v.tensor_tensor(m_sum[:, :], m_sum[:, :], msk_b[:, 1, :], ALU.add).then_inc(msum_d.sem, 1)
                w8 = QT * TOPK
                v.tensor_copy(sel_r[:, bass.ds(b * w8, w8)], r_st[:, :, :].rearrange("p q k -> p (q k)")).then_inc(selr_d.sem, 1)
                v.tensor_copy(id_st[:, :], ids_all[:, bass.ds(b * QT, QT)])
                v.tensor_copy(ad_i[:, :, :], ad_f[:, :, :]).then_inc(addr_d.sem, 1)

            def batch(b, p):
                conv_(b, p)
                gate_z(b, p)
                u_(b, p)
                delta(b, p)
                for t in range(NTAU):
                    scan(b, p, t)
                    outflow(b, p, t)
                y(b, p, 0)
                y(b, p, 1)
                kv(b, p)
                ln0(b, p)
                normalise(b, 0, x1)
                softmax(b, p)
                ln1(b, p)
                normalise(b, 1, x2a)
                ln2(b, p)
                normalise(b, 2, x2)
                ln3(b, p)
                normalise(b, 3, x2)
                router(b, p)
                shared(b, p)
                shared_out(b, p)
                choose(b, p)
                rank(b, p)

            all_batches(dve, batch)
            dve.wait_ge(selr_d.sem, selr_d.at(NB - 1, 1))

        front.close()

        cnt_f, cnt_c = sig("cnt_f"), sig("cnt_c")
        tab_s = sig("tab_s")
        tab_w, tab_in = sig("tab_w"), sig("tab_in")
        wt_in = [sig(f"wt_in{i}", 16) for i in range(UNROLL)]
        ids_in = [sig(f"ids_in{i}", 16) for i in range(UNROLL)]
        xg_in = [sig(f"xg_in{i}", 16) for i in range(UNROLL)]
        y_st = [sig(f"y_st{i}", 16) for i in range(UNROLL)]
        xgT_f, xgT_c = sig("xgT_f", UNROLL), sig("xgT_c", UNROLL)
        up_f, up_c = sig("up_f", UNROLL), sig("up_c", UNROLL)
        dn_f, dn_c = sig("dn_f", UNROLL), sig("dn_c", UNROLL)
        slot_d = sig("slot_d", 2)
        slot_i = sig("slot_i")

        slot = sb("slot", [P, 2 * TURNS])
        slot_n = sb("slot_n", [P, 2 * TURNS], I32)
        mid = ExitStack()

        def sm(name, shape, dt=FP32):
            return mid.enter_context(nc.sbuf_tensor(name, shape, dt))

        cnt = sm("cnt", [P, NE])
        cnt_i = sm("cnt_i", [P, NE], I32)
        nblk = sm("nblk", [P, NE])
        incl = sm("incl", [P, NE])
        first = sm("first", [P, NE])
        one_f = sm("one_f", [P, NE])
        jn_i = sm("jn_i", [BJ, 3], I32)
        jn = sm("jn", [BJ, 3])
        blk_e = sm("blk_e", [BJ, 3])
        blk_b = sm("blk_b", [BJ, 3])
        blk_o = sm("blk_o", [BJ, 3])
        blk_i = sm("blk_i", [BJ, 3, 2], I32)
        junk2 = sm("junk2", [P, 3, NE])
        junk3 = sm("junk3", [P, 2, NE])
        tab = sm("tab", [1, NBLK * 2], I32)
        wt = [sm(f"wt{i}", [P, KD * INTER + D]) for i in range(UNROLL)]
        idb = [sm(f"idb{i}", [P, 1], I32) for i in range(UNROLL)]
        xg = [sm(f"xg{i}", [P, D]) for i in range(UNROLL)]
        xgT = [sm(f"xgT{i}", [P, KD, P]) for i in range(2)]
        h1 = [sm(f"h1{i}", [P, P]) for i in range(2)]
        ys = [sm(f"ys{i}", [P, D]) for i in range(UNROLL)]
        XT = [PB[0], PB[1]]
        UP = [Y[0], Y[1]]
        DN = [QB[0], QB[1]]
        CN = QB[2]

        block = mid.enter_context(nc.Block())

        @block.sync
        def _(sp):
            sp.wait_ge(tab_s.sem, tab_s.at(0, 13))
            sp.dma_start(blk_dram.rearrange("(c p) f -> p c f", p=BJ), blk_i[:, :, :]).then_inc(tab_w.sem, 16)
            sp.wait_ge(tab_w.sem, 16)
            sp.dma_start(tab[0:1, :], blk_dram.rearrange("j f -> (j f)").unsqueeze(0)).then_inc(tab_in.sem, 16)
            sp.wait_ge(tab_in.sem, 16)

            def load(i, s_):
                at = i * (2 * UNROLL) + 2 * s_
                e = sp.value_load(tab[0:1, bass.ds(at, 1)], min_val=0, max_val=NE - 1)
                o = sp.value_load(tab[0:1, bass.ds(at + 1, 1)], min_val=0, max_val=NE * CAP - P)
                if xg_in[s_].at(i - 1, 16, True):
                    sp.wait_ge(xg_in[s_].sem, xg_in[s_].at(i - 1, 16))
                sp.sem_inc(tick, 1)
                sp.dma_start(idb[s_][:, :], tok_dram[bass.ds(o, P), :]).then_inc(ids_in[s_].sem, 16)
                if dn_f.at(i - 1, s_ + 1, True):
                    sp.wait_ge(dn_f.sem, dn_f.at(i - 1, s_ + 1))
                sp.sem_inc(tick, 1)
                sp.dma_start(wt[s_][:, :], a["w_moe"][bass.ds(e * P, P), :]).then_inc(wt_in[s_].sem, 16)

            for s_ in range(UNROLL):
                load(0, s_)
            with sp.Fori(1, TURNS) as i:
                for s_ in range(UNROLL):
                    load(i, s_)

        @block.gpsimd
        def _(pool):
            nc.gpsimd.iota(jn_i[:, :], pattern=[[BJ, 3]], base=0, channel_multiplier=1).then_inc(cnt_c.sem, 1)

            def gather(i, s_):
                pool.wait_ge(ids_in[s_].sem, ids_in[s_].at(i, 16))
                if xgT_f.at(i - 1, s_ + 1, True):
                    pool.wait_ge(xgT_f.sem, xgT_f.at(i - 1, s_ + 1))
                pool.sem_inc(tick, 1)
                nc.gpsimd.indirect_dma_start(xg[s_][:, :], None, x2_dram,
                                             bass.IndirectOffsetOnAxis(ap=idb[s_][:, 0:1], axis=0)).then_inc(xg_in[s_].sem, 16)

            for s_ in range(UNROLL):
                gather(0, s_)
            with pool.Fori(1, TURNS) as i:
                for s_ in range(UNROLL):
                    gather(i, s_)

        @block.tensor
        def _(pe):
            mm = nc.tensor.matmul
            mm(CN[:, 0:NE], ones[:, :], m_sum[:, :], start=True, stop=True).then_inc(cnt_f.sem, 1)

            def turn(i, s_):
                pe.wait_ge(xg_in[s_].sem, xg_in[s_].at(i, 16))
                if xgT_c.at(i, s_ - 1, True):
                    pe.wait_ge(xgT_c.sem, xgT_c.at(i, s_ - 1))
                for k in range(KD):
                    ins = nc.tensor.transpose(XT[s_ % 2][:, k * P:(k + 1) * P], xg[s_][:, k * P:(k + 1) * P], ident[:, :])
                ins.then_inc(xgT_f.sem, 1)

            def up(i, s_):
                pe.wait_ge(xgT_c.sem, xgT_c.at(i, s_ + 1))
                pe.wait_ge(wt_in[s_].sem, wt_in[s_].at(i, 16))
                if up_c.at(i, s_ - 1, True):
                    pe.wait_ge(up_c.sem, up_c.at(i, s_ - 1))
                for k in range(KD):
                    ins = mm(UP[s_ % 2][:, 0:P], wt[s_][:, k * INTER:(k + 1) * INTER], xgT[s_ % 2][:, k, :], start=k == 0, stop=k == KD - 1)
                ins.then_inc(up_f.sem, 1)

            def down(i, s_):
                pe.wait_ge(up_c.sem, up_c.at(i, s_ + 1))
                if dn_c.at(i, s_ - 1, True):
                    pe.wait_ge(dn_c.sem, dn_c.at(i, s_ - 1))
                mm(DN[s_ % 2][:, 0:D], h1[s_ % 2][:, :], wt[s_][:, KD * INTER:], start=True, stop=True).then_inc(dn_f.sem, 1)

            def body(i):
                for s_ in range(UNROLL):
                    turn(i, s_)
                    if s_ > 0:
                        down(i, s_ - 1)
                    elif not (isinstance(i, int) and i == 0):
                        down(i - 1, UNROLL - 1)
                    up(i, s_)

            body(0)
            with pe.Fori(1, TURNS) as i:
                body(i)
            down(TURNS - 1, UNROLL - 1)

        @block.scalar
        def _(act):
            s = nc.scalar

            def silu(i, s_):
                act.wait_ge(up_f.sem, up_f.at(i, s_ + 1))
                if dn_f.at(i, s_ - 1, True):
                    act.wait_ge(dn_f.sem, dn_f.at(i, s_ - 1))
                s.activation(h1[s_ % 2][:, :], UP[s_ % 2][:, 0:P], ACT.Silu).then_inc(up_c.sem, 1)

            def store(i, s_):
                act.wait_ge(dn_f.sem, dn_f.at(i, s_ + 1))
                if y_st[s_].at(i - 1, 16, True):
                    act.wait_ge(y_st[s_].sem, y_st[s_].at(i - 1, 16))
                s.activation(ys[s_][:, :], DN[s_ % 2][:, 0:D], ACT.Copy).then_inc(dn_c.sem, 1)
                act.wait_ge(dn_c.sem, dn_c.at(i, s_ + 1))
                act.dma_start(y_dram[bass.ds((i * UNROLL + s_) * P, P), :], ys[s_][:, :]).then_inc(y_st[s_].sem, 16)

            def body(i):
                for s_ in range(UNROLL):
                    if s_ > 0:
                        store(i, s_ - 1)
                    elif not (isinstance(i, int) and i == 0):
                        store(i - 1, UNROLL - 1)
                    silu(i, s_)

            body(0)
            with act.Fori(1, TURNS) as i:
                body(i)
            store(TURNS - 1, UNROLL - 1)
            for s_ in range(UNROLL):
                act.wait_ge(y_st[s_].sem, y_st[s_].at(TURNS - 1, 16))

        @block.vector
        def _(dve):
            v = nc.vector
            n = [0]

            def link(ins):
                n[0] += 1
                ins.then_inc(tab_s.sem, 1)
                dve.wait_ge(tab_s.sem, n[0])

            dve.wait_ge(cnt_f.sem, 1)
            dve.wait_ge(cnt_c.sem, 1)
            link(v.tensor_scalar(cnt_i[:, :], CN[:, 0:NE], float(P - 1), None, ALU.add))
            link(v.tensor_scalar(cnt_i[:, :], cnt_i[:, :], 7, None, ALU.arith_shift_right))
            link(v.tensor_copy(nblk[:, :], cnt_i[:, :]))
            v.memset(one_f[:, :], 1.0).then_inc(tab_s.sem, 1)
            n[0] += 1
            link(v.tensor_copy(jn[:, :], jn_i[:, :]))
            link(v.tensor_tensor_scan(incl[:, :], one_f[:, :], nblk[:, :], 0.0, ALU.mult, ALU.add))
            link(v.tensor_tensor(first[:, :], incl[:, :], nblk[:, :], ALU.subtract))
            for c in range(3):
                v.scalar_tensor_tensor(junk2[0:BJ, c, :], incl[0:BJ, :], jn[:, c:c + 1], one_f[0:BJ, :], ALU.is_le, ALU.mult,
                                       accum_out=blk_e[:, c:c + 1])
            link(v.tensor_scalar(first[:, :], first[:, :], float(P), None, ALU.mult))
            for c in range(3):
                ins = v.scalar_tensor_tensor(junk2[0:BJ, c, :], incl[0:BJ, :], jn[:, c:c + 1], nblk[0:BJ, :], ALU.is_le, ALU.mult,
                                             accum_out=blk_b[:, c:c + 1])
            link(ins)
            link(v.tensor_tensor(blk_b[:, :], jn[:, :], blk_b[:, :], ALU.subtract))
            link(v.tensor_scalar(blk_b[:, :], blk_b[:, :], float(P), None, ALU.mult))
            link(v.scalar_tensor_tensor(blk_o[:, :], blk_e[:, :], float(CAP), blk_b[:, :], ALU.mult, ALU.add))
            v.tensor_scalar(blk_i[:, :, 0], blk_e[:, :], float(NE - 1), None, ALU.min)
            link(v.tensor_scalar(blk_i[:, :, 1], blk_o[:, :], float(NE * CAP - P), None, ALU.min))
            assert n[0] == 13

            def body(i):
                for s_ in range(UNROLL):
                    dve.wait_ge(xgT_f.sem, xgT_f.at(i, s_ + 1))
                    if up_f.at(i, s_ - 1, True):
                        dve.wait_ge(up_f.sem, up_f.at(i, s_ - 1))
                    v.tensor_copy(xgT[s_ % 2][:, :, :], XT[s_ % 2][:, 0:KD * P].rearrange("p (k t) -> p k t", k=KD)).then_inc(xgT_c.sem, 1)
                    if s_ < 2:
                        f = i * 2 + s_
                        if slot_d.at(i - 1, s_ + 1, True):
                            dve.wait_ge(slot_d.sem, slot_d.at(i - 1, s_ + 1))
                        v.scalar_tensor_tensor(junk3[:, s_, :], iota_e[:, :], sel_e[:, bass.ds(f, 1)], first[:, :],
                                               ALU.is_equal, ALU.mult, accum_out=slot[:, bass.ds(f, 1)]).then_inc(slot_d.sem, 1)

            body(0)
            with dve.Fori(1, TURNS) as i:
                body(i)
            dve.wait_ge(slot_d.sem, slot_d.at(TURNS - 1, 2))
            v.tensor_tensor(slot[:, :], slot[:, :], sel_r[:, :], ALU.add).then_inc(slot_i.sem, 1)
            dve.wait_ge(slot_i.sem, 1)
            v.tensor_copy(slot_n[:, :], slot[:, :]).then_inc(slot_i.sem, 1)
            dve.wait_ge(slot_i.sem, 2)

        mid.close()

        gat_in = [sig(f"gat_in{i}", 8 * TOPK) for i in range(2)]
        acc_in = [sig(f"acc_in{i}", 8) for i in range(2)]
        out_st = [sig(f"out_st{i}", 8) for i in range(2)]
        add_s = sig("add_s", TOPK)
        sidx = sig("sidx")
        bst, bag = sig("bst"), sig("bag")
        var_d, std_d, rstd_d, fin_d = sig("var_d"), sig("std_d"), sig("rstd_d"), sig("fin_d")
        end = ExitStack()

        def se(name, shape, dt=FP32):
            return end.enter_context(nc.sbuf_tensor(name, shape, dt))

        G = [se(f"G{i}", [P, TOPK, D]) for i in range(2)]
        si = [se(f"si{i}", [P, TOPK], I32) for i in range(2)]
        ac = [se(f"ac{i}", [P, D]) for i in range(2)]
        bs = se("bs", [P, 6])
        bm = se("bm", [P, 2])
        vr = se("vr", [P, 1])
        sd = se("sd", [P, 1])
        rd = se("rd", [P, 1])

        def tiles(eng, body):
            for t in range(2):
                body(t, t)
            with eng.Fori(1, NTILE // 2) as i:
                for p in range(2):
                    body(i * 2 + p, p)

        block = end.enter_context(nc.Block())

        @block.sync
        def _(sp):
            def body(t, p):
                if out_st[p].at(t - p - 2, 16, True):
                    sp.wait_ge(out_st[p].sem, out_st[p].at(t - p - 2, 16))
                sp.dma_start(ac[p][:, :], acc_dram[bass.ds(t * P, P), :]).then_inc(acc_in[p].sem, 16)
                if isinstance(t, int) and t == 0:
                    return
                if fin_d.at(t - 1, 1, True):
                    sp.wait_ge(fin_d.sem, fin_d.at(t - 1, 1))
                sp.dma_start(out[bass.ds((t - 1) * P, P), :], ac[1 - p][:, :]).then_inc(out_st[1 - p].sem, 16)

            tiles(sp, body)
            sp.wait_ge(fin_d.sem, fin_d.at(NTILE - 1, 1))
            sp.dma_start(out[(NTILE - 1) * P:, :], ac[(NTILE - 1) % 2][:, :]).then_inc(out_st[1].sem, 16)
            for p in range(2):
                sp.wait_ge(out_st[p].sem, out_st[p].at(NTILE - 2, 16))

        @block.gpsimd
        def _(pool):
            def body(t, p):
                pool.wait_ge(sidx.sem, sidx.at(t, 1))
                if add_s.at(t - 2, TOPK, True):
                    pool.wait_ge(add_s.sem, add_s.at(t - 2, TOPK))
                pool.sem_inc(tick, 1)
                for k in range(TOPK):
                    nc.gpsimd.indirect_dma_start(G[p][:, k, :], None, y_dram,
                                                 bass.IndirectOffsetOnAxis(ap=si[p][:, k:k + 1], axis=0)).then_inc(gat_in[p].sem, 16)

            tiles(pool, body)

        @block.scalar
        def _(act):
            def body(t, p):
                act.wait_ge(var_d.sem, var_d.at(t, 1))
                nc.scalar.activation(sd[:, :], vr[:, :], ACT.Sqrt).then_inc(std_d.sem, 1)

            tiles(act, body)

        @block.vector
        def _(dve):
            v = nc.vector

            def body(t, p):
                if gat_in[p].at(t - p - 2, 16 * TOPK, True):
                    dve.wait_ge(gat_in[p].sem, gat_in[p].at(t - p - 2, 16 * TOPK))
                v.tensor_copy(si[p][:, :], slot_n[:, bass.ds(t * TOPK, TOPK)]).then_inc(sidx.sem, 1)

            def add(t, p):
                dve.wait_ge(acc_in[p].sem, acc_in[p].at(t - p, 16))
                dve.wait_ge(gat_in[p].sem, gat_in[p].at(t - p, 16 * TOPK))
                for k in range(TOPK):
                    dve.wait_ge(add_s.sem, add_s.at(t, k))
                    v.scalar_tensor_tensor(ac[p][:, :], G[p][:, k, :], gate[:, bass.ds(t * TOPK + k, 1)], ac[p][:, :],
                                           ALU.mult, ALU.add).then_inc(add_s.sem, 1)
                dve.wait_ge(add_s.sem, add_s.at(t, TOPK))
                v.bn_stats(bs[:, :], ac[p][:, :]).then_inc(bst.sem, 1)
                dve.wait_ge(bst.sem, bst.at(t, 1))
                dve.sem_inc(tick, 1)
                v.bn_aggr(bm[:, :], bs[:, :]).then_inc(bag.sem, 1)
                dve.wait_ge(bag.sem, bag.at(t, 1))
                v.tensor_scalar(vr[:, :], bm[:, 1:2], LN_EPS, None, ALU.add).then_inc(var_d.sem, 1)
                dve.wait_ge(std_d.sem, std_d.at(t, 1))
                v.reciprocal(rd[:, :], sd[:, :]).then_inc(rstd_d.sem, 1)
                dve.wait_ge(rstd_d.sem, rstd_d.at(t, 1))
                v.tensor_scalar(ac[p][:, :], ac[p][:, :], bm[:, 0:1], rd[:, 0:1], ALU.subtract, ALU.mult).then_inc(fin_d.sem, 1)

            body(0, 0)
            body(1, 1)
            add(0, 0)
            body(2, 0)
            add(1, 1)
            body(3, 1)
            with dve.Fori(1, NTILE // 2 - 1) as i:
                for p in range(2):
                    add(i * 2 + p, p)
                    body(i * 2 + (p + 2), p)
            for p in range(2):
                add(NTILE - 2 + p, p)

        end.close()


def chunked(w, p=128):
    n = w.shape[0] // p
    return np.ascontiguousarray(w.reshape(n, p, *w.shape[1:]).swapaxes(0, 1))


def kernel(**inputs):
    import concourse.bacc as _bacc
    from concourse import mybir as _mybir
    from concourse.bass_utils import run_bass_kernel_spmd as _run

    g = {k: np.asarray(v) for k, v in inputs.items()}
    m = {k[len("L0_attn_h_"):]: v for k, v in g.items() if k.startswith("L0_attn_h_")}
    x = {k[len("L0_xattn_"):]: v for k, v in g.items() if k.startswith("L0_xattn_")}
    f = {k[len("L0_ffn_"):]: v for k, v in g.items() if k.startswith("L0_ffn_")}
    xs, cs = g["x"].reshape(NT, D), g["ctx_1024"].reshape(NT, D)
    xp = m["x_proj_w"]
    xp = np.concatenate([xp[:R], np.zeros((R, DI), xp.dtype), xp[R:]], 0)
    moe = np.concatenate([f["w_gate"].reshape(NE, INTER, KD, P).transpose(0, 3, 2, 1).reshape(NE, P, KD * INTER),
                          f["w_down"].transpose(0, 2, 1)], 2).reshape(NE * P, KD * INTER + D)
    arrays = {
        "x": xs, "xT": chunked(xs.T), "c": cs, "cT": chunked(cs.T),
        "w_in": chunked(m["in_proj_w"].T), "conv_w": chunked(m["conv_w"]), "conv_b": chunked(m["conv_b"]),
        "w_xp": chunked(xp.T), "w_dt": m["dt_proj_w"].T, "dt_b": chunked(m["dt_proj_b"]),
        "A_log": chunked(m["A_log"]), "D": chunked(m["D_param"]), "w_out": chunked(m["out_proj_w"].T),
        "w_q": chunked(x["Wq"]), "w_k": chunked(x["Wk"]), "w_v": chunked(x["Wv"]), "w_o": chunked(x["Wo"]),
        "b_q": chunked(x["bq"]), "b_k": chunked(x["bk"]), "w_1": chunked(x["W1"]), "b_1": chunked(x["b1"]),
        "w_2": chunked(x["W2"]), "w_r": chunked(f["router_w"].T), "b_r": f["expert_bias"],
        "ws_g": chunked(f["w_gate_shared"].T), "ws_d": f["w_down_shared"].T, "w_moe": moe,
    } | {n: x[n] for n in ROWS}
    arrays = {k: np.ascontiguousarray(v) for k, v in arrays.items()}
    nc = _bacc.Bacc("TRN2", target_bir_lowering=False, num_devices=1)
    aps = {k: nc.dram_tensor(f"in_{k}", v.shape, _mybir.dt.from_np(v.dtype), kind="ExternalInput").ap()
           for k, v in arrays.items()}
    out = nc.dram_tensor("out", (NT, D), FP32, kind="ExternalOutput").ap()
    decoder_kernel(nc, aps, out)
    r = _run(nc, [{f"in_{k}": v for k, v in arrays.items()}], core_ids=[0])
    return r.results[0]["out"].reshape(NB, T, D)
```

```python
import concourse.bass as bass
from concourse import mybir
from contextlib import ExitStack
import numpy as np

FP32 = mybir.dt.float32
BF16 = mybir.dt.bfloat16
I32 = mybir.dt.int32
U32 = mybir.dt.uint32
ACT = mybir.ActivationFunctionType
ALU = mybir.AluOpType
AX = mybir.AxisListType

P = 128
NB, T, D = 8, 256, 256
NT = NB * T
KD = D // P
QT = T // P
DI = 512
NC = DI // P
NS = 16
R = 16
TAPS = 4
XP = 64
NG = 4
SG = NS // NG
NTAU = NG * NC
NBUF = 4
LEAD = 2
FF = 1024
KF = FF // P
NE, TOPK, INTER = 160, 8, 128
CAP = NT
NTILE = NT // P
NBLK = NT * TOPK // P + NE
BJ = NBLK // 3
LN_EPS = 1e-5
SCALE = 1.0 / 16.0
UNROLL = 8
TURNS = NBLK // UNROLL
SURE = NT * TOPK // P // UNROLL
YG = 4
NSEL = NTILE * TOPK
ROWS = ("bv", "bo", "ln1_g", "ln1_b", "b2", "ln2_g", "ln2_b")


def whole(t):
    return t[tuple(slice(None) for _ in t.shape)]


class Sig:

    def __init__(self, sem, per):
        self.sem, self.per = sem, per

    def at(self, b, c, due=False):
        v = b * self.per + c
        return (not isinstance(v, int) or v > 0) if due else v


def decoder_kernel(nc, a, out):
    ctx = ExitStack()
    with ctx:
        def sb(name, shape, dt=FP32):
            return ctx.enter_context(nc.sbuf_tensor(name, shape, dt))

        def ps(name, shape=(P, 512), dt=FP32):
            return ctx.enter_context(nc.psum_tensor(name, list(shape), dt))

        def sig(name, per=1):
            return Sig(ctx.enter_context(nc.semaphore(name)), per)

        x2_dram = nc.dram_tensor("x2_dram", (NT, D), FP32, kind="Internal").ap()
        acc_dram = nc.dram_tensor("acc_dram", (NT, D), FP32, kind="Internal").ap()
        bc_dram = nc.dram_tensor("bc_dram", (NB, 2, NS * T), FP32, kind="Internal").ap()
        tok_dram = nc.dram_tensor("tok_dram", (NE * CAP, 1), I32, kind="Internal").ap()
        y_dram = nc.dram_tensor("y_dram", (NBLK * P, D), FP32, kind="Internal").ap()
        blk_dram = nc.dram_tensor("blk_dram", (NBLK,), I32, kind="Internal").ap()

        w_in = sb("w_in", [P, KD, 2 * DI])
        w_conv = sb("w_conv", [P, NC, TAPS])
        b_conv = sb("b_conv", [P, NC])
        w_xp = sb("w_xp", [P, NC, XP])
        w_dt = sb("w_dt", [R, DI])
        b_dt = sb("b_dt", [P, NC])
        a_neg = sb("a_neg", [P, NC, NS])
        d_par = sb("d_par", [P, NC])
        w_out = sb("w_out", [P, NC, D])
        w_q = sb("w_q", [P, KD, D])
        w_k = sb("w_k", [P, KD, D])
        w_v = sb("w_v", [P, KD, D])
        w_o = sb("w_o", [P, KD, D])
        b_q = sb("b_q", [P, KD])
        b_k = sb("b_k", [P, KD])
        w_1 = sb("w_1", [P, KD, FF])
        b_1 = sb("b_1", [P, KF])
        w_2 = sb("w_2", [P, KF, D])
        rows = sb("rows", [P, 7, D])
        BV, BO, G1, B1, B2, G2, BB2 = range(7)
        w_r = sb("w_r", [P, KD, NE])
        b_r = sb("b_r", [P, NE])
        ws_g = sb("ws_g", [P, KD, INTER])
        ws_d = sb("ws_d", [P, D])
        ident = sb("ident", [P, P])
        earlier = sb("earlier", [P, P], BF16)
        ones = sb("ones", [P, P], BF16)
        iota_i = sb("iota_i", [P, NE], I32)
        iota_e = sb("iota_e", [P, NE])
        ids_all = sb("ids_all", [P, NTILE], I32)
        m_half = sb("m_half", [P, QT])
        zeros = sb("zeros", [P, D])

        sel_e = sb("sel_e", [P, NSEL])
        sel_r = sb("sel_r", [P, NSEL])
        gate = sb("gate", [P, NSEL])
        m_sum = sb("m_sum", [P, NE], BF16)

        PB = [ps("PB0"), ps("PB1")]
        Y = [ps("Y0"), ps("Y1")]
        QA = [ps(f"QA{i}") for i in range(2)]
        QF = [ps(f"QF{i}") for i in range(2)]

        w_mamba = sig("w_mamba")
        w_rest = sig("w_rest")
        k_pool = sig("k_pool")
        k_scaled = sig("k_scaled")
        zeroed = sig("zeroed")
        xt_in = sig("xt_in", 16)
        proj_f = sig("proj_f", 7)
        proj_c = sig("proj_c", 6)
        conv = sig("conv", NC * TAPS)
        z_tanh = sig("z_tanh", 2)
        gate_d = sig("gate_d")
        u_tanh = sig("u_tanh")
        u_d = sig("u_d")
        xdb_c = sig("xdb_c")
        bc_w = sig("bc_w", 16)
        bc_in = [sig(f"bc_in{i}", 8 * NG) for i in range(2)]
        softp = sig("softp", 3)
        lost = sig("lost", 3)
        dl_d = sig("dl_d")
        du_d = sig("du_d")
        decay_d = sig("decay_d", NTAU)
        inflow_d = sig("inflow_d", NTAU)
        scan_d = sig("scan_d", NTAU)
        outflow_d = sig("outflow_d", NTAU)
        sum_d = sig("sum_d", NTAU)
        y_read = sig("y_read", NC)
        y_d = sig("y_d", NC)
        q_in = sig("q_in", 48)
        v_f, v_c, kT_f, kT_c = sig("v_f"), sig("v_c"), sig("kT_f"), sig("kT_c")
        out_f, r0_d = sig("out_f"), sig("r0_d")
        x1T_f, x1T_c, qT_f, qT_c = sig("x1T_f"), sig("x1T_c"), sig("qT_f"), sig("qT_c")
        sco_f, max_d, p_d = sig("sco_f"), sig("max_d", 2), sig("p_d")
        pT_f, pT_c, aT_f, aT_c = sig("pT_f"), sig("pT_c"), sig("aT_f"), sig("aT_c")
        rsum_d, mg_f, mg_c = sig("rsum_d"), sig("mg_f"), sig("mg_c")
        x2aT_f, x2aT_c, h_f, h_c = sig("x2aT_f"), sig("x2aT_c"), sig("h_f", 4), sig("h_c", 4)
        ff_f, ff_c = sig("ff_f"), sig("ff_c")
        stat1 = [sig(f"stat1_{i}", QT) for i in range(4)]
        stat2 = [sig(f"stat2_{i}") for i in range(4)]
        root_d = [sig(f"root_d{i}", 2) for i in range(4)]
        norm_d = [sig(f"norm_d{i}") for i in range(4)]
        base_d = sig("base_d", 3)
        aff1_d = sig("aff1_d", 3)
        aff2_d = sig("aff2_d", 2)
        res_d = sig("res_d")
        x2T_f, x2T_c = sig("x2T_f"), sig("x2T_c")
        lg_f, lg_c, lg_e, key_d = sig("lg_f"), sig("lg_c"), sig("lg_e"), sig("key_d")
        sh_f, sh_c, hs_d, so_f, acc_d = sig("sh_f"), sig("sh_c", 2), sig("hs_d"), sig("so_f"), sig("acc_d")
        x2_st, acc_st = sig("x2_st", 16), sig("acc_st", 16)
        pick = sig("pick", 14)
        mask_d, cum_f, cum_c, msum_d = sig("mask_d"), sig("cum_f"), sig("cum_c"), sig("msum_d")
        addr = sig("addr", 2)
        addr_d = sig("addr_d")
        scat = sig("scat", 16 * QT * TOPK)
        settled = sig("settled")
        y_zero = sig("y_zero", 16)
        zero_read, a_exp, k_conv = sig("zero_read"), sig("a_exp"), sig("k_conv")
        rank_s, selr_d = sig("rank_s", QT * TOPK), sig("selr_d")
        tick = sig("tick").sem

        front = ExitStack()
        def sf(name, shape, dt=FP32):
            return front.enter_context(nc.sbuf_tensor(name, shape, dt))

        xt = sf("xt", [P, KD, T])
        xr = sf("xr", [P, QT, D])
        ct = sf("ct", [P, KD, T])
        cr = sf("cr", [P, QT, D])
        xin = sf("xin", [P, NC, TAPS - 1 + T])
        cv = sf("cv", [P, NC, T])
        th = sf("th", [P, NC, T])
        u = [sf(f"u{i}", [P, NC, T]) for i in range(2)]
        sz = [sf(f"sz{i}", [P, NC, T]) for i in range(2)]
        dl = [sf(f"dl{i}", [P, NC, T]) for i in range(2)]
        du = [sf(f"du{i}", [P, NC, T]) for i in range(2)]
        xdb = sf("xdb", [XP, T])
        yb = sf("yb", [P, NC, T])
        bc = [sf(f"bc{i}", [P, 2, SG, T]) for i in range(2)]
        da = [sf(f"da{i}", [P, SG, T]) for i in range(NBUF)]
        hb = [sf(f"hb{i}", [P, SG, T]) for i in range(NBUF)]
        x1 = [sf(f"x1_{i}", [P, QT, D]) for i in range(2)]
        aT = sf("aT", [P, KD, T])
        fT = sf("fT", [P, KD, T])
        qT = sf("qT", [P, KD, T])
        kT = sf("kT", [P, KD, T])
        vv = sf("vv", [P, QT, D])
        pe_ = sf("pe_", [P, QT, T])
        base = sf("base", [P, QT, D])
        base2 = sf("base2", [P, QT, D])
        x2a = sf("x2a", [P, QT, D])
        hT = sf("hT", [P, KF, T])
        x2 = sf("x2", [P, QT, D])
        hs = sf("hs", [P, T])
        hth = sf("hth", [P, T])
        acc = sf("acc", [P, QT, D])
        stats = sf("stats", [P, 4, QT, 6])
        mv = sf("mv", [P, 4, QT, 2])
        ve = sf("ve", [P, 4, QT])
        rs = sf("rs", [P, 4, QT])
        nmx = sf("nmx", [P, QT])
        ssum = sf("ssum", [P, QT])
        rsum = sf("rsum", [P, QT])
        key = sf("key", [P, QT, NE])
        rep = sf("rep", [P, QT, NE])
        msk_b = sf("msk_b", [P, QT, NE], BF16)
        junk = [sf(f"junk{i}", [P, NE]) for i in range(2)]
        top = sf("top", [P, QT, TOPK])
        ti = sf("ti", [P, QT, TOPK], U32)
        pr = sf("pr", [P, QT, TOPK])
        psm = sf("psm", [P, QT])
        e_st = sf("e_st", [P, QT, TOPK])
        r_st = sf("r_st", [P, QT, TOPK])
        ad_f = sf("ad_f", [P, QT, TOPK])
        ad_i = sf("ad_i", [P, QT, TOPK], I32)
        id_st = sf("id_st", [P, QT], I32)
        zi = th[:, :, :].rearrange("p c t -> p (c t)").bitcast(I32)

        def pair(bank):
            return bank[:, :].rearrange("p (c t) -> p c t", c=2)

        def exists(b):
            return not isinstance(b, int) or 0 <= b < NB

        def tile_at(s, p, t):
            if t < 0:
                return s - 1, 1 - p, t + NTAU
            if t >= NTAU:
                return s + 1, 1 - p, t - NTAU
            return s, p, t

        def all_turns(eng, turn):
            for s in range(-1, 3):
                turn(s, s % 2)
            with eng.Fori(1, 3) as i:
                for k in range(2):
                    turn(i * 2 + (k + 1), 1 - k)
            for s in range(7, NB + 3):
                turn(s, s % 2)

        block = front.enter_context(nc.Block())

        @block.sync
        def _(sp):
            for dst, src in ((w_in, "w_in"), (w_conv, "conv_w"), (b_conv, "conv_b"), (w_xp, "w_xp"),
                             (w_dt, "w_dt"), (b_dt, "dt_b"), (a_neg, "A_log"), (d_par, "D")):
                sp.dma_start(whole(dst), a[src]).then_inc(w_mamba.sem, 16)

            def x_load(b):
                if proj_f.at(b - 1, 4, True):
                    sp.wait_ge(proj_f.sem, proj_f.at(b - 1, 4))
                sp.sem_inc(tick, 1)
                sp.dma_start(xt[:, :, :], a["xT"][:, :, bass.ts(b, T)]).then_inc(xt_in.sem, 16)

            def bc_out(b):
                sp.wait_ge(xdb_c.sem, xdb_c.at(b, 1))
                sp.sem_inc(tick, 1)
                sp.dma_start(bc_dram[b].rearrange("a (n t) -> (a n) t", n=NS), xdb[2 * R:XP, :]).then_inc(bc_w.sem, 16)

            def bc_load(b, g):
                if g == 0:
                    sp.wait_ge(bc_w.sem, bc_w.at(b, 16))
                    sp.sem_inc(tick, 1)
                if outflow_d.at(b, NC * (g - 1), True):
                    sp.wait_ge(outflow_d.sem, outflow_d.at(b, NC * (g - 1)))
                src = bc_dram[b][:, g * SG * T:(g + 1) * SG * T]
                sp.sem_inc(tick, 1)
                sp.dma_start(bc[g % 2][:, :, :, :].rearrange("p a n t -> p a (n t)"),
                             src.unsqueeze(0).broadcast_to([P, 2, SG * T])).then_inc(bc_in[g % 2].sem, 16)

            def q_load(b):
                if v_f.at(b - 1, 1, True):
                    sp.wait_ge(v_f.sem, v_f.at(b - 1, 1))
                if base_d.at(b - 1, 3, True):
                    sp.wait_ge(base_d.sem, base_d.at(b - 1, 3))
                if r0_d.at(b - 1, 1, True):
                    sp.wait_ge(r0_d.sem, r0_d.at(b - 1, 1))
                sp.sem_inc(tick, 1)
                sp.dma_start(ct[:, :, :], a["cT"][:, :, bass.ts(b, T)]).then_inc(q_in.sem, 16)
                sp.dma_start(cr[:, :, :], a["c"][bass.ts(b, T), :].rearrange("(q p) d -> p q d", p=P)).then_inc(q_in.sem, 16)
                sp.dma_start(xr[:, :, :], a["x"][bass.ts(b, T), :].rearrange("(q p) d -> p q d", p=P)).then_inc(q_in.sem, 16)

            def x2_store(b):
                sp.wait_ge(norm_d[3].sem, norm_d[3].at(b, 1))
                sp.sem_inc(tick, 1)
                sp.dma_start(x2_dram[bass.ts(b, T), :].rearrange("(q p) d -> p q d", p=P), x2[:, :, :]).then_inc(x2_st.sem, 16)

            def y_clear(b):
                if isinstance(b, int) and b == 0:
                    sp.wait_ge(k_pool.sem, 16)
                n = (NBLK - SURE * UNROLL) // NB
                sp.dma_start(y_dram[bass.ds((b * n + SURE * UNROLL) * P, n * P), :].rearrange("(j p) d -> p j d", p=P),
                             zeros[:, :].unsqueeze(1).to_broadcast([P, n, D])).then_inc(y_zero.sem, 16)

            def acc_store(b):
                sp.wait_ge(acc_d.sem, acc_d.at(b, 1))
                sp.sem_inc(tick, 1)
                sp.dma_start(acc_dram[bass.ts(b, T), :].rearrange("(q p) d -> p q d", p=P), acc[:, :, :]).then_inc(acc_st.sem, 16)

            x_load(0)
            for dst, src in ((w_out, "w_out"), (w_q, "w_q"), (w_k, "w_k"), (w_v, "w_v"), (w_o, "w_o"), (b_q, "b_q"),
                             (b_k, "b_k"), (w_1, "w_1"), (b_1, "b_1"), (w_2, "w_2"), (w_r, "w_r"),
                             (ws_g, "ws_g"), (ws_d, "ws_d")):
                sp.dma_start(whole(dst), a[src]).then_inc(w_rest.sem, 16)
            for i in range(7):
                sp.dma_start(rows[:, i, :], a[ROWS[i]].unsqueeze(0).broadcast_to([P, D])).then_inc(w_rest.sem, 16)
            sp.dma_start(b_r[:, :], a["b_r"].unsqueeze(0).broadcast_to([P, NE])).then_inc(w_rest.sem, 16)

            def turn(s, p):
                if exists(s + 1) and not (isinstance(s, int) and s == -1):
                    x_load(s + 1)
                if exists(s):
                    bc_load(s, 1)
                if exists(s):
                    bc_load(s, 2)
                    q_load(s)
                if exists(s + 1):
                    bc_out(s + 1)
                if exists(s):
                    bc_load(s, 3)
                if exists(s - 2):
                    x2_store(s - 2)
                if exists(s + 1):
                    bc_load(s + 1, 0)
                if exists(s):
                    y_clear(s)
                if exists(s - 2):
                    acc_store(s - 2)

            all_turns(sp, turn)
            sp.wait_ge(x2_st.sem, x2_st.at(NB - 1, 16))
            sp.wait_ge(acc_st.sem, acc_st.at(NB - 1, 16))
            sp.wait_ge(y_zero.sem, y_zero.at(NB - 1, 16))

        @block.gpsimd
        def _(pool):
            g = nc.gpsimd
            g.memset(ident[:, :], 0.0).then_inc(k_pool.sem, 1)
            g.memset(earlier[:, :], 1.0).then_inc(k_pool.sem, 1)
            g.memset(ones[:, :], 1.0).then_inc(k_pool.sem, 1)
            g.memset(xin[:, :, 0:TAPS - 1], 0.0).then_inc(k_pool.sem, 1)
            for i in range(NBUF):
                g.memset(da[i][:, :, 0:1], 0.0).then_inc(k_pool.sem, 1)
            g.memset(m_sum[:, :], 0.0).then_inc(k_pool.sem, 1)
            g.memset(m_half[:, :], -0.5).then_inc(k_pool.sem, 1)
            g.memset(zi, 0).then_inc(k_pool.sem, 1)
            g.memset(zeros[:, :], 0.0).then_inc(k_pool.sem, 1)
            g.iota(iota_i[:, :], pattern=[[1, NE]], base=0, channel_multiplier=0).then_inc(k_pool.sem, 1)
            g.iota(ids_all[:, :], pattern=[[P, NTILE]], base=0, channel_multiplier=1).then_inc(k_pool.sem, 1)
            pool.wait_ge(k_pool.sem, 14)
            g.affine_select(out=ident[:, :], in_=ident[:, :], compare_op=ALU.not_equal, fill=1.0, base=0,
                            pattern=[[-1, P]], channel_multiplier=1).then_inc(k_pool.sem, 1)
            g.affine_select(out=earlier[:, :], in_=earlier[:, :], compare_op=ALU.is_gt, fill=0.0, base=0,
                            pattern=[[1, P]], channel_multiplier=-1).then_inc(k_pool.sem, 1)
            table = tok_dram.rearrange("(p n) o -> p (n o)", p=P)
            pieces = -(-table.shape[1] // (NC * T))
            for i in range(pieces):
                lo, hi = i * NC * T, min((i + 1) * NC * T, table.shape[1])
                pool.dma_start(table[:, lo:hi], zi[:, 0:hi - lo]).then_inc(zeroed.sem, 16)
            pool.wait_ge(zeroed.sem, 16 * pieces)
            pool.sem_inc(zero_read.sem, 1)

            def inflow(b, p, t):
                gr, c = t // NC, t % NC
                if t == 0:
                    pool.wait_ge(du_d.sem, du_d.at(b, 1))
                if c == 0:
                    pool.wait_ge(bc_in[gr % 2].sem, bc_in[gr % 2].at(b, 16 * (gr // 2 + 1)))
                if sum_d.at(b, t - NBUF + 1, True):
                    pool.wait_ge(sum_d.sem, sum_d.at(b, t - NBUF + 1))
                g.tensor_tensor(hb[t % NBUF][:, :, :], bc[gr % 2][:, 0, :, :],
                                du[p][:, c, :].unsqueeze(1).to_broadcast([P, SG, T]), ALU.mult).then_inc(inflow_d.sem, 1)

            def ln_root(b, i):
                pool.wait_ge(stat2[i].sem, stat2[i].at(b, 1))
                pool.sem_inc(tick, 1)
                g.tensor_scalar(ve[:, i, :], mv[:, i, :, 1], LN_EPS, None, ALU.add).then_inc(root_d[i].sem, 1)
                pool.wait_ge(root_d[i].sem, root_d[i].at(b, 1))
                g.tensor_tensor(rs[:, i, :], ve[:, i, :], m_half[:, :], ALU.pow).then_inc(root_d[i].sem, 1)

            def row(i):
                return rows[:, i, :].unsqueeze(1).to_broadcast([P, QT, D])

            def base_(b, p):
                if isinstance(b, int) and b == 0:
                    pool.wait_ge(w_rest.sem, 16 * 21)
                pool.wait_ge(norm_d[0].sem, norm_d[0].at(b, 1))
                pool.wait_ge(q_in.sem, q_in.at(b, 48))
                if mg_c.at(b - 1, 1, True):
                    pool.wait_ge(mg_c.sem, mg_c.at(b - 1, 1))
                g.tensor_tensor(base[:, :, :], x1[p][:, :, :], cr[:, :, :], ALU.add).then_inc(base_d.sem, 1)
                pool.wait_ge(base_d.sem, base_d.at(b, 1))
                g.tensor_tensor(base[:, :, :], base[:, :, :], cr[:, :, :], ALU.add).then_inc(base_d.sem, 1)
                pool.wait_ge(base_d.sem, base_d.at(b, 2))
                g.tensor_tensor(base[:, :, :], base[:, :, :], row(BO), ALU.add).then_inc(base_d.sem, 1)

            def ln1_affine(b):
                pool.wait_ge(norm_d[1].sem, norm_d[1].at(b, 1))
                g.tensor_tensor(x2a[:, :, :], x2a[:, :, :], row(G1), ALU.mult).then_inc(aff1_d.sem, 1)
                pool.wait_ge(aff1_d.sem, aff1_d.at(b, 1))
                g.tensor_tensor(x2a[:, :, :], x2a[:, :, :], row(B1), ALU.add).then_inc(aff1_d.sem, 1)
                pool.wait_ge(aff1_d.sem, aff1_d.at(b, 2))
                if ff_c.at(b - 1, 1, True):
                    pool.wait_ge(ff_c.sem, ff_c.at(b - 1, 1))
                g.tensor_tensor(base2[:, :, :], x2a[:, :, :], row(B2), ALU.add).then_inc(aff1_d.sem, 1)

            def ln2_affine(b):
                pool.wait_ge(norm_d[2].sem, norm_d[2].at(b, 1))
                g.tensor_tensor(x2[:, :, :], x2[:, :, :], row(G2), ALU.mult).then_inc(aff2_d.sem, 1)
                pool.wait_ge(aff2_d.sem, aff2_d.at(b, 1))
                g.tensor_tensor(x2[:, :, :], x2[:, :, :], row(BB2), ALU.add).then_inc(aff2_d.sem, 1)

            def scatter(b, c):
                if c == 0:
                    pool.wait_ge(addr_d.sem, addr_d.at(b, 1))
                    pool.sem_inc(tick, 1)
                q, k = c // TOPK, c % TOPK
                g.indirect_dma_start(tok_dram, bass.IndirectOffsetOnAxis(ap=ad_i[:, q, k:k + 1], axis=0),
                                     id_st[:, q:q + 1], None).then_inc(scat.sem, 16)

            def settle(b):
                pool.wait_ge(scat.sem, scat.at(b, 16 * QT * TOPK))
                pool.sem_inc(settled.sem, 1)

            pool.sem_inc(settled.sem, 1)

            def turn(s, p):
                for t in range(NTAU):
                    b, bp, tl = tile_at(s, p, t + LEAD)
                    if exists(b):
                        inflow(b, bp, tl)
                    if exists(s - 1):
                        if t == 2:
                            ln_root(s - 1, 0)
                        elif t == 5:
                            base_(s - 1, 1 - p)
                        elif t == 11:
                            ln_root(s - 1, 1)
                        elif t == 13:
                            ln1_affine(s - 1)
                    if exists(s - 2):
                        if t == 8:
                            ln_root(s - 2, 2)
                        elif t == 9:
                            ln2_affine(s - 2)
                        elif t == 10:
                            ln_root(s - 2, 3)
                    if exists(s - 3) and 3 <= t < 11:
                        scatter(s - 3, 2 * (t - 3))
                        scatter(s - 3, 2 * (t - 3) + 1)
                    if exists(s - 3) and t == 14:
                        settle(s - 3)

            all_turns(pool, turn)
            pool.wait_ge(scat.sem, scat.at(NB - 1, 16 * QT * TOPK))

        @block.scalar
        def _(act):
            s = nc.scalar

            def in_proj(b, p, f):
                act.wait_ge(proj_f.sem, proj_f.at(b, f + 1))
                if f < 2:
                    if conv.at(b - 1, NC * TAPS, True):
                        act.wait_ge(conv.sem, conv.at(b - 1, NC * TAPS))
                    if isinstance(b, int) and b == 0:
                        act.wait_ge(k_pool.sem, 16)
                    s.activation(xin[:, 2 * f:2 * f + 2, TAPS - 1:], pair(PB[f]), ACT.Copy).then_inc(proj_c.sem, 1)
                    return
                f -= 2
                if isinstance(b, int) and b == 0 and f == 0:
                    act.wait_ge(w_mamba.sem, 16 * 8)
                    s.activation(a_neg[:, :, :], a_neg[:, :, :], ACT.Exp).then_inc(a_exp.sem, 1)
                    act.wait_ge(zero_read.sem, 1)
                if dl_d.at(b - 1, 1, True):
                    act.wait_ge(dl_d.sem, dl_d.at(b - 1, 1))
                if y_d.at(b - 2, NC, True):
                    act.wait_ge(y_d.sem, y_d.at(b - 2, NC))
                s.activation(th[:, 2 * f:2 * f + 2, :], pair(PB[f]), ACT.Tanh, scale=0.5).then_inc(z_tanh.sem, 1)
                s.activation(sz[p][:, 2 * f:2 * f + 2, :], pair(PB[f]), ACT.Copy, scale=0.5).then_inc(proj_c.sem, 1)

            def u_(b, p):
                act.wait_ge(conv.sem, conv.at(b, NC * TAPS))
                act.wait_ge(gate_d.sem, gate_d.at(b, 1))
                s.activation(th[:, :, :], cv[:, :, :], ACT.Tanh).then_inc(u_tanh.sem, 1)

            def x_proj(b, p):
                act.wait_ge(proj_f.sem, proj_f.at(b, 5))
                if proj_f.at(b - 1, 7, True):
                    act.wait_ge(proj_f.sem, proj_f.at(b - 1, 7))
                if bc_w.at(b - 1, 16, True):
                    act.wait_ge(bc_w.sem, bc_w.at(b - 1, 16))
                s.activation(xdb[:, :], PB[0][0:XP, 0:T], ACT.Copy).then_inc(xdb_c.sem, 1)

            def dt_proj(b, p):
                if du_d.at(b - 2, 1, True):
                    act.wait_ge(du_d.sem, du_d.at(b - 2, 1))
                act.wait_ge(u_d.sem, u_d.at(b, 1))
                for f in range(2):
                    act.wait_ge(proj_f.sem, proj_f.at(b, 6 + f))
                    for i in range(2):
                        c = 2 * f + i
                        ins = s.activation(dl[p][:, c, :], pair(PB[(f + 1) % 2])[:, i, :], ACT.Identity, bias=b_dt[:, c:c + 1])
                    ins.then_inc(proj_c.sem, 1)

            def softplus(b, p):
                act.wait_ge(proj_c.sem, proj_c.at(b, 6))
                s.activation(th[:, :, :], dl[p][:, :, :], ACT.Abs).then_inc(softp.sem, 1)
                act.wait_ge(softp.sem, softp.at(b, 1))
                s.activation(th[:, :, :], th[:, :, :], ACT.Exp, scale=-1.0).then_inc(softp.sem, 1)
                act.wait_ge(softp.sem, softp.at(b, 2))
                s.activation(cv[:, :, :], th[:, :, :], ACT.Ln, bias=1.0).then_inc(softp.sem, 1)

            def decay(b, p, t):
                gr, c = t // NC, t % NC
                if t == 0:
                    act.wait_ge(dl_d.sem, dl_d.at(b, 1))
                    if isinstance(b, int) and b == 0:
                        act.wait_ge(k_scaled.sem, 2)
                if scan_d.at(b, t - NBUF + 1, True):
                    act.wait_ge(scan_d.sem, scan_d.at(b, t - NBUF + 1))
                for n in range(SG):
                    st = gr * SG + n
                    ins = s.activation(da[t % NBUF][:, n, 1:T], dl[p][:, c, 1:T], ACT.Exp, scale=a_neg[:, c, st:st + 1])
                ins.then_inc(decay_d.sem, 1)

            def copy_out(b, filled, bank, dst, done):
                act.wait_ge(filled.sem, filled.at(b, 1))
                s.activation(dst[:, :, :], pair(bank), ACT.Copy).then_inc(done.sem, 1)

            def kv(b):
                act.wait_ge(kT_f.sem, kT_f.at(b, 1))
                for i in range(KD):
                    ins = s.activation(kT[:, i, :], pair(QA[1])[:, i, :], ACT.Identity, bias=b_k[:, i:i + 1])
                ins.then_inc(kT_c.sem, 1)

            def q_(b):
                act.wait_ge(qT_f.sem, qT_f.at(b, 1))
                for i in range(KD):
                    ins = s.activation(qT[:, i, :], pair(QA[0])[:, i, :], ACT.Identity, bias=b_q[:, i:i + 1])
                ins.then_inc(qT_c.sem, 1)

            def softmax(b):
                act.wait_ge(max_d.sem, max_d.at(b, 2))
                for i in range(QT):
                    ins = s.activation(pe_[:, i, :], pair(QA[1])[:, i, :], ACT.Exp, bias=nmx[:, i:i + 1], scale=SCALE,
                                       accum_out=ssum[:, i:i + 1])
                ins.then_inc(p_d.sem, 1)

            def ffn1(b, f):
                act.wait_ge(h_f.sem, h_f.at(b, f + 1))
                for i in range(2):
                    c = 2 * f + i
                    ins = s.activation(hT[:, c, :], pair(QF[f % 2])[:, i, :], ACT.Relu, bias=b_1[:, c:c + 1])
                ins.then_inc(h_c.sem, 1)

            def shared(b):
                act.wait_ge(sh_f.sem, sh_f.at(b, 1))
                s.activation(hth[:, :], QF[1][:, 0:T], ACT.Tanh, scale=0.5).then_inc(sh_c.sem, 1)
                s.activation(hs[:, :], QF[1][:, 0:T], ACT.Copy, scale=0.5).then_inc(sh_c.sem, 1)

            def router(b):
                act.wait_ge(lg_c.sem, lg_c.at(b, 1))
                s.activation(key[:, :, :], key[:, :, :], ACT.Exp, scale=-1.0).then_inc(lg_e.sem, 1)

            def turn(s, p):
                for t in range(NTAU):
                    b, bp, tl = tile_at(s, p, t + LEAD)
                    if exists(b):
                        decay(b, bp, tl)
                    if exists(s + 1):
                        if t < 4:
                            in_proj(s + 1, 1 - p, t)
                        elif t == 5:
                            u_(s + 1, 1 - p)
                        elif t == 6:
                            x_proj(s + 1, 1 - p)
                        elif t == 7:
                            dt_proj(s + 1, 1 - p)
                        elif t == 8:
                            softplus(s + 1, 1 - p)
                    if exists(s - 1):
                        if t == 4:
                            copy_out(s - 1, x1T_f, QA[1], aT, x1T_c)
                        elif t == 5:
                            q_(s - 1)
                        elif t == 7:
                            softmax(s - 1)
                        elif t == 8:
                            copy_out(s - 1, pT_f, QA[0], qT, pT_c)
                        elif t == 9:
                            copy_out(s - 1, aT_f, QA[1], kT, aT_c)
                    if exists(s) and t == 13:
                        kv(s)
                    if exists(s - 2):
                        if t == 0:
                            copy_out(s - 2, x2aT_f, QF[1], fT, x2aT_c)
                        elif 2 <= t < 6:
                            ffn1(s - 2, t - 2)
                        elif t == 12:
                            copy_out(s - 2, x2T_f, QF[1], fT, x2T_c)
                        elif t == 13:
                            router(s - 2)
                            shared(s - 2)

            all_turns(act, turn)

        @block.tensor
        def _(pe):
            mm, tr = nc.tensor.matmul, nc.tensor.transpose

            def in_proj(b, f):
                if isinstance(b, int) and b == 0 and f == 0:
                    pe.wait_ge(w_mamba.sem, 16 * 8)
                if f == 0:
                    pe.wait_ge(xt_in.sem, xt_in.at(b, 16))
                if f < 2:
                    if proj_c.at(b - 1, 6, True):
                        pe.wait_ge(proj_c.sem, proj_c.at(b - 1, 6))
                else:
                    pe.wait_ge(proj_c.sem, proj_c.at(b, f - 1))
                for i in range(2):
                    c = 2 * f + i
                    for k in range(KD):
                        ins = mm(pair(PB[f % 2])[:, i, :], w_in[:, k, c * P:(c + 1) * P], xt[:, k, :],
                                 start=k == 0, stop=k == KD - 1)
                ins.then_inc(proj_f.sem, 1)

            def x_proj(b, p):
                pe.wait_ge(u_d.sem, u_d.at(b, 1))
                pe.wait_ge(proj_c.sem, proj_c.at(b, 3))
                for c in range(NC):
                    ins = mm(PB[0][0:XP, 0:T], w_xp[:, c, :], u[p][:, c, :], start=c == 0, stop=c == NC - 1)
                ins.then_inc(proj_f.sem, 1)

            def dt_proj(b):
                pe.wait_ge(xdb_c.sem, xdb_c.at(b, 1))
                pe.wait_ge(proj_c.sem, proj_c.at(b, 4))
                for f in range(2):
                    for i in range(2):
                        c = 2 * f + i
                        ins = mm(pair(PB[(f + 1) % 2])[:, i, :], w_dt[:, c * P:(c + 1) * P], xdb[0:R, :], start=True, stop=True)
                    ins.then_inc(proj_f.sem, 1)

            def sum_(b, t):
                gr, c = t // NC, t % NC
                if gr == 0 and c % 2 == 0:
                    if y_read.at(b - 1, c + 2, True):
                        pe.wait_ge(y_read.sem, y_read.at(b - 1, c + 2))
                pe.wait_ge(outflow_d.sem, outflow_d.at(b, t + 1))
                for n in range(SG):
                    ins = mm(pair(Y[c // 2])[:, c % 2, :], ident[:, :], hb[t % NBUF][:, n, :],
                             start=gr == 0 and c % 2 == 0 and n == 0, stop=gr == NG - 1 and n == SG - 1,
                             skip_group_check=True)
                ins.then_inc(sum_d.sem, 1)

            def out_proj(b):
                pe.wait_ge(y_d.sem, y_d.at(b, NC))
                pe.wait_ge(v_c.sem, v_c.at(b, 1))
                for q in range(QT):
                    for c in range(NC):
                        ins = mm(pair(QA[0])[:, q, :], yb[:, c, q * P:(q + 1) * P], w_out[:, c, :], start=c == 0, stop=c == NC - 1)
                ins.then_inc(out_f.sem, 1)

            def turned(src, bank, filled):
                for q in range(QT):
                    for k in range(KD):
                        ins = tr(pair(bank)[:, k, q * P:(q + 1) * P], src[:, q, k * P:(k + 1) * P], ident[:, :])
                ins.then_inc(filled.sem, 1)

            def x1T(b, p):
                pe.wait_ge(norm_d[0].sem, norm_d[0].at(b, 1))
                pe.wait_ge(kT_c.sem, kT_c.at(b, 1))
                turned(x1[p], QA[1], x1T_f)

            def q_(b):
                pe.wait_ge(x1T_c.sem, x1T_c.at(b, 1))
                pe.wait_ge(r0_d.sem, r0_d.at(b, 1))
                for i in range(KD):
                    for k in range(KD):
                        ins = mm(pair(QA[0])[:, i, :], w_q[:, k, i * P:(i + 1) * P], aT[:, k, :], start=k == 0, stop=k == KD - 1)
                ins.then_inc(qT_f.sem, 1)

            def scores(b):
                pe.wait_ge(qT_c.sem, qT_c.at(b, 1))
                for q in range(QT):
                    for k in range(KD):
                        ins = mm(pair(QA[1])[:, q, :], qT[:, k, q * P:(q + 1) * P], kT[:, k, :], start=k == 0, stop=k == KD - 1)
                ins.then_inc(sco_f.sem, 1)

            def pT(b):
                pe.wait_ge(p_d.sem, p_d.at(b, 1))
                turned(pe_, QA[0], pT_f)

            def pv(b):
                pe.wait_ge(pT_c.sem, pT_c.at(b, 1))
                for i in range(KD):
                    for k in range(QT):
                        ins = mm(pair(QA[1])[:, i, :], vv[:, k, i * P:(i + 1) * P], qT[:, k, :], start=k == 0, stop=k == QT - 1)
                ins.then_inc(aT_f.sem, 1)

            def merge(b):
                pe.wait_ge(aT_c.sem, aT_c.at(b, 1))
                for q in range(QT):
                    for k in range(KD):
                        ins = mm(pair(QA[0])[:, q, :], kT[:, k, q * P:(q + 1) * P], w_o[:, k, :], start=k == 0, stop=k == KD - 1)
                ins.then_inc(mg_f.sem, 1)

            def kv(b):
                if isinstance(b, int) and b == 0:
                    pe.wait_ge(w_rest.sem, 16 * 21)
                pe.wait_ge(q_in.sem, q_in.at(b, 48))
                if aT_c.at(b - 1, 1, True):
                    pe.wait_ge(aT_c.sem, aT_c.at(b - 1, 1))
                for i in range(KD):
                    for k in range(KD):
                        ins = mm(pair(QA[1])[:, i, :], w_k[:, k, i * P:(i + 1) * P], ct[:, k, :], start=k == 0, stop=k == KD - 1)
                ins.then_inc(kT_f.sem, 1)
                if mg_c.at(b - 1, 1, True):
                    pe.wait_ge(mg_c.sem, mg_c.at(b - 1, 1))
                for q in range(QT):
                    for k in range(KD):
                        ins = mm(pair(QA[0])[:, q, :], ct[:, k, q * P:(q + 1) * P], w_v[:, k, :], start=k == 0, stop=k == KD - 1)
                ins.then_inc(v_f.sem, 1)

            def x2aT(b):
                pe.wait_ge(aff1_d.sem, aff1_d.at(b, 2))
                if acc_d.at(b - 1, 1, True):
                    pe.wait_ge(acc_d.sem, acc_d.at(b - 1, 1))
                turned(x2a, QF[1], x2aT_f)

            def ffn1(b, f):
                if f == 0:
                    pe.wait_ge(x2aT_c.sem, x2aT_c.at(b, 1))
                    if cum_c.at(b - 1, 1, True):
                        pe.wait_ge(cum_c.sem, cum_c.at(b - 1, 1))
                if f >= 2:
                    pe.wait_ge(h_c.sem, h_c.at(b, f - 1))
                for i in range(2):
                    c = 2 * f + i
                    for k in range(KD):
                        ins = mm(pair(QF[f % 2])[:, i, :], w_1[:, k, c * P:(c + 1) * P], fT[:, k, :], start=k == 0, stop=k == KD - 1)
                ins.then_inc(h_f.sem, 1)

            def ffn2(b, q):
                pe.wait_ge(h_c.sem, h_c.at(b, 4))
                for k in range(KF):
                    ins = mm(pair(QF[0])[:, q, :], hT[:, k, q * P:(q + 1) * P], w_2[:, k, :], start=k == 0, stop=k == KF - 1)
                if q == QT - 1:
                    ins.then_inc(ff_f.sem, 1)

            def x2T(b):
                pe.wait_ge(norm_d[3].sem, norm_d[3].at(b, 1))
                turned(x2, QF[1], x2T_f)

            def router(b):
                pe.wait_ge(x2T_c.sem, x2T_c.at(b, 1))
                pe.wait_ge(ff_c.sem, ff_c.at(b, 1))
                for q in range(QT):
                    for k in range(KD):
                        ins = mm(QF[0][:, q * NE:(q + 1) * NE], fT[:, k, q * P:(q + 1) * P], w_r[:, k, :], start=k == 0, stop=k == KD - 1)
                ins.then_inc(lg_f.sem, 1)

            def shared(b):
                for k in range(KD):
                    ins = mm(QF[1][:, 0:T], ws_g[:, k, :], fT[:, k, :], start=k == 0, stop=k == KD - 1)
                ins.then_inc(sh_f.sem, 1)

            def shared_out(b):
                pe.wait_ge(hs_d.sem, hs_d.at(b, 1))
                for q in range(QT):
                    ins = mm(pair(QF[1])[:, q, :], hs[:, q * P:(q + 1) * P], ws_d[:, :], start=True, stop=True)
                ins.then_inc(so_f.sem, 1)

            def rank(b):
                pe.wait_ge(mask_d.sem, mask_d.at(b, 1))
                pe.wait_ge(lg_c.sem, lg_c.at(b, 1))
                if msum_d.at(b - 1, 1, True):
                    pe.wait_ge(msum_d.sem, msum_d.at(b - 1, 1))
                mm(QF[0][:, 0:NE], earlier[:, :], msk_b[:, 0, :], start=True, stop=False)
                mm(QF[0][:, 0:NE], ones[:, :], m_sum[:, :], start=False, stop=True)
                mm(QF[0][:, NE:2 * NE], earlier[:, :], msk_b[:, 1, :], start=True, stop=False)
                mm(QF[0][:, NE:2 * NE], ones[:, :], msk_b[:, 0, :], start=False, stop=False)
                mm(QF[0][:, NE:2 * NE], ones[:, :], m_sum[:, :], start=False, stop=True).then_inc(cum_f.sem, 1)

            def turn(s, p):
                for t in range(NTAU):
                    b, bp, tl = tile_at(s, p, t - LEAD)
                    if exists(b):
                        sum_(b, tl)
                    if exists(s + 1):
                        if t < 4:
                            in_proj(s + 1, t)
                        elif t == 6:
                            x_proj(s + 1, 1 - p)
                        elif t == 7:
                            dt_proj(s + 1)
                    if exists(s - 1):
                        if t == 1:
                            out_proj(s - 1)
                        elif t == 4:
                            x1T(s - 1, 1 - p)
                        elif t == 5:
                            q_(s - 1)
                        elif t == 6:
                            scores(s - 1)
                        elif t == 8:
                            pT(s - 1)
                        elif t == 9:
                            pv(s - 1)
                        elif t == 10:
                            merge(s - 1)
                    if exists(s) and t == 13:
                        kv(s)
                    if exists(s - 2):
                        if t == 0:
                            x2aT(s - 2)
                        elif 2 <= t < 6:
                            ffn1(s - 2, t - 2)
                        elif 6 <= t < 8:
                            ffn2(s - 2, t - 6)
                        elif t == 12:
                            x2T(s - 2)
                        elif t == 13:
                            router(s - 2)
                            shared(s - 2)
                        elif t == 14:
                            shared_out(s - 2)
                        elif t == 15:
                            rank(s - 2)

            all_turns(pe, turn)

        @block.vector
        def _(dve):
            v = nc.vector
            dve.wait_ge(w_mamba.sem, 16 * 8)
            dve.wait_ge(k_pool.sem, 16)
            v.tensor_scalar(w_conv[:, :, :], w_conv[:, :, :], 0.5, None, ALU.mult).then_inc(k_conv.sem, 1)
            v.tensor_scalar(b_conv[:, :], b_conv[:, :], 0.5, None, ALU.mult).then_inc(k_conv.sem, 1)
            v.tensor_copy(iota_e[:, :], iota_i[:, :]).then_inc(k_conv.sem, 1)
            dve.wait_ge(k_conv.sem, 3)

            def conv_(b, k):
                if k == 0:
                    dve.wait_ge(proj_c.sem, proj_c.at(b, 2))
                for c in range(NC):
                    if k == 0:
                        ins = v.tensor_scalar(cv[:, c, :], xin[:, c, 0:T], w_conv[:, c, 0:1], b_conv[:, c:c + 1], ALU.mult, ALU.add)
                    else:
                        dve.wait_ge(conv.sem, conv.at(b, (k - 1) * NC + c + 1))
                        ins = v.scalar_tensor_tensor(cv[:, c, :], xin[:, c, k:k + T], w_conv[:, c, k:k + 1], cv[:, c, :], ALU.mult, ALU.add)
                    ins.then_inc(conv.sem, 1)

            def gate_z(b, p):
                dve.wait_ge(z_tanh.sem, z_tanh.at(b, 2))
                dve.wait_ge(proj_c.sem, proj_c.at(b, 4))
                v.scalar_tensor_tensor(sz[p][:, :, :], th[:, :, :], 1.0, sz[p][:, :, :], ALU.add, ALU.mult).then_inc(gate_d.sem, 1)

            def u_(b, p):
                dve.wait_ge(u_tanh.sem, u_tanh.at(b, 1))
                v.scalar_tensor_tensor(u[p][:, :, :], th[:, :, :], 1.0, cv[:, :, :], ALU.add, ALU.mult).then_inc(u_d.sem, 1)

            def softplus(b, p):
                dve.wait_ge(softp.sem, softp.at(b, 3))
                v.tensor_scalar(du[p][:, :, :], th[:, :, :], 1.0, -1.0, ALU.add, ALU.add).then_inc(lost.sem, 1)
                v.scalar_tensor_tensor(dl[p][:, :, :], dl[p][:, :, :], 0.0, cv[:, :, :], ALU.max, ALU.add).then_inc(lost.sem, 1)

            def delta(b, p):
                dve.wait_ge(lost.sem, lost.at(b, 1))
                v.tensor_tensor(th[:, :, :], th[:, :, :], du[p][:, :, :], ALU.subtract).then_inc(lost.sem, 1)
                dve.wait_ge(lost.sem, lost.at(b, 3))
                v.tensor_tensor(dl[p][:, :, :], dl[p][:, :, :], th[:, :, :], ALU.add).then_inc(dl_d.sem, 1)

            def delta_u(b, p):
                dve.wait_ge(dl_d.sem, dl_d.at(b, 1))
                v.tensor_tensor(du[p][:, :, :], dl[p][:, :, :], u[p][:, :, :], ALU.mult).then_inc(du_d.sem, 1)
                if isinstance(b, int) and b == 0:
                    dve.wait_ge(a_exp.sem, 1)
                    v.tensor_scalar(a_neg[:, :, :], a_neg[:, :, :], -1.0, None, ALU.mult).then_inc(k_scaled.sem, 2)

            def scan(b, t):
                dve.wait_ge(decay_d.sem, decay_d.at(b, t + 1))
                dve.wait_ge(inflow_d.sem, inflow_d.at(b, t + 1))
                flat = hb[t % NBUF][:, :, :].rearrange("p n t -> p (n t)")
                v.tensor_tensor_scan(flat, da[t % NBUF][:, :, :].rearrange("p n t -> p (n t)"), flat, 0.0,
                                     ALU.mult, ALU.add).then_inc(scan_d.sem, 1)

            def outflow(b, t):
                dve.wait_ge(scan_d.sem, scan_d.at(b, t + 1))
                v.tensor_tensor(hb[t % NBUF][:, :, :], hb[t % NBUF][:, :, :], bc[(t // NC) % 2][:, 1, :, :],
                                ALU.mult).then_inc(outflow_d.sem, 1)

            def y(b, p, c):
                dve.wait_ge(sum_d.sem, sum_d.at(b, NTAU - NC + c // 2 * 2 + 2))
                v.scalar_tensor_tensor(yb[:, c, :], u[p][:, c, :], d_par[:, c:c + 1], pair(Y[c // 2])[:, c % 2, :],
                                       ALU.mult, ALU.add).then_inc(y_read.sem, 1)
                dve.wait_ge(y_read.sem, y_read.at(b, c + 1))
                v.tensor_tensor(yb[:, c, :], yb[:, c, :], sz[p][:, c, :], ALU.mult).then_inc(y_d.sem, 1)

            def kv(b):
                dve.wait_ge(v_f.sem, v_f.at(b, 1))
                v.tensor_tensor(vv[:, :, :], pair(QA[0]), rows[:, BV, :].unsqueeze(1).to_broadcast([P, QT, D]), ALU.add).then_inc(v_c.sem, 1)

            def moments(i, src, b):
                for q in range(QT):
                    v.bn_stats(stats[:, i, q, :], src[:, q, :]).then_inc(stat1[i].sem, 1)
                dve.wait_ge(stat1[i].sem, stat1[i].at(b, QT))
                dve.sem_inc(tick, 1)
                for q in range(QT):
                    ins = v.bn_aggr(mv[:, i, q, :], stats[:, i, q, :])
                ins.then_inc(stat2[i].sem, 1)

            def normalise(b, i, src):
                dve.wait_ge(root_d[i].sem, root_d[i].at(b, 2))
                for q in range(QT):
                    ins = v.tensor_scalar(src[:, q, :], src[:, q, :], mv[:, i, q, 0:1], rs[:, i, q:q + 1], ALU.subtract, ALU.mult)
                ins.then_inc(norm_d[i].sem, 1)

            def ln0(b, p):
                dve.wait_ge(out_f.sem, out_f.at(b, 1))
                dve.wait_ge(q_in.sem, q_in.at(b, 48))
                v.tensor_tensor(x1[p][:, :, :], pair(QA[0]), xr[:, :, :], ALU.add).then_inc(r0_d.sem, 1)
                dve.wait_ge(r0_d.sem, r0_d.at(b, 1))
                moments(0, x1[p], b)

            def softmax(b):
                dve.wait_ge(sco_f.sem, sco_f.at(b, 1))
                v.tensor_reduce(nmx[:, :], pair(QA[1]), AX.X, ALU.max).then_inc(max_d.sem, 1)
                dve.wait_ge(max_d.sem, max_d.at(b, 1))
                v.tensor_scalar(nmx[:, :], nmx[:, :], -SCALE, None, ALU.mult).then_inc(max_d.sem, 1)

            def ln1(b):
                dve.wait_ge(p_d.sem, p_d.at(b, 1))
                v.reciprocal(rsum[:, :], ssum[:, :]).then_inc(rsum_d.sem, 1)
                dve.wait_ge(rsum_d.sem, rsum_d.at(b, 1))
                dve.wait_ge(mg_f.sem, mg_f.at(b, 1))
                dve.wait_ge(base_d.sem, base_d.at(b, 3))
                if x2aT_f.at(b - 1, 1, True):
                    dve.wait_ge(x2aT_f.sem, x2aT_f.at(b - 1, 1))
                for q in range(QT):
                    ins = v.scalar_tensor_tensor(x2a[:, q, :], pair(QA[0])[:, q, :], rsum[:, q:q + 1], base[:, q, :], ALU.mult, ALU.add)
                ins.then_inc(mg_c.sem, 1)
                dve.wait_ge(mg_c.sem, mg_c.at(b, 1))
                moments(1, x2a, b)

            def ln2(b):
                dve.wait_ge(ff_f.sem, ff_f.at(b, 1))
                dve.wait_ge(aff1_d.sem, aff1_d.at(b, 3))
                if x2_st.at(b - 1, 16, True):
                    dve.wait_ge(x2_st.sem, x2_st.at(b - 1, 16))
                v.tensor_tensor(x2[:, :, :], pair(QF[0]), base2[:, :, :], ALU.add).then_inc(ff_c.sem, 1)
                dve.wait_ge(ff_c.sem, ff_c.at(b, 1))
                moments(2, x2, b)

            def ln3(b, p):
                dve.wait_ge(aff2_d.sem, aff2_d.at(b, 2))
                v.tensor_tensor(x2[:, :, :], x2[:, :, :], x1[p][:, :, :], ALU.add).then_inc(res_d.sem, 1)
                dve.wait_ge(res_d.sem, res_d.at(b, 1))
                moments(3, x2, b)

            def router(b):
                dve.wait_ge(lg_f.sem, lg_f.at(b, 1))
                v.tensor_tensor(key[:, :, :], QF[0][:, 0:QT * NE].rearrange("p (q e) -> p q e", q=QT),
                                b_r[:, :].unsqueeze(1).to_broadcast([P, QT, NE]), ALU.add).then_inc(lg_c.sem, 1)

            def shared(b):
                dve.wait_ge(sh_c.sem, sh_c.at(b, 2))
                v.scalar_tensor_tensor(hs[:, :], hth[:, :], 1.0, hs[:, :], ALU.add, ALU.mult).then_inc(hs_d.sem, 1)

            def shared_out(b):
                dve.wait_ge(so_f.sem, so_f.at(b, 1))
                if acc_st.at(b - 1, 16, True):
                    dve.wait_ge(acc_st.sem, acc_st.at(b - 1, 16))
                dve.wait_ge(norm_d[3].sem, norm_d[3].at(b, 1))
                v.tensor_tensor(acc[:, :, :], pair(QF[1]), x2[:, :, :], ALU.add).then_inc(acc_d.sem, 1)

            def choose(b):
                dve.wait_ge(lg_e.sem, lg_e.at(b, 1))
                v.tensor_scalar(key[:, :, :], key[:, :, :], -1.0, -1.0, ALU.mult, ALU.add).then_inc(key_d.sem, 1)
                dve.wait_ge(key_d.sem, key_d.at(b, 1))
                dve.sem_inc(tick, 1)
                for q in range(QT):
                    v.max(top[:, q, :], key[:, q, :]).then_inc(pick.sem, 1)
                for q in range(QT):
                    dve.wait_ge(pick.sem, pick.at(b, q + 1))
                    dve.sem_inc(tick, 1)
                    v.match_replace(rep[:, q, :], top[:, q, :], key[:, q, :], 1.0).then_inc(pick.sem, 1)
                dve.wait_ge(pick.sem, pick.at(b, 4))
                v.tensor_scalar(msk_b[:, :, :], rep[:, :, :], 0.0, None, ALU.is_gt).then_inc(mask_d.sem, 1)

            def weigh(b):
                for q in range(QT):
                    v.max_index(ti[:, q, :], top[:, q, :], key[:, q, :]).then_inc(pick.sem, 1)
                dve.wait_ge(pick.sem, pick.at(b, 6))
                v.tensor_copy(e_st[:, :, :], ti[:, :, :]).then_inc(pick.sem, 1)
                v.reciprocal(pr[:, :, :], top[:, :, :]).then_inc(pick.sem, 1)
                dve.wait_ge(pick.sem, pick.at(b, 8))
                v.tensor_reduce(psm[:, :], pr[:, :, :], AX.X, ALU.add).then_inc(pick.sem, 1)
                dve.wait_ge(pick.sem, pick.at(b, 9))
                v.tensor_scalar(psm[:, :], psm[:, :], -1.0, 1e-9, ALU.mult, ALU.add).then_inc(pick.sem, 1)
                dve.wait_ge(pick.sem, pick.at(b, 10))
                v.reciprocal(psm[:, :], psm[:, :]).then_inc(pick.sem, 1)
                v.tensor_scalar(pr[:, :, :], pr[:, :, :], -2.5, None, ALU.mult).then_inc(pick.sem, 1)
                dve.wait_ge(pick.sem, pick.at(b, 12))
                w8 = QT * TOPK
                v.tensor_tensor(gate[:, bass.ds(b * w8, w8)].rearrange("p (q k) -> p q k", q=QT), pr[:, :, :],
                                psm[:, :].unsqueeze(2).to_broadcast([P, QT, TOPK]), ALU.mult).then_inc(pick.sem, 1)
                v.tensor_copy(sel_e[:, bass.ds(b * w8, w8)], e_st[:, :, :].rearrange("p q k -> p (q k)")).then_inc(pick.sem, 1)

            def rank(b, q):
                if q == 0:
                    dve.wait_ge(cum_f.sem, cum_f.at(b, 1))
                for k in range(TOPK):
                    c = q * TOPK + k
                    if c >= 2:
                        dve.wait_ge(rank_s.sem, rank_s.at(b, c - 1))
                    v.scalar_tensor_tensor(junk[k % 2][:, :], iota_e[:, :], e_st[:, q, k:k + 1], QF[0][:, q * NE:(q + 1) * NE],
                                           ALU.is_equal, ALU.mult, accum_out=r_st[:, q, k:k + 1]).then_inc(rank_s.sem, 1)

            def address(b):
                dve.wait_ge(rank_s.sem, rank_s.at(b, QT * TOPK))
                dve.sem_inc(cum_c.sem, 1)
                v.tensor_tensor(m_sum[:, :], m_sum[:, :], msk_b[:, 0, :], ALU.add).then_inc(addr.sem, 1)
                v.scalar_tensor_tensor(ad_f[:, :, :], e_st[:, :, :], float(CAP), r_st[:, :, :], ALU.mult, ALU.add).then_inc(addr.sem, 1)
                dve.wait_ge(addr.sem, addr.at(b, 2))
                v.tensor_tensor(m_sum[:, :], m_sum[:, :], msk_b[:, 1, :], ALU.add).then_inc(msum_d.sem, 1)
                w8 = QT * TOPK
                v.tensor_copy(sel_r[:, bass.ds(b * w8, w8)], r_st[:, :, :].rearrange("p q k -> p (q k)")).then_inc(selr_d.sem, 1)
                dve.wait_ge(settled.sem, settled.at(b, 1))
                v.tensor_copy(id_st[:, :], ids_all[:, bass.ds(b * QT, QT)])
                v.tensor_copy(ad_i[:, :, :], ad_f[:, :, :]).then_inc(addr_d.sem, 1)

            def turn(s, p):
                for t in range(NTAU):
                    if exists(s):
                        scan(s, t)
                    b, bp, tl = tile_at(s, p, t - 1)
                    if exists(b):
                        outflow(b, tl)
                    if exists(s) and t == NTAU - 1:
                        y(s, p, 0)
                        y(s, p, 1)
                    if exists(s - 1) and t == 1:
                        y(s - 1, 1 - p, 2)
                        y(s - 1, 1 - p, 3)
                    if exists(s + 1):
                        if t == 2:
                            conv_(s + 1, 0)
                            conv_(s + 1, 1)
                        elif t == 3:
                            conv_(s + 1, 2)
                        elif t == 4:
                            conv_(s + 1, 3)
                        elif t == 5:
                            gate_z(s + 1, 1 - p)
                            u_(s + 1, 1 - p)
                        elif t == 9:
                            softplus(s + 1, 1 - p)
                        elif t == 10:
                            delta(s + 1, 1 - p)
                        elif t == 11:
                            delta_u(s + 1, 1 - p)
                    if exists(s - 1):
                        if t == 2:
                            ln0(s - 1, 1 - p)
                        elif t == 3:
                            normalise(s - 1, 0, x1[1 - p])
                        elif t == 6:
                            softmax(s - 1)
                        elif t == 11:
                            ln1(s - 1)
                        elif t == 12:
                            normalise(s - 1, 1, x2a)
                    if exists(s) and t == 13:
                        kv(s)
                    if exists(s - 2):
                        if t == 8:
                            ln2(s - 2)
                        elif t == 9:
                            normalise(s - 2, 2, x2)
                        elif t == 10:
                            ln3(s - 2, p)
                        elif t == 11:
                            normalise(s - 2, 3, x2)
                        elif t == 13:
                            router(s - 2)
                            shared(s - 2)
                        elif t == 14:
                            shared_out(s - 2)
                            choose(s - 2)
                        elif t == 15:
                            weigh(s - 2)
                    if exists(s - 3):
                        if t < 2:
                            rank(s - 3, t)
                        if t == 1:
                            address(s - 3)

            all_turns(dve, turn)
            dve.wait_ge(selr_d.sem, selr_d.at(NB - 1, 1))

        front.close()

        cnt_f, cnt_c = sig("cnt_f"), sig("cnt_c")
        tab_s = sig("tab_s")
        tab_w, tab_in = sig("tab_w"), sig("tab_in")
        idr_in, idr_c, idT_f, ids_c = sig("idr_in"), sig("idr_c"), sig("idT_f"), sig("ids_c")
        idb_d = sig("idb_d", UNROLL)
        wt_in = [sig(f"wt_in{i}", 16) for i in range(UNROLL)]
        xg_in = [sig(f"xg_in{i}", 16) for i in range(UNROLL)]
        y_st = [sig(f"y_st{i}", 16) for i in range(UNROLL // YG)]
        xgT_f, xgT_c = sig("xgT_f", UNROLL), sig("xgT_c", UNROLL)
        up_f, up_c = sig("up_f", UNROLL), sig("up_c", UNROLL)
        dn_f, dn_c = sig("dn_f", UNROLL), sig("dn_c", UNROLL)
        slot_d = sig("slot_d", UNROLL)
        slot_i = sig("slot_i")

        slot = sb("slot", [P, NSEL])
        slot_n = sb("slot_n", [P, NSEL], I32)
        mid = ExitStack()

        def sm(name, shape, dt=FP32):
            return mid.enter_context(nc.sbuf_tensor(name, shape, dt))

        cnt = sm("cnt", [P, NE])
        cnt_i = sm("cnt_i", [P, NE], I32)
        nblk = sm("nblk", [P, NE])
        incl = sm("incl", [P, NE])
        first = sm("first", [P, NE])
        one_f = sm("one_f", [P, NE])
        jn_i = sm("jn_i", [BJ, 3], I32)
        jn = sm("jn", [BJ, 3])
        blk_e = sm("blk_e", [BJ, 3])
        blk_b = sm("blk_b", [BJ, 3])
        blk_o = sm("blk_o", [BJ, 3])
        blk_i = sm("blk_i", [BJ, 3], I32)
        blk_r = sm("blk_r", [BJ, 3], I32)
        last_turn = sm("last_turn", [1, 1], I32)
        idr = sm("idr", [BJ, 3, P], I32)
        idr_f = sm("idr_f", [BJ, 3, P])
        ids = sm("ids", [P, NBLK + UNROLL], I32)
        junk2 = sm("junk2", [P, 3, NE])
        junk3 = sm("junk3", [P, 2, NE])
        tab = sm("tab", [1, NBLK], I32)
        wt = [sm(f"wt{i}", [P, KD * INTER + D]) for i in range(UNROLL)]
        idb = [sm(f"idb{i}", [P, 1], I32) for i in range(UNROLL)]
        xg = [sm(f"xg{i}", [P, D]) for i in range(UNROLL)]
        xgT = [sm(f"xgT{i}", [P, KD, P]) for i in range(2)]
        h1 = [sm(f"h1{i}", [P, P]) for i in range(2)]
        ys = [sm(f"ys{i}", [P, YG, D]) for i in range(UNROLL // YG)]
        XT = [PB[0], PB[1]]
        UP = [Y[0], Y[1]]
        DN = [QA[0], QA[1]]
        CN = QF[0]
        TAB_DONE = 15

        def last_filled(eng):
            eng.wait_ge(tab_s.sem, TAB_DONE)
            return eng.value_load(last_turn[0:1, 0:1], min_val=SURE - 1, max_val=TURNS - 1)

        def further_turns(eng, last, body):
            with eng.Fori(1, SURE) as i:
                body(i, True)
            with eng.Fori(SURE, TURNS) as i:
                with eng.If(last >= i):
                    body(i, False)

        def back(i, s, lag):
            return (i, s - lag) if s >= lag else (i - 1, s - lag + UNROLL)

        block = mid.enter_context(nc.Block())

        @block.sync
        def _(sp):
            last = last_filled(sp)
            sp.dma_start(blk_dram.rearrange("(p c) -> p c", p=BJ), blk_i[:, :]).then_inc(tab_w.sem, 16)
            sp.wait_ge(tab_w.sem, 16)
            sp.dma_start(tab[0:1, :], blk_dram.unsqueeze(0)).then_inc(tab_in.sem, 16)
            sp.wait_ge(tab_in.sem, 16)

            def weights(i, s_):
                e = sp.value_load(tab[0:1, bass.ds(i * UNROLL + s_, 1)], min_val=0, max_val=NE - 1)
                if dn_f.at(i - 1, s_ + 1, True):
                    sp.wait_ge(dn_f.sem, dn_f.at(i - 1, s_ + 1))
                sp.sem_inc(tick, 1)
                sp.dma_start(wt[s_][:, :], a["w_moe"][bass.ds(e * P, P), :]).then_inc(wt_in[s_].sem, 16)

            def store(i, h):
                sp.wait_ge(dn_c.sem, dn_c.at(i, (h + 1) * YG))
                sp.sem_inc(tick, 1)
                rows_ = y_dram[bass.ds((i * UNROLL + h * YG) * P, YG * P), :]
                sp.dma_start(rows_.rearrange("(j p) d -> p j d", p=P), ys[h][:, :, :]).then_inc(y_st[h].sem, 16)

            def body(i, sure):
                for s_ in range(UNROLL):
                    weights(i, s_)
                    if s_ % YG == YG - 1:
                        store(i - 1, s_ // YG)

            for s_ in range(UNROLL):
                weights(0, s_)
            further_turns(sp, last, body)
            for h in range(UNROLL // YG):
                store(last, h)
            for h in range(UNROLL // YG):
                sp.wait_ge(y_st[h].sem, y_st[h].at(last, 16))
                sp.sem_inc(tick, 1)

        @block.gpsimd
        def _(pool):
            g = nc.gpsimd
            g.iota(jn_i[:, :], pattern=[[1, 3]], base=0, channel_multiplier=3).then_inc(cnt_c.sem, 1)
            last = last_filled(pool)
            by_block = tok_dram.rearrange("(r p) o -> r (p o)", p=P)
            for c in range(3):
                g.indirect_dma_start(idr[:, c, :], None, by_block,
                                     bass.IndirectOffsetOnAxis(ap=blk_r[:, c:c + 1], axis=0)).then_inc(idr_in.sem, 16)

            def gather(i, s_):
                pool.wait_ge(idb_d.sem, idb_d.at(i, s_ + 1))
                if xgT_f.at(i - 1, s_ + 1, True):
                    pool.wait_ge(xgT_f.sem, xgT_f.at(i - 1, s_ + 1))
                pool.sem_inc(tick, 1)
                g.indirect_dma_start(xg[s_][:, :], None, x2_dram,
                                     bass.IndirectOffsetOnAxis(ap=idb[s_][:, 0:1], axis=0)).then_inc(xg_in[s_].sem, 16)

            def body(i, sure):
                for s_ in range(UNROLL):
                    gather(i, s_)

            body(0, True)
            further_turns(pool, last, body)

        @block.tensor
        def _(pe):
            mm = nc.tensor.matmul
            mm(CN[:, 0:NE], ones[:, :], m_sum[:, :], start=True, stop=True).then_inc(cnt_f.sem, 1)
            last = last_filled(pe)
            pe.wait_ge(idr_c.sem, 1)
            for c in range(3):
                ins = nc.tensor.transpose(QF[1][:, c * BJ:(c + 1) * BJ], idr_f[:, c, :], ident[0:BJ, 0:BJ])
            ins.then_inc(idT_f.sem, 1)

            def turned(i, s_):
                pe.wait_ge(xg_in[s_].sem, xg_in[s_].at(i, 16))
                if xgT_c.at(i, s_ - 1, True):
                    pe.wait_ge(xgT_c.sem, xgT_c.at(i, s_ - 1))
                for k in range(KD):
                    ins = nc.tensor.transpose(XT[s_ % 2][:, k * P:(k + 1) * P], xg[s_][:, k * P:(k + 1) * P], ident[:, :])
                ins.then_inc(xgT_f.sem, 1)

            def up(i, s_):
                pe.wait_ge(xgT_c.sem, xgT_c.at(i, s_ + 1))
                pe.wait_ge(wt_in[s_].sem, wt_in[s_].at(i, 16))
                if up_c.at(i, s_ - 1, True):
                    pe.wait_ge(up_c.sem, up_c.at(i, s_ - 1))
                for k in range(KD):
                    ins = mm(UP[s_ % 2][:, 0:P], wt[s_][:, k * INTER:(k + 1) * INTER], xgT[s_ % 2][:, k, :], start=k == 0, stop=k == KD - 1)
                ins.then_inc(up_f.sem, 1)

            def down(i, s_):
                pe.wait_ge(up_c.sem, up_c.at(i, s_ + 1))
                if dn_c.at(i, s_ - 1, True):
                    pe.wait_ge(dn_c.sem, dn_c.at(i, s_ - 1))
                mm(DN[s_ % 2][:, 0:D], h1[s_ % 2][:, :], wt[s_][:, KD * INTER:], start=True, stop=True).then_inc(dn_f.sem, 1)

            def body(i, sure):
                first_turn = isinstance(i, int)
                for s_ in range(UNROLL):
                    turned(i, s_)
                    if not (first_turn and s_ < 2):
                        down(*back(i, s_, 2))
                    if not (first_turn and s_ < 1):
                        up(*back(i, s_, 1))

            body(0, True)
            further_turns(pe, last, body)
            down(last, UNROLL - 2)
            up(last, UNROLL - 1)
            down(last, UNROLL - 1)

        @block.scalar
        def _(act):
            s = nc.scalar
            last = last_filled(act)

            def silu(i, s_):
                act.wait_ge(up_f.sem, up_f.at(i, s_ + 1))
                if dn_f.at(i, s_ - 1, True):
                    act.wait_ge(dn_f.sem, dn_f.at(i, s_ - 1))
                s.activation(h1[s_ % 2][:, :], UP[s_ % 2][:, 0:P], ACT.Silu).then_inc(up_c.sem, 1)

            def copy_y(i, s_):
                h = s_ // YG
                act.wait_ge(dn_f.sem, dn_f.at(i, s_ + 1))
                if s_ % YG == 0:
                    if y_st[h].at(i - 1, 16, True):
                        act.wait_ge(y_st[h].sem, y_st[h].at(i - 1, 16))
                s.activation(ys[h][:, s_ % YG, :], DN[s_ % 2][:, 0:D], ACT.Copy).then_inc(dn_c.sem, 1)

            def body(i, sure):
                first_turn = isinstance(i, int)
                for s_ in range(UNROLL):
                    if not (first_turn and s_ < 2):
                        copy_y(*back(i, s_, 2))
                    if not (first_turn and s_ < 1):
                        silu(*back(i, s_, 1))

            body(0, True)
            further_turns(act, last, body)
            copy_y(last, UNROLL - 2)
            silu(last, UNROLL - 1)
            copy_y(last, UNROLL - 1)

        @block.vector
        def _(dve):
            v = nc.vector
            steps = [0]

            def link(ins):
                steps[0] += 1
                ins.then_inc(tab_s.sem, 1)
                dve.wait_ge(tab_s.sem, steps[0])

            dve.wait_ge(cnt_f.sem, 1)
            dve.wait_ge(cnt_c.sem, 1)
            link(v.tensor_scalar(cnt_i[:, :], CN[:, 0:NE], float(P - 1), None, ALU.add))
            link(v.tensor_scalar(cnt_i[:, :], cnt_i[:, :], 7, None, ALU.arith_shift_right))
            link(v.tensor_copy(nblk[:, :], cnt_i[:, :]))
            link(v.memset(one_f[:, :], 1.0))
            link(v.tensor_copy(jn[:, :], jn_i[:, :]))
            link(v.tensor_tensor_scan(incl[:, :], one_f[:, :], nblk[:, :], 0.0, ALU.mult, ALU.add))
            link(v.tensor_tensor(first[:, :], incl[:, :], nblk[:, :], ALU.subtract))
            for c in range(3):
                v.scalar_tensor_tensor(junk2[0:BJ, c, :], incl[0:BJ, :], jn[:, c:c + 1], one_f[0:BJ, :], ALU.is_le, ALU.mult,
                                       accum_out=blk_e[:, c:c + 1])
            link(v.tensor_scalar(first[:, :], first[:, :], float(P), None, ALU.mult))
            for c in range(3):
                ins = v.scalar_tensor_tensor(junk2[0:BJ, c, :], incl[0:BJ, :], jn[:, c:c + 1], nblk[0:BJ, :], ALU.is_le, ALU.mult,
                                             accum_out=blk_b[:, c:c + 1])
            link(ins)
            link(v.tensor_tensor(blk_b[:, :], jn[:, :], blk_b[:, :], ALU.subtract))
            link(v.scalar_tensor_tensor(blk_o[:, :], blk_e[:, :], float(CAP // P), blk_b[:, :], ALU.mult, ALU.add))
            link(v.tensor_scalar(blk_r[:, :], blk_o[:, :], float(NE * CAP // P - 1), None, ALU.min))
            link(v.tensor_scalar(blk_i[:, :], blk_e[:, :], float(NE - 1), None, ALU.min))
            link(v.tensor_scalar(last_turn[:, :], incl[0:1, NE - 1:NE], -1.0, None, ALU.add))
            link(v.tensor_scalar(last_turn[:, :], last_turn[:, :], 3, None, ALU.arith_shift_right))
            assert steps[0] == TAB_DONE and UNROLL == 1 << 3 and P == 1 << 7
            last = last_filled(dve)
            dve.wait_ge(idr_in.sem, 16 * 3)
            v.tensor_copy(idr_f[:, :, :], idr[:, :, :]).then_inc(idr_c.sem, 1)
            v.memset(ids[:, NBLK:], 0).then_inc(ids_c.sem, 1)
            dve.wait_ge(idT_f.sem, 1)
            v.tensor_copy(ids[:, 0:NBLK].rearrange("p (j c) -> p c j", c=3),
                          QF[1][:, 0:NBLK].rearrange("p (c j) -> p c j", c=3)).then_inc(ids_c.sem, 1)
            dve.wait_ge(ids_c.sem, 2)
            for s_ in range(UNROLL):
                v.tensor_copy(idb[s_][:, :], ids[:, s_:s_ + 1]).then_inc(idb_d.sem, 1)

            def body(i, sure):
                for s_ in range(UNROLL):
                    dve.wait_ge(xgT_f.sem, xgT_f.at(i, s_ + 1))
                    if up_f.at(i, s_ - 1, True):
                        dve.wait_ge(up_f.sem, up_f.at(i, s_ - 1))
                    v.tensor_copy(xgT[s_ % 2][:, :, :], XT[s_ % 2][:, 0:KD * P].rearrange("p (k t) -> p k t", k=KD)).then_inc(xgT_c.sem, 1)
                    dve.wait_ge(xg_in[s_].sem, xg_in[s_].at(i, 16))
                    v.tensor_copy(idb[s_][:, :], ids[:, bass.ds((i + 1) * UNROLL + s_, 1)]).then_inc(idb_d.sem, 1)
                    if sure:
                        f = i * UNROLL + s_
                        if slot_d.at(i, s_ - 1, True):
                            dve.wait_ge(slot_d.sem, slot_d.at(i, s_ - 1))
                        v.scalar_tensor_tensor(junk3[:, s_ % 2, :], iota_e[:, :], sel_e[:, bass.ds(f, 1)], first[:, :],
                                               ALU.is_equal, ALU.mult, accum_out=slot[:, bass.ds(f, 1)]).then_inc(slot_d.sem, 1)

            body(0, True)
            further_turns(dve, last, body)
            dve.wait_ge(slot_d.sem, slot_d.at(SURE - 1, UNROLL))
            v.tensor_tensor(slot[:, :], slot[:, :], sel_r[:, :], ALU.add).then_inc(slot_i.sem, 1)
            dve.wait_ge(slot_i.sem, 1)
            v.tensor_copy(slot_n[:, :], slot[:, :]).then_inc(slot_i.sem, 1)
            dve.wait_ge(slot_i.sem, 2)
            dve.wait_ge(idb_d.sem, UNROLL * (SURE + 1))

        mid.close()

        gat_in = [sig(f"gat_in{i}", 8 * TOPK) for i in range(2)]
        acc_in = [sig(f"acc_in{i}", 8) for i in range(2)]
        out_st = [sig(f"out_st{i}", 8) for i in range(2)]
        add_s = sig("add_s", TOPK)
        sidx = sig("sidx")
        bst, bag = sig("bst"), sig("bag")
        var_d, std_d, rstd_d, fin_d = sig("var_d"), sig("std_d"), sig("rstd_d"), sig("fin_d")
        end = ExitStack()

        def se(name, shape, dt=FP32):
            return end.enter_context(nc.sbuf_tensor(name, shape, dt))

        G = [se(f"G{i}", [P, TOPK, D]) for i in range(2)]
        si = [se(f"si{i}", [P, TOPK], I32) for i in range(2)]
        ac = [se(f"ac{i}", [P, D]) for i in range(2)]
        bs = se("bs", [P, 6])
        bm = se("bm", [P, 2])
        vr = se("vr", [P, 1])
        sd = se("sd", [P, 1])
        rd = se("rd", [P, 1])

        def tiles(eng, body):
            for t in range(2):
                body(t, t)
            with eng.Fori(1, NTILE // 2) as i:
                for p in range(2):
                    body(i * 2 + p, p)

        block = end.enter_context(nc.Block())

        @block.sync
        def _(sp):
            def body(t, p):
                if out_st[p].at(t - p - 2, 16, True):
                    sp.wait_ge(out_st[p].sem, out_st[p].at(t - p - 2, 16))
                sp.dma_start(ac[p][:, :], acc_dram[bass.ds(t * P, P), :]).then_inc(acc_in[p].sem, 16)
                if isinstance(t, int) and t == 0:
                    return
                if fin_d.at(t - 1, 1, True):
                    sp.wait_ge(fin_d.sem, fin_d.at(t - 1, 1))
                sp.dma_start(out[bass.ds((t - 1) * P, P), :], ac[1 - p][:, :]).then_inc(out_st[1 - p].sem, 16)

            tiles(sp, body)
            sp.wait_ge(fin_d.sem, fin_d.at(NTILE - 1, 1))
            sp.dma_start(out[(NTILE - 1) * P:, :], ac[(NTILE - 1) % 2][:, :]).then_inc(out_st[1].sem, 16)
            for p in range(2):
                sp.wait_ge(out_st[p].sem, out_st[p].at(NTILE - 2, 16))

        @block.gpsimd
        def _(pool):
            def body(t, p):
                pool.wait_ge(sidx.sem, sidx.at(t, 1))
                if add_s.at(t - 2, TOPK, True):
                    pool.wait_ge(add_s.sem, add_s.at(t - 2, TOPK))
                pool.sem_inc(tick, 1)
                for k in range(TOPK):
                    nc.gpsimd.indirect_dma_start(G[p][:, k, :], None, y_dram,
                                                 bass.IndirectOffsetOnAxis(ap=si[p][:, k:k + 1], axis=0)).then_inc(gat_in[p].sem, 16)

            tiles(pool, body)

        @block.scalar
        def _(act):
            def body(t, p):
                act.wait_ge(var_d.sem, var_d.at(t, 1))
                nc.scalar.activation(sd[:, :], vr[:, :], ACT.Sqrt).then_inc(std_d.sem, 1)

            tiles(act, body)

        @block.vector
        def _(dve):
            v = nc.vector

            def body(t, p):
                if gat_in[p].at(t - p - 2, 16 * TOPK, True):
                    dve.wait_ge(gat_in[p].sem, gat_in[p].at(t - p - 2, 16 * TOPK))
                v.tensor_copy(si[p][:, :], slot_n[:, bass.ds(t * TOPK, TOPK)]).then_inc(sidx.sem, 1)

            def add(t, p):
                dve.wait_ge(acc_in[p].sem, acc_in[p].at(t - p, 16))
                dve.wait_ge(gat_in[p].sem, gat_in[p].at(t - p, 16 * TOPK))
                for k in range(TOPK):
                    dve.wait_ge(add_s.sem, add_s.at(t, k))
                    v.scalar_tensor_tensor(ac[p][:, :], G[p][:, k, :], gate[:, bass.ds(t * TOPK + k, 1)], ac[p][:, :],
                                           ALU.mult, ALU.add).then_inc(add_s.sem, 1)
                dve.wait_ge(add_s.sem, add_s.at(t, TOPK))
                v.bn_stats(bs[:, :], ac[p][:, :]).then_inc(bst.sem, 1)
                dve.wait_ge(bst.sem, bst.at(t, 1))
                dve.sem_inc(tick, 1)
                v.bn_aggr(bm[:, :], bs[:, :]).then_inc(bag.sem, 1)
                dve.wait_ge(bag.sem, bag.at(t, 1))
                v.tensor_scalar(vr[:, :], bm[:, 1:2], LN_EPS, None, ALU.add).then_inc(var_d.sem, 1)
                dve.wait_ge(std_d.sem, std_d.at(t, 1))
                v.reciprocal(rd[:, :], sd[:, :]).then_inc(rstd_d.sem, 1)
                dve.wait_ge(rstd_d.sem, rstd_d.at(t, 1))
                v.tensor_scalar(ac[p][:, :], ac[p][:, :], bm[:, 0:1], rd[:, 0:1], ALU.subtract, ALU.mult).then_inc(fin_d.sem, 1)

            body(0, 0)
            body(1, 1)
            add(0, 0)
            body(2, 0)
            add(1, 1)
            body(3, 1)
            with dve.Fori(1, NTILE // 2 - 1) as i:
                for p in range(2):
                    add(i * 2 + p, p)
                    body(i * 2 + (p + 2), p)
            for p in range(2):
                add(NTILE - 2 + p, p)

        end.close()


def chunked(w, p=128):
    n = w.shape[0] // p
    return np.ascontiguousarray(w.reshape(n, p, *w.shape[1:]).swapaxes(0, 1))


def kernel(**inputs):
    import concourse.bacc as _bacc
    from concourse import mybir as _mybir
    from concourse.bass_utils import run_bass_kernel_spmd as _run

    g = {k: np.asarray(v) for k, v in inputs.items()}
    m = {k[len("L0_attn_h_"):]: v for k, v in g.items() if k.startswith("L0_attn_h_")}
    x = {k[len("L0_xattn_"):]: v for k, v in g.items() if k.startswith("L0_xattn_")}
    f = {k[len("L0_ffn_"):]: v for k, v in g.items() if k.startswith("L0_ffn_")}
    xs, cs = g["x"].reshape(NT, D), g["ctx_1024"].reshape(NT, D)
    xp = m["x_proj_w"]
    xp = np.concatenate([xp[:R], np.zeros((R, DI), xp.dtype), xp[R:]], 0)
    moe = np.concatenate([f["w_gate"].reshape(NE, INTER, KD, P).transpose(0, 3, 2, 1).reshape(NE, P, KD * INTER),
                          f["w_down"].transpose(0, 2, 1)], 2).reshape(NE * P, KD * INTER + D)
    arrays = {
        "x": xs, "xT": chunked(xs.T), "c": cs, "cT": chunked(cs.T),
        "w_in": chunked(m["in_proj_w"].T), "conv_w": chunked(m["conv_w"]), "conv_b": chunked(m["conv_b"]),
        "w_xp": chunked(xp.T), "w_dt": m["dt_proj_w"].T, "dt_b": chunked(m["dt_proj_b"]),
        "A_log": chunked(m["A_log"]), "D": chunked(m["D_param"]), "w_out": chunked(m["out_proj_w"].T),
        "w_q": chunked(x["Wq"]), "w_k": chunked(x["Wk"]), "w_v": chunked(x["Wv"]), "w_o": chunked(x["Wo"]),
        "b_q": chunked(x["bq"]), "b_k": chunked(x["bk"]), "w_1": chunked(x["W1"]), "b_1": chunked(x["b1"]),
        "w_2": chunked(x["W2"]), "w_r": chunked(f["router_w"].T), "b_r": f["expert_bias"],
        "ws_g": chunked(f["w_gate_shared"].T), "ws_d": f["w_down_shared"].T, "w_moe": moe,
    } | {n: x[n] for n in ROWS}
    arrays = {k: np.ascontiguousarray(v) for k, v in arrays.items()}
    nc = _bacc.Bacc("TRN2", target_bir_lowering=False, num_devices=1)
    aps = {k: nc.dram_tensor(f"in_{k}", v.shape, _mybir.dt.from_np(v.dtype), kind="ExternalInput").ap()
           for k, v in arrays.items()}
    out = nc.dram_tensor("out", (NT, D), FP32, kind="ExternalOutput").ap()
    decoder_kernel(nc, aps, out)
    r = _run(nc, [{f"in_{k}": v for k, v in arrays.items()}], core_ids=[0])
    return r.results[0]["out"].reshape(NB, T, D)
```

```python
import concourse.bass as bass
from concourse import mybir
from contextlib import ExitStack
import numpy as np

FP32 = mybir.dt.float32
BF16 = mybir.dt.bfloat16
I32 = mybir.dt.int32
U32 = mybir.dt.uint32
ACT = mybir.ActivationFunctionType
ALU = mybir.AluOpType
AX = mybir.AxisListType

P = 128
NB, T, D = 8, 256, 256
NT = NB * T
KD = D // P
QT = T // P
DI = 512
NC = DI // P
NS = 16
R = 16
TAPS = 4
XP = 64
FOLD_DVE = (4, 5, 6, 7)
FOLD_POOL = (1, 15)
NG = 4
SG = NS // NG
NTAU = NG * NC
NBUF = 4
NH = 8
LEAD = 2
FF = 1024
KF = FF // P
NE, TOPK, INTER = 160, 8, 128
CAP = NT
NTILE = NT // P
NBLK = NT * TOPK // P + NE
BJ = NBLK // 3
LN_EPS = 1e-5
SCALE = 1.0 / 16.0
UNROLL = 8
TURNS = NBLK // UNROLL
SURE = NT * TOPK // P // UNROLL
YG = 4
NSEL = NTILE * TOPK
ROWS = ("bv", "bo", "ln1_g", "ln1_b", "b2", "ln2_g", "ln2_b")


def whole(t):
    return t[tuple(slice(None) for _ in t.shape)]


class Sig:

    def __init__(self, sem, per):
        self.sem, self.per = sem, per

    def at(self, b, c, due=False):
        v = b * self.per + c
        return (not isinstance(v, int) or v > 0) if due else v


def decoder_kernel(nc, a, out):
    ctx = ExitStack()
    with ctx:
        def sb(name, shape, dt=FP32):
            return ctx.enter_context(nc.sbuf_tensor(name, shape, dt))

        def ps(name, shape=(P, 512), dt=FP32):
            return ctx.enter_context(nc.psum_tensor(name, list(shape), dt))

        def sig(name, per=1):
            return Sig(ctx.enter_context(nc.semaphore(name)), per)

        x2_dram = nc.dram_tensor("x2_dram", (NT, D), FP32, kind="Internal").ap()
        acc_dram = nc.dram_tensor("acc_dram", (NT, D), FP32, kind="Internal").ap()
        bc_dram = nc.dram_tensor("bc_dram", (NB, 2, NS * T), FP32, kind="Internal").ap()
        tok_dram = nc.dram_tensor("tok_dram", (NE * CAP, 1), I32, kind="Internal").ap()
        y_dram = nc.dram_tensor("y_dram", (NBLK * P, D), FP32, kind="Internal").ap()
        blk_dram = nc.dram_tensor("blk_dram", (2, NBLK), I32, kind="Internal").ap()

        w_in = sb("w_in", [P, KD, 2 * DI])
        w_conv = sb("w_conv", [P, NC, TAPS])
        b_conv = sb("b_conv", [P, NC])
        w_xp = sb("w_xp", [P, NC, XP])
        w_dt = sb("w_dt", [R, DI])
        b_dt = sb("b_dt", [P, NC])
        a_neg = sb("a_neg", [P, NC, NS])
        d_par = sb("d_par", [P, NC])
        w_out = sb("w_out", [P, NC, D])
        w_q = sb("w_q", [P, KD, D])
        w_k = sb("w_k", [P, KD, D])
        w_v = sb("w_v", [P, KD, D])
        w_o = sb("w_o", [P, KD, D])
        b_q = sb("b_q", [P, KD])
        b_k = sb("b_k", [P, KD])
        w_1 = sb("w_1", [P, KD, FF])
        b_1 = sb("b_1", [P, KF])
        w_2 = sb("w_2", [P, KF, D])
        rows = sb("rows", [P, 7, D])
        BV, BO, G1, B1, B2, G2, BB2 = range(7)
        w_r = sb("w_r", [P, KD, NE])
        b_r = sb("b_r", [P, NE])
        ws_g = sb("ws_g", [P, KD, INTER])
        ws_d = sb("ws_d", [P, D])
        ident = sb("ident", [P, P])
        earlier = sb("earlier", [P, P], BF16)
        ones = sb("ones", [P, P], BF16)
        iota_e = sb("iota_e", [P, NE])
        ids_all = sb("ids_all", [P, NTILE], I32)
        m_half = sb("m_half", [P, QT])
        zeros = sb("zeros", [P, D])

        sel_e = sb("sel_e", [P, NSEL])
        sel_r = sb("sel_r", [P, NSEL])
        gate = sb("gate", [P, NSEL])
        m_sum = sb("m_sum", [P, NE], BF16)

        PB = [ps("PB0"), ps("PB1")]
        Y = [ps("Y0"), ps("Y1")]
        QA = [ps(f"QA{i}") for i in range(2)]
        QF = [ps(f"QF{i}") for i in range(2)]

        w_mamba = sig("w_mamba")
        w_rest = sig("w_rest")
        k_pool = sig("k_pool")
        k_scaled = sig("k_scaled")
        zeroed = sig("zeroed")
        xt_in = sig("xt_in", 16)
        proj_f = sig("proj_f", 7)
        proj_c = sig("proj_c", 6)
        tap0 = sig("tap0")
        conv = sig("conv", NC * (TAPS - 1))
        u_d = sig("u_d")
        xdb_c = sig("xdb_c")
        bc_w = sig("bc_w", 16)
        bc_in = [sig(f"bc_in{i}", 8 * NG) for i in range(2)]
        softp = sig("softp", 4)
        lost = sig("lost", 2)
        dl_d = sig("dl_d")
        du_d = sig("du_d")
        decay_d = sig("decay_d", NTAU)
        inflow_d = sig("inflow_d", NTAU)
        scan_d = sig("scan_d", NTAU)
        outflow_d = sig("outflow_d", NTAU)
        fold_v = sig("fold_v", len(FOLD_DVE))
        fold_g = sig("fold_g", len(FOLD_POOL))
        sum_d = sig("sum_d", NTAU)
        y_read = sig("y_read", NC)
        y_d = sig("y_d", NC)
        q_in, res_in = sig("q_in", 32), sig("res_in", 16)
        v_f, v_c, kT_f, kT_c = sig("v_f"), sig("v_c"), sig("kT_f"), sig("kT_c")
        out_f, r0_d = sig("out_f"), sig("r0_d")
        x1T_f, x1T_c, qT_f, qT_c = sig("x1T_f"), sig("x1T_c"), sig("qT_f"), sig("qT_c")
        sco_f, max_d, p_d = sig("sco_f"), sig("max_d", 2), sig("p_d")
        pT_f, pT_c, aT_f, aT_c = sig("pT_f"), sig("pT_c"), sig("aT_f"), sig("aT_c")
        rsum_d, mg_f, mg_c = sig("rsum_d"), sig("mg_f"), sig("mg_c")
        x2aT_f, x2aT_c, h_f, h_c = sig("x2aT_f"), sig("x2aT_c"), sig("h_f", 4), sig("h_c", 4)
        ff_f, ff_c = sig("ff_f"), sig("ff_c")
        stat1 = [sig(f"stat1_{i}", QT) for i in range(4)]
        stat2 = [sig(f"stat2_{i}") for i in range(4)]
        root_d = [sig(f"root_d{i}", 2) for i in range(4)]
        norm_d = [sig(f"norm_d{i}") for i in range(4)]
        base_d = sig("base_d", 3)
        aff1_d = sig("aff1_d", 3)
        aff2_d = sig("aff2_d", 2)
        res_d = sig("res_d")
        x2T_f, x2T_c = sig("x2T_f"), sig("x2T_c")
        lg_f, lg_c, lg_e, key_d = sig("lg_f"), sig("lg_c"), sig("lg_e"), sig("key_d")
        sh_f, sh_c, hs_d, so_f, acc_d = sig("sh_f"), sig("sh_c", 2), sig("hs_d"), sig("so_f"), sig("acc_d")
        x2_st, acc_st = sig("x2_st", 16), sig("acc_st", 16)
        pick = sig("pick", 14)
        mask_d, cum_f, cum_c, msum_d = sig("mask_d"), sig("cum_f"), sig("cum_c"), sig("msum_d")
        addr = sig("addr", 2)
        addr_d = sig("addr_d")
        ranked = sig("ranked")
        scat = sig("scat", 16 * QT * TOPK)
        settled = sig("settled")
        y_zero = sig("y_zero", 16)
        zero_read, a_exp, k_conv = sig("zero_read"), sig("a_exp"), sig("k_conv")
        rank_s, selr_d = sig("rank_s", QT * TOPK), sig("selr_d")
        tick = sig("tick").sem

        front = ExitStack()
        def sf(name, shape, dt=FP32):
            return front.enter_context(nc.sbuf_tensor(name, shape, dt))

        xt = sf("xt", [P, KD, T])
        ct = sf("ct", [P, KD, T])
        cr = sf("cr", [P, QT, D])
        xin = sf("xin", [P, NC, TAPS - 1 + T])
        cv = sf("cv", [P, NC, T])
        th = sf("th", [P, NC, T])
        u = [sf(f"u{i}", [P, NC, T]) for i in range(2)]
        sz = [sf(f"sz{i}", [P, NC, T]) for i in range(2)]
        dl = [sf(f"dl{i}", [P, NC, T]) for i in range(2)]
        du = sf("du", [P, NC, T])
        xdb = sf("xdb", [XP, T])
        bc = [sf(f"bc{i}", [P, 2, SG, T]) for i in range(2)]
        da = [sf(f"da{i}", [P, SG, T]) for i in range(NBUF)]
        hb = [sf(f"hb{i}", [P, SG, T]) for i in range(NH)]
        x1 = [sf(f"x1_{i}", [P, QT, D]) for i in range(2)]
        aT = sf("aT", [P, KD, T])
        fT = sf("fT", [P, KD, T])
        qT = sf("qT", [P, KD, T])
        kT = sf("kT", [P, KD, T])
        vv = sf("vv", [P, QT, D])
        pe_ = sf("pe_", [P, QT, T])
        base = sf("base", [P, QT, D])
        base2 = sf("base2", [P, QT, D])
        x2a = sf("x2a", [P, QT, D])
        hT = sf("hT", [P, KF, T])
        x2 = sf("x2", [P, QT, D])
        hs = sf("hs", [P, T])
        acc = sf("acc", [P, QT, D])
        stats = sf("stats", [P, 4, QT, 6])
        mv = sf("mv", [P, 4, QT, 2])
        ve = sf("ve", [P, 4, QT])
        rs = sf("rs", [P, 4, QT])
        nmx = sf("nmx", [P, QT])
        ssum = sf("ssum", [P, QT])
        rsum = sf("rsum", [P, QT])
        key = sf("key", [P, QT, NE])
        rep = sf("rep", [P, QT, NE])
        msk_b = sf("msk_b", [P, QT, NE], BF16)
        cum = sf("cum", [P, QT, NE])
        hth = cum[:, :, :].rearrange("p q e -> p (q e)")[:, 0:T]
        junk = [sf(f"junk{i}", [P, NE]) for i in range(2)]
        iota_i = junk[0][:, :].bitcast(I32)
        top = sf("top", [P, QT, TOPK])
        ti = sf("ti", [P, QT, TOPK], U32)
        pr = sf("pr", [P, QT, TOPK])
        psm = sf("psm", [P, QT])
        e_st = sf("e_st", [P, QT, TOPK])
        r_st = sf("r_st", [P, QT, TOPK])
        ad_f = sf("ad_f", [P, QT, TOPK])
        ad_i = sf("ad_i", [P, QT, TOPK], I32)
        id_st = sf("id_st", [P, QT], I32)
        zi = th[:, :, :].rearrange("p c t -> p (c t)").bitcast(I32)

        def pair(bank):
            return bank[:, :].rearrange("p (c t) -> p c t", c=2)

        def exists(b):
            return not isinstance(b, int) or 0 <= b < NB

        def tile_at(s, p, t):
            if t < 0:
                return s - 1, 1 - p, t + NTAU
            if t >= NTAU:
                return s + 1, 1 - p, t - NTAU
            return s, p, t

        def all_turns(eng, turn):
            for s in range(-1, 3):
                turn(s, s % 2)
            with eng.Fori(1, 3) as i:
                for k in range(2):
                    turn(i * 2 + (k + 1), 1 - k)
            for s in range(7, NB + 3):
                turn(s, s % 2)

        block = front.enter_context(nc.Block())

        @block.sync
        def _(sp):
            for dst, src in ((w_in, "w_in"), (w_conv, "conv_w"), (b_conv, "conv_b"), (w_xp, "w_xp"),
                             (w_dt, "w_dt"), (b_dt, "dt_b"), (a_neg, "A_log"), (d_par, "D")):
                sp.dma_start(whole(dst), a[src]).then_inc(w_mamba.sem, 16)

            def x_load(b):
                if proj_f.at(b - 1, 4, True):
                    sp.wait_ge(proj_f.sem, proj_f.at(b - 1, 4))
                sp.sem_inc(tick, 1)
                sp.dma_start(xt[:, :, :], a["xT"][:, :, bass.ts(b, T)]).then_inc(xt_in.sem, 16)

            def bc_out(b):
                sp.wait_ge(xdb_c.sem, xdb_c.at(b, 1))
                sp.sem_inc(tick, 1)
                sp.dma_start(bc_dram[b].rearrange("a (n t) -> (a n) t", n=NS), xdb[2 * R:XP, :]).then_inc(bc_w.sem, 16)

            def bc_load(b, g):
                if g == 0:
                    sp.wait_ge(bc_w.sem, bc_w.at(b, 16))
                    sp.sem_inc(tick, 1)
                if outflow_d.at(b, NC * (g - 1), True):
                    sp.wait_ge(outflow_d.sem, outflow_d.at(b, NC * (g - 1)))
                src = bc_dram[b][:, g * SG * T:(g + 1) * SG * T]
                sp.sem_inc(tick, 1)
                sp.dma_start(bc[g % 2][:, :, :, :].rearrange("p a n t -> p a (n t)"),
                             src.unsqueeze(0).broadcast_to([P, 2, SG * T])).then_inc(bc_in[g % 2].sem, 16)

            def q_load(b):
                if v_f.at(b - 1, 1, True):
                    sp.wait_ge(v_f.sem, v_f.at(b - 1, 1))
                if base_d.at(b - 1, 3, True):
                    sp.wait_ge(base_d.sem, base_d.at(b - 1, 3))
                sp.sem_inc(tick, 1)
                sp.dma_start(ct[:, :, :], a["cT"][:, :, bass.ts(b, T)]).then_inc(q_in.sem, 16)
                sp.dma_start(cr[:, :, :], a["c"][bass.ts(b, T), :].rearrange("(q p) d -> p q d", p=P)).then_inc(q_in.sem, 16)

            def residual_load(b, p):
                if res_d.at(b - 2, 1, True):
                    sp.wait_ge(res_d.sem, res_d.at(b - 2, 1))
                sp.sem_inc(tick, 1)
                sp.dma_start(x1[p][:, :, :], a["x"][bass.ts(b, T), :].rearrange("(q p) d -> p q d", p=P)).then_inc(res_in.sem, 16)

            def x2_store(b):
                sp.wait_ge(norm_d[3].sem, norm_d[3].at(b, 1))
                sp.sem_inc(tick, 1)
                sp.dma_start(x2_dram[bass.ts(b, T), :].rearrange("(q p) d -> p q d", p=P), x2[:, :, :]).then_inc(x2_st.sem, 16)

            def y_clear(b):
                if isinstance(b, int) and b == 0:
                    sp.wait_ge(k_pool.sem, 16)
                n = (NBLK - SURE * UNROLL) // NB
                sp.dma_start(y_dram[bass.ds((b * n + SURE * UNROLL) * P, n * P), :].rearrange("(j p) d -> p j d", p=P),
                             zeros[:, :].unsqueeze(1).to_broadcast([P, n, D])).then_inc(y_zero.sem, 16)

            def acc_store(b):
                sp.wait_ge(acc_d.sem, acc_d.at(b, 1))
                sp.sem_inc(tick, 1)
                sp.dma_start(acc_dram[bass.ts(b, T), :].rearrange("(q p) d -> p q d", p=P), acc[:, :, :]).then_inc(acc_st.sem, 16)

            x_load(0)
            for dst, src in ((w_out, "w_out"), (w_q, "w_q"), (w_k, "w_k"), (w_v, "w_v"), (w_o, "w_o"), (b_q, "b_q"),
                             (b_k, "b_k"), (w_1, "w_1"), (b_1, "b_1"), (w_2, "w_2"), (w_r, "w_r"),
                             (ws_g, "ws_g"), (ws_d, "ws_d")):
                sp.dma_start(whole(dst), a[src]).then_inc(w_rest.sem, 16)
            for i in range(7):
                sp.dma_start(rows[:, i, :], a[ROWS[i]].unsqueeze(0).broadcast_to([P, D])).then_inc(w_rest.sem, 16)
            sp.dma_start(b_r[:, :], a["b_r"].unsqueeze(0).broadcast_to([P, NE])).then_inc(w_rest.sem, 16)

            def turn(s, p):
                if exists(s + 1) and not (isinstance(s, int) and s == -1):
                    x_load(s + 1)
                if exists(s):
                    bc_load(s, 1)
                if exists(s):
                    bc_load(s, 2)
                    q_load(s)
                if exists(s + 1):
                    bc_out(s + 1)
                if exists(s):
                    bc_load(s, 3)
                if exists(s - 2):
                    x2_store(s - 2)
                if exists(s + 1):
                    bc_load(s + 1, 0)
                if exists(s):
                    residual_load(s, p)
                    y_clear(s)
                if exists(s - 2):
                    acc_store(s - 2)

            all_turns(sp, turn)
            sp.wait_ge(x2_st.sem, x2_st.at(NB - 1, 16))
            sp.wait_ge(acc_st.sem, acc_st.at(NB - 1, 16))
            sp.wait_ge(y_zero.sem, y_zero.at(NB - 1, 16))

        @block.gpsimd
        def _(pool):
            g = nc.gpsimd
            g.memset(ident[:, :], 0.0).then_inc(k_pool.sem, 1)
            g.memset(earlier[:, :], 1.0).then_inc(k_pool.sem, 1)
            g.memset(ones[:, :], 1.0).then_inc(k_pool.sem, 1)
            g.memset(xin[:, :, 0:TAPS - 1], 0.0).then_inc(k_pool.sem, 1)
            for i in range(NBUF):
                g.memset(da[i][:, :, 0:1], 0.0).then_inc(k_pool.sem, 1)
            g.memset(m_sum[:, :], 0.0).then_inc(k_pool.sem, 1)
            g.memset(m_half[:, :], -0.5).then_inc(k_pool.sem, 1)
            g.memset(zi, 0).then_inc(k_pool.sem, 1)
            g.memset(zeros[:, :], 0.0).then_inc(k_pool.sem, 1)
            g.iota(iota_i[:, :], pattern=[[1, NE]], base=0, channel_multiplier=0).then_inc(k_pool.sem, 1)
            g.iota(ids_all[:, :], pattern=[[P, NTILE]], base=0, channel_multiplier=1).then_inc(k_pool.sem, 1)
            pool.wait_ge(k_pool.sem, 14)
            g.affine_select(out=ident[:, :], in_=ident[:, :], compare_op=ALU.not_equal, fill=1.0, base=0,
                            pattern=[[-1, P]], channel_multiplier=1).then_inc(k_pool.sem, 1)
            g.affine_select(out=earlier[:, :], in_=earlier[:, :], compare_op=ALU.is_gt, fill=0.0, base=0,
                            pattern=[[1, P]], channel_multiplier=-1).then_inc(k_pool.sem, 1)
            table = tok_dram.rearrange("(p n) o -> p (n o)", p=P)
            pieces = -(-table.shape[1] // (NC * T))
            for i in range(pieces):
                lo, hi = i * NC * T, min((i + 1) * NC * T, table.shape[1])
                pool.dma_start(table[:, lo:hi], zi[:, 0:hi - lo]).then_inc(zeroed.sem, 16)
            pool.wait_ge(zeroed.sem, 16 * pieces)
            pool.sem_inc(zero_read.sem, 1)

            def inflow(b, p, t):
                gr, c = t // NC, t % NC
                if t == 0:
                    pool.wait_ge(du_d.sem, du_d.at(b, 1))
                if c == 0:
                    pool.wait_ge(bc_in[gr % 2].sem, bc_in[gr % 2].at(b, 16 * (gr // 2 + 1)))
                if sum_d.at(b, t - NH + 1, True):
                    pool.wait_ge(sum_d.sem, sum_d.at(b, t - NH + 1))
                g.tensor_tensor(hb[t % NH][:, :, :], bc[gr % 2][:, 0, :, :],
                                du[:, c, :].unsqueeze(1).to_broadcast([P, SG, T]), ALU.mult).then_inc(inflow_d.sem, 1)

            def fold(b, t):
                pool.wait_ge(outflow_d.sem, outflow_d.at(b, t + 1))
                h = hb[t % NH]
                g.tensor_tensor(h[:, 0:SG // 2, :], h[:, 0:SG // 2, :], h[:, SG // 2:, :], ALU.add).then_inc(fold_g.sem, 1)

            def ln_root(b, i):
                pool.wait_ge(stat2[i].sem, stat2[i].at(b, 1))
                pool.sem_inc(tick, 1)
                g.tensor_scalar(ve[:, i, :], mv[:, i, :, 1], LN_EPS, None, ALU.add).then_inc(root_d[i].sem, 1)
                pool.wait_ge(root_d[i].sem, root_d[i].at(b, 1))
                g.tensor_tensor(rs[:, i, :], ve[:, i, :], m_half[:, :], ALU.pow).then_inc(root_d[i].sem, 1)

            def row(i):
                return rows[:, i, :].unsqueeze(1).to_broadcast([P, QT, D])

            def base_(b, p):
                if isinstance(b, int) and b == 0:
                    pool.wait_ge(w_rest.sem, 16 * 21)
                pool.wait_ge(norm_d[0].sem, norm_d[0].at(b, 1))
                pool.wait_ge(q_in.sem, q_in.at(b, 32))
                if mg_c.at(b - 1, 1, True):
                    pool.wait_ge(mg_c.sem, mg_c.at(b - 1, 1))
                g.tensor_tensor(base[:, :, :], x1[p][:, :, :], cr[:, :, :], ALU.add).then_inc(base_d.sem, 1)

            def base_c(b):
                pool.wait_ge(base_d.sem, base_d.at(b, 1))
                g.tensor_tensor(base[:, :, :], base[:, :, :], cr[:, :, :], ALU.add).then_inc(base_d.sem, 1)

            def base_bo(b):
                pool.wait_ge(base_d.sem, base_d.at(b, 2))
                g.tensor_tensor(base[:, :, :], base[:, :, :], row(BO), ALU.add).then_inc(base_d.sem, 1)

            def ln1_affine(b):
                pool.wait_ge(norm_d[1].sem, norm_d[1].at(b, 1))
                g.tensor_tensor(x2a[:, :, :], x2a[:, :, :], row(G1), ALU.mult).then_inc(aff1_d.sem, 1)
                pool.wait_ge(aff1_d.sem, aff1_d.at(b, 1))
                g.tensor_tensor(x2a[:, :, :], x2a[:, :, :], row(B1), ALU.add).then_inc(aff1_d.sem, 1)

            def base2_(b):
                pool.wait_ge(aff1_d.sem, aff1_d.at(b, 2))
                if ff_c.at(b - 1, 1, True):
                    pool.wait_ge(ff_c.sem, ff_c.at(b - 1, 1))
                g.tensor_tensor(base2[:, :, :], x2a[:, :, :], row(B2), ALU.add).then_inc(aff1_d.sem, 1)

            def ln2_affine(b):
                pool.wait_ge(norm_d[2].sem, norm_d[2].at(b, 1))
                g.tensor_tensor(x2[:, :, :], x2[:, :, :], row(G2), ALU.mult).then_inc(aff2_d.sem, 1)
                pool.wait_ge(aff2_d.sem, aff2_d.at(b, 1))
                g.tensor_tensor(x2[:, :, :], x2[:, :, :], row(BB2), ALU.add).then_inc(aff2_d.sem, 1)

            def scatter(b, c):
                if c == 0:
                    pool.wait_ge(addr_d.sem, addr_d.at(b, 1))
                    pool.sem_inc(tick, 1)
                q, k = c // TOPK, c % TOPK
                g.indirect_dma_start(tok_dram, bass.IndirectOffsetOnAxis(ap=ad_i[:, q, k:k + 1], axis=0),
                                     id_st[:, q:q + 1], None).then_inc(scat.sem, 16)

            def settle(b):
                pool.wait_ge(scat.sem, scat.at(b, 16 * QT * TOPK))
                pool.sem_inc(settled.sem, 1)

            pool.sem_inc(settled.sem, 1)
            SCATTER_AT = (4, 4, 5, 5, 5, 6, 7, 8, 9, 9, 11, 12, 12, 13, 13, 13)

            def turn(s, p):
                for t in range(NTAU):
                    b, bp, tl = tile_at(s, p, t + LEAD)
                    if exists(b):
                        inflow(b, bp, tl)
                    b, bp, tl = tile_at(s, p, t - 1)
                    if exists(b) and tl in FOLD_POOL:
                        fold(b, tl)
                    if exists(s - 1):
                        if t == 3:
                            ln_root(s - 1, 0)
                        elif t == 6:
                            base_(s - 1, 1 - p)
                        elif t == 7:
                            base_c(s - 1)
                        elif t == 8:
                            base_bo(s - 1)
                        elif t == 12:
                            ln_root(s - 1, 1)
                        elif t == 14:
                            ln1_affine(s - 1)
                        elif t == 15:
                            base2_(s - 1)
                    if exists(s - 2):
                        if t == 9:
                            ln_root(s - 2, 2)
                        elif t == 10:
                            ln2_affine(s - 2)
                        elif t == 11:
                            ln_root(s - 2, 3)
                    if exists(s - 3):
                        for c in range(QT * TOPK):
                            if t == SCATTER_AT[c]:
                                scatter(s - 3, c)
                        if t == 15:
                            settle(s - 3)

            all_turns(pool, turn)
            pool.wait_ge(scat.sem, scat.at(NB - 1, 16 * QT * TOPK))

        @block.scalar
        def _(act):
            s = nc.scalar

            def x_in(b, f):
                act.wait_ge(proj_f.sem, proj_f.at(b, f + 1))
                if dl_d.at(b - 1, 1, True):
                    act.wait_ge(dl_d.sem, dl_d.at(b - 1, 1))
                if isinstance(b, int) and b == 0:
                    act.wait_ge(k_pool.sem, 16)
                s.activation(xin[:, 2 * f:2 * f + 2, TAPS - 1:], pair(PB[f]), ACT.Copy).then_inc(proj_c.sem, 1)

            def first_tap(b):
                act.wait_ge(proj_c.sem, proj_c.at(b, 2))
                if dl_d.at(b - 1, 1, True):
                    act.wait_ge(dl_d.sem, dl_d.at(b - 1, 1))
                for c in range(NC):
                    ins = s.activation(cv[:, c, :], xin[:, c, 0:T], ACT.Identity, bias=b_conv[:, c:c + 1], scale=w_conv[:, c, 0:1])
                ins.then_inc(tap0.sem, 1)

            def gates(b, p):
                if out_f.at(b - 2, 1, True):
                    act.wait_ge(out_f.sem, out_f.at(b - 2, 1))
                for f in range(2):
                    act.wait_ge(proj_f.sem, proj_f.at(b, f + 3))
                    s.activation(sz[p][:, 2 * f:2 * f + 2, :], pair(PB[f]), ACT.Silu).then_inc(proj_c.sem, 1)
                act.wait_ge(conv.sem, conv.at(b, NC * (TAPS - 1)))
                s.activation(u[p][:, :, :], cv[:, :, :], ACT.Silu).then_inc(u_d.sem, 1)

            def x_proj(b, p):
                act.wait_ge(proj_f.sem, proj_f.at(b, 5))
                if proj_f.at(b - 1, 7, True):
                    act.wait_ge(proj_f.sem, proj_f.at(b - 1, 7))
                if bc_w.at(b - 1, 16, True):
                    act.wait_ge(bc_w.sem, bc_w.at(b - 1, 16))
                s.activation(xdb[:, :], PB[0][0:XP, 0:T], ACT.Copy).then_inc(xdb_c.sem, 1)

            def dt_proj(b, p):
                if du_d.at(b - 2, 1, True):
                    act.wait_ge(du_d.sem, du_d.at(b - 2, 1))
                for f in range(2):
                    act.wait_ge(proj_f.sem, proj_f.at(b, 6 + f))
                    for i in range(2):
                        c = 2 * f + i
                        ins = s.activation(dl[p][:, c, :], pair(PB[(f + 1) % 2])[:, i, :], ACT.Identity, bias=b_dt[:, c:c + 1])
                    ins.then_inc(proj_c.sem, 1)

            def softplus(b, p):
                if isinstance(b, int) and b == 0:
                    s.activation(a_neg[:, :, :], a_neg[:, :, :], ACT.Exp).then_inc(a_exp.sem, 1)
                    act.wait_ge(zero_read.sem, 1)
                act.wait_ge(proj_c.sem, proj_c.at(b, 6))
                if dl_d.at(b - 1, 1, True):
                    act.wait_ge(dl_d.sem, dl_d.at(b - 1, 1))
                s.activation(th[:, :, :], dl[p][:, :, :], ACT.Abs).then_inc(softp.sem, 1)
                act.wait_ge(softp.sem, softp.at(b, 1))
                s.activation(th[:, :, :], th[:, :, :], ACT.Exp, scale=-1.0).then_inc(softp.sem, 1)

            def softplus_ln(b, p):
                act.wait_ge(softp.sem, softp.at(b, 2))
                s.activation(xin[:, :, TAPS - 1:], th[:, :, :], ACT.Identity, bias=1.0).then_inc(softp.sem, 1)
                act.wait_ge(u_d.sem, u_d.at(b, 1))
                s.activation(cv[:, :, :], th[:, :, :], ACT.Ln, bias=1.0).then_inc(softp.sem, 1)

            def decay(b, p, t):
                gr, c = t // NC, t % NC
                if t == 0:
                    act.wait_ge(dl_d.sem, dl_d.at(b, 1))
                    if isinstance(b, int) and b == 0:
                        act.wait_ge(k_scaled.sem, 2)
                if scan_d.at(b, t - NBUF + 1, True):
                    act.wait_ge(scan_d.sem, scan_d.at(b, t - NBUF + 1))
                for n in range(SG):
                    st = gr * SG + n
                    ins = s.activation(da[t % NBUF][:, n, 1:T], dl[p][:, c, 1:T], ACT.Exp, scale=a_neg[:, c, st:st + 1])
                ins.then_inc(decay_d.sem, 1)

            def copy_out(b, filled, bank, dst, done):
                act.wait_ge(filled.sem, filled.at(b, 1))
                s.activation(dst[:, :, :], pair(bank), ACT.Copy).then_inc(done.sem, 1)

            def k_(b):
                act.wait_ge(kT_f.sem, kT_f.at(b, 1))
                for i in range(KD):
                    ins = s.activation(kT[:, i, :], pair(QA[1])[:, i, :], ACT.Identity, bias=b_k[:, i:i + 1])
                ins.then_inc(kT_c.sem, 1)

            def q_(b):
                act.wait_ge(qT_f.sem, qT_f.at(b, 1))
                for i in range(KD):
                    ins = s.activation(qT[:, i, :], pair(QA[0])[:, i, :], ACT.Identity, bias=b_q[:, i:i + 1])
                ins.then_inc(qT_c.sem, 1)

            def softmax(b):
                act.wait_ge(max_d.sem, max_d.at(b, 2))
                for i in range(QT):
                    ins = s.activation(pe_[:, i, :], pair(QA[1])[:, i, :], ACT.Exp, bias=nmx[:, i:i + 1], scale=SCALE,
                                       accum_out=ssum[:, i:i + 1])
                ins.then_inc(p_d.sem, 1)

            def ffn1(b, f):
                act.wait_ge(h_f.sem, h_f.at(b, f + 1))
                for i in range(2):
                    c = 2 * f + i
                    ins = s.activation(hT[:, c, :], pair(QF[1 - f % 2])[:, i, :], ACT.Relu, bias=b_1[:, c:c + 1])
                ins.then_inc(h_c.sem, 1)

            def shared(b):
                act.wait_ge(sh_f.sem, sh_f.at(b, 1))
                act.wait_ge(ranked.sem, ranked.at(b, 1))
                s.activation(hth, QF[1][:, 0:T], ACT.Tanh, scale=0.5).then_inc(sh_c.sem, 1)
                s.activation(hs[:, :], QF[1][:, 0:T], ACT.Copy, scale=0.5).then_inc(sh_c.sem, 1)

            def cum_out(b):
                act.wait_ge(cum_f.sem, cum_f.at(b, 1))
                act.wait_ge(ranked.sem, ranked.at(b, 1))
                s.activation(cum[:, :, :], QF[0][:, 0:QT * NE].rearrange("p (q e) -> p q e", q=QT), ACT.Copy).then_inc(cum_c.sem, 1)

            def router(b):
                act.wait_ge(lg_c.sem, lg_c.at(b, 1))
                s.activation(key[:, :, :], key[:, :, :], ACT.Exp, scale=-1.0).then_inc(lg_e.sem, 1)

            def turn(s, p):
                for t in range(NTAU):
                    b, bp, tl = tile_at(s, p, t + LEAD)
                    if exists(b):
                        decay(b, bp, tl)
                    if exists(s + 1):
                        if t == 0:
                            x_in(s + 1, 0)
                        elif t == 1:
                            x_in(s + 1, 1)
                            first_tap(s + 1)
                        elif t == 7:
                            gates(s + 1, 1 - p)
                        elif t == 8:
                            x_proj(s + 1, 1 - p)
                        elif t == 9:
                            dt_proj(s + 1, 1 - p)
                    if exists(s - 1):
                        if t == 5:
                            copy_out(s - 1, x1T_f, QA[1], aT, x1T_c)
                        elif t == 6:
                            q_(s - 1)
                        elif t == 8:
                            softmax(s - 1)
                        elif t == 9:
                            copy_out(s - 1, pT_f, QA[0], qT, pT_c)
                        elif t == 10:
                            copy_out(s - 1, aT_f, QA[1], kT, aT_c)
                    if exists(s) and t == 12:
                        k_(s)
                    if exists(s - 2):
                        if t == 0:
                            copy_out(s - 2, x2aT_f, QF[1], fT, x2aT_c)
                        elif t == 1:
                            ffn1(s - 2, 0)
                        elif t == 3:
                            ffn1(s - 2, 1)
                            ffn1(s - 2, 2)
                        elif t == 4:
                            ffn1(s - 2, 3)
                        elif t == 13:
                            copy_out(s - 2, x2T_f, QF[1], fT, x2T_c)
                        elif t == 14:
                            router(s - 2)
                            shared(s - 2)
                    if exists(s + 1):
                        if t == 9:
                            softplus(s + 1, 1 - p)
                        elif t == 10:
                            softplus_ln(s + 1, 1 - p)
                    if exists(s - 3) and t == 0:
                        cum_out(s - 3)

            all_turns(act, turn)

        @block.tensor
        def _(pe):
            mm, tr = nc.tensor.matmul, nc.tensor.transpose

            def in_proj(b, f):
                if isinstance(b, int) and b == 0 and f == 0:
                    pe.wait_ge(w_mamba.sem, 16 * 8)
                if f == 0:
                    pe.wait_ge(xt_in.sem, xt_in.at(b, 16))
                if f < 2:
                    if proj_c.at(b - 1, 6, True):
                        pe.wait_ge(proj_c.sem, proj_c.at(b - 1, 6))
                else:
                    pe.wait_ge(proj_c.sem, proj_c.at(b, f - 1))
                for i in range(2):
                    c = 2 * f + i
                    for k in range(KD):
                        ins = mm(pair(PB[f % 2])[:, i, :], w_in[:, k, c * P:(c + 1) * P], xt[:, k, :],
                                 start=k == 0, stop=k == KD - 1)
                ins.then_inc(proj_f.sem, 1)

            def x_proj(b, p):
                pe.wait_ge(u_d.sem, u_d.at(b, 1))
                pe.wait_ge(proj_c.sem, proj_c.at(b, 3))
                for c in range(NC):
                    ins = mm(PB[0][0:XP, 0:T], w_xp[:, c, :], u[p][:, c, :], start=c == 0, stop=c == NC - 1)
                ins.then_inc(proj_f.sem, 1)

            def dt_proj(b):
                pe.wait_ge(xdb_c.sem, xdb_c.at(b, 1))
                pe.wait_ge(proj_c.sem, proj_c.at(b, 4))
                for f in range(2):
                    for i in range(2):
                        c = 2 * f + i
                        ins = mm(pair(PB[(f + 1) % 2])[:, i, :], w_dt[:, c * P:(c + 1) * P], xdb[0:R, :], start=True, stop=True)
                    ins.then_inc(proj_f.sem, 1)

            def sum_(b, t):
                gr, c = t // NC, t % NC
                if gr == 0 and c % 2 == 0:
                    if y_read.at(b - 1, c + 2, True):
                        pe.wait_ge(y_read.sem, y_read.at(b - 1, c + 2))
                n_states = SG // 2
                if t in FOLD_DVE:
                    pe.wait_ge(fold_v.sem, fold_v.at(b, FOLD_DVE.index(t) + 1))
                elif t in FOLD_POOL:
                    pe.wait_ge(fold_g.sem, fold_g.at(b, FOLD_POOL.index(t) + 1))
                else:
                    pe.wait_ge(outflow_d.sem, outflow_d.at(b, t + 1))
                    n_states = SG
                for n in range(n_states):
                    ins = mm(pair(Y[c // 2])[:, c % 2, :], ident[:, :], hb[t % NH][:, n, :],
                             start=gr == 0 and c % 2 == 0 and n == 0, stop=gr == NG - 1 and n == n_states - 1,
                             skip_group_check=True)
                ins.then_inc(sum_d.sem, 1)

            def out_proj(b, p):
                pe.wait_ge(y_d.sem, y_d.at(b, NC))
                pe.wait_ge(v_c.sem, v_c.at(b, 1))
                for q in range(QT):
                    for c in range(NC):
                        ins = mm(pair(QA[0])[:, q, :], u[p][:, c, q * P:(q + 1) * P], w_out[:, c, :], start=c == 0, stop=c == NC - 1)
                ins.then_inc(out_f.sem, 1)

            def turned(src, bank, filled):
                for q in range(QT):
                    for k in range(KD):
                        ins = tr(pair(bank)[:, k, q * P:(q + 1) * P], src[:, q, k * P:(k + 1) * P], ident[:, :])
                ins.then_inc(filled.sem, 1)

            def x1T(b, p):
                pe.wait_ge(norm_d[0].sem, norm_d[0].at(b, 1))
                pe.wait_ge(kT_c.sem, kT_c.at(b, 1))
                turned(x1[p], QA[1], x1T_f)

            def q_(b):
                pe.wait_ge(x1T_c.sem, x1T_c.at(b, 1))
                pe.wait_ge(r0_d.sem, r0_d.at(b, 1))
                for i in range(KD):
                    for k in range(KD):
                        ins = mm(pair(QA[0])[:, i, :], w_q[:, k, i * P:(i + 1) * P], aT[:, k, :], start=k == 0, stop=k == KD - 1)
                ins.then_inc(qT_f.sem, 1)

            def scores(b):
                pe.wait_ge(qT_c.sem, qT_c.at(b, 1))
                for q in range(QT):
                    for k in range(KD):
                        ins = mm(pair(QA[1])[:, q, :], qT[:, k, q * P:(q + 1) * P], kT[:, k, :], start=k == 0, stop=k == KD - 1)
                ins.then_inc(sco_f.sem, 1)

            def pT(b):
                pe.wait_ge(p_d.sem, p_d.at(b, 1))
                turned(pe_, QA[0], pT_f)

            def pv(b):
                pe.wait_ge(pT_c.sem, pT_c.at(b, 1))
                for i in range(KD):
                    for k in range(QT):
                        ins = mm(pair(QA[1])[:, i, :], vv[:, k, i * P:(i + 1) * P], qT[:, k, :], start=k == 0, stop=k == QT - 1)
                ins.then_inc(aT_f.sem, 1)

            def merge(b):
                pe.wait_ge(aT_c.sem, aT_c.at(b, 1))
                for q in range(QT):
                    for k in range(KD):
                        ins = mm(pair(QA[0])[:, q, :], kT[:, k, q * P:(q + 1) * P], w_o[:, k, :], start=k == 0, stop=k == KD - 1)
                ins.then_inc(mg_f.sem, 1)

            def k_(b):
                if isinstance(b, int) and b == 0:
                    pe.wait_ge(w_rest.sem, 16 * 21)
                pe.wait_ge(q_in.sem, q_in.at(b, 32))
                if aT_c.at(b - 1, 1, True):
                    pe.wait_ge(aT_c.sem, aT_c.at(b - 1, 1))
                for i in range(KD):
                    for k in range(KD):
                        ins = mm(pair(QA[1])[:, i, :], w_k[:, k, i * P:(i + 1) * P], ct[:, k, :], start=k == 0, stop=k == KD - 1)
                ins.then_inc(kT_f.sem, 1)

            def v_(b):
                if mg_c.at(b - 1, 1, True):
                    pe.wait_ge(mg_c.sem, mg_c.at(b - 1, 1))
                for q in range(QT):
                    for k in range(KD):
                        ins = mm(pair(QA[0])[:, q, :], ct[:, k, q * P:(q + 1) * P], w_v[:, k, :], start=k == 0, stop=k == KD - 1)
                ins.then_inc(v_f.sem, 1)

            def x2aT(b):
                pe.wait_ge(aff1_d.sem, aff1_d.at(b, 2))
                if acc_d.at(b - 1, 1, True):
                    pe.wait_ge(acc_d.sem, acc_d.at(b - 1, 1))
                turned(x2a, QF[1], x2aT_f)

            def ffn1(b, f):
                if f == 0:
                    pe.wait_ge(x2aT_c.sem, x2aT_c.at(b, 1))
                if f == 1:
                    if cum_c.at(b - 1, 1, True):
                        pe.wait_ge(cum_c.sem, cum_c.at(b - 1, 1))
                if f >= 2:
                    pe.wait_ge(h_c.sem, h_c.at(b, f - 1))
                for i in range(2):
                    c = 2 * f + i
                    for k in range(KD):
                        ins = mm(pair(QF[1 - f % 2])[:, i, :], w_1[:, k, c * P:(c + 1) * P], fT[:, k, :], start=k == 0, stop=k == KD - 1)
                ins.then_inc(h_f.sem, 1)

            def ffn2(b, q, chunks):
                pe.wait_ge(h_c.sem, h_c.at(b, 4))
                for k in chunks:
                    ins = mm(pair(QF[0])[:, q, :], hT[:, k, q * P:(q + 1) * P], w_2[:, k, :], start=k == 0, stop=k == KF - 1)
                if q == QT - 1 and k == KF - 1:
                    ins.then_inc(ff_f.sem, 1)

            def x2T(b):
                pe.wait_ge(norm_d[3].sem, norm_d[3].at(b, 1))
                turned(x2, QF[1], x2T_f)

            def router(b):
                pe.wait_ge(x2T_c.sem, x2T_c.at(b, 1))
                pe.wait_ge(ff_c.sem, ff_c.at(b, 1))
                for q in range(QT):
                    for k in range(KD):
                        ins = mm(QF[0][:, q * NE:(q + 1) * NE], fT[:, k, q * P:(q + 1) * P], w_r[:, k, :], start=k == 0, stop=k == KD - 1)
                ins.then_inc(lg_f.sem, 1)

            def shared(b):
                for k in range(KD):
                    ins = mm(QF[1][:, 0:T], ws_g[:, k, :], fT[:, k, :], start=k == 0, stop=k == KD - 1)
                ins.then_inc(sh_f.sem, 1)

            def shared_out(b):
                pe.wait_ge(hs_d.sem, hs_d.at(b, 1))
                for q in range(QT):
                    ins = mm(pair(QF[1])[:, q, :], hs[:, q * P:(q + 1) * P], ws_d[:, :], start=True, stop=True)
                ins.then_inc(so_f.sem, 1)

            def rank(b):
                pe.wait_ge(mask_d.sem, mask_d.at(b, 1))
                pe.wait_ge(lg_c.sem, lg_c.at(b, 1))
                pe.wait_ge(msum_d.sem, msum_d.at(b, 1))
                mm(QF[0][:, 0:NE], earlier[:, :], msk_b[:, 0, :], start=True, stop=False)
                mm(QF[0][:, 0:NE], ones[:, :], m_sum[:, :], start=False, stop=True)
                mm(QF[0][:, NE:2 * NE], earlier[:, :], msk_b[:, 1, :], start=True, stop=False)
                mm(QF[0][:, NE:2 * NE], ones[:, :], msk_b[:, 0, :], start=False, stop=False)
                mm(QF[0][:, NE:2 * NE], ones[:, :], m_sum[:, :], start=False, stop=True).then_inc(cum_f.sem, 1)

            def turn(s, p):
                for t in range(NTAU):
                    b, bp, tl = tile_at(s, p, t - LEAD)
                    if exists(b):
                        sum_(b, tl)
                    if exists(s + 1):
                        if t < 2:
                            in_proj(s + 1, t)
                        elif t in (4, 5):
                            in_proj(s + 1, t - 2)
                        elif t == 8:
                            x_proj(s + 1, 1 - p)
                        elif t == 9:
                            dt_proj(s + 1)
                    if exists(s - 1):
                        if t == 2:
                            out_proj(s - 1, 1 - p)
                        elif t == 5:
                            x1T(s - 1, 1 - p)
                        elif t == 6:
                            q_(s - 1)
                        elif t == 7:
                            scores(s - 1)
                        elif t == 9:
                            pT(s - 1)
                        elif t == 10:
                            pv(s - 1)
                        elif t == 11:
                            merge(s - 1)
                    if exists(s):
                        if t == 12:
                            k_(s)
                        elif t == 15:
                            v_(s)
                    if exists(s - 2):
                        if t == 0:
                            x2aT(s - 2)
                        elif t == 1:
                            ffn1(s - 2, 0)
                        elif t == 3:
                            ffn1(s - 2, 1)
                            ffn1(s - 2, 2)
                        elif t == 4:
                            ffn1(s - 2, 3)
                        elif 5 <= t < 9:
                            half = (t - 5) % 2
                            ffn2(s - 2, (t - 5) // 2, range(half * KF // 2, (half + 1) * KF // 2))
                        elif t == 13:
                            x2T(s - 2)
                        elif t == 14:
                            router(s - 2)
                            shared(s - 2)
                        elif t == 15:
                            shared_out(s - 2)
                    if exists(s - 3) and t == 0:
                        rank(s - 3)

            all_turns(pe, turn)

        @block.vector
        def _(dve):
            v = nc.vector
            dve.wait_ge(w_mamba.sem, 16 * 8)
            dve.wait_ge(k_pool.sem, 16)
            v.tensor_copy(iota_e[:, :], iota_i[:, :]).then_inc(k_conv.sem, 1)
            dve.wait_ge(k_conv.sem, 1)
            dve.sem_inc(ranked.sem, 1)
            dve.sem_inc(msum_d.sem, 1)

            def conv_(b, k):
                if k == 1:
                    dve.wait_ge(tap0.sem, tap0.at(b, 1))
                for c in range(NC):
                    if k > 1:
                        dve.wait_ge(conv.sem, conv.at(b, (k - 2) * NC + c + 1))
                    v.scalar_tensor_tensor(cv[:, c, :], xin[:, c, k:k + T], w_conv[:, c, k:k + 1], cv[:, c, :],
                                           ALU.mult, ALU.add).then_inc(conv.sem, 1)

            def softplus(b, p):
                dve.wait_ge(softp.sem, softp.at(b, 4))
                v.scalar_tensor_tensor(th[:, :, :], xin[:, :, TAPS - 1:], -1.0, th[:, :, :], ALU.add, ALU.subtract).then_inc(lost.sem, 1)

            def softplus_max(b, p):
                v.scalar_tensor_tensor(dl[p][:, :, :], dl[p][:, :, :], 0.0, cv[:, :, :], ALU.max, ALU.add).then_inc(lost.sem, 1)

            def delta(b, p):
                dve.wait_ge(lost.sem, lost.at(b, 2))
                v.tensor_tensor(dl[p][:, :, :], dl[p][:, :, :], th[:, :, :], ALU.subtract).then_inc(dl_d.sem, 1)

            def delta_u(b, p):
                dve.wait_ge(dl_d.sem, dl_d.at(b, 1))
                if inflow_d.at(b - 1, NTAU, True):
                    dve.wait_ge(inflow_d.sem, inflow_d.at(b - 1, NTAU))
                v.tensor_tensor(du[:, :, :], dl[p][:, :, :], u[p][:, :, :], ALU.mult).then_inc(du_d.sem, 1)
                if isinstance(b, int) and b == 0:
                    dve.wait_ge(a_exp.sem, 1)
                    v.tensor_scalar(a_neg[:, :, :], a_neg[:, :, :], -1.0, None, ALU.mult).then_inc(k_scaled.sem, 2)

            def scan(b, t):
                dve.wait_ge(decay_d.sem, decay_d.at(b, t + 1))
                dve.wait_ge(inflow_d.sem, inflow_d.at(b, t + 1))
                flat = hb[t % NH][:, :, :].rearrange("p n t -> p (n t)")
                v.tensor_tensor_scan(flat, da[t % NBUF][:, :, :].rearrange("p n t -> p (n t)"), flat, 0.0,
                                     ALU.mult, ALU.add).then_inc(scan_d.sem, 1)

            def outflow(b, t):
                dve.wait_ge(scan_d.sem, scan_d.at(b, t + 1))
                v.tensor_tensor(hb[t % NH][:, :, :], hb[t % NH][:, :, :], bc[(t // NC) % 2][:, 1, :, :],
                                ALU.mult).then_inc(outflow_d.sem, 1)

            def fold(b, t):
                dve.wait_ge(outflow_d.sem, outflow_d.at(b, t + 1))
                h = hb[t % NH]
                v.tensor_tensor(h[:, 0:SG // 2, :], h[:, 0:SG // 2, :], h[:, SG // 2:, :], ALU.add).then_inc(fold_v.sem, 1)

            def y(b, p, c):
                dve.wait_ge(sum_d.sem, sum_d.at(b, NTAU - NC + c // 2 * 2 + 2))
                v.scalar_tensor_tensor(u[p][:, c, :], u[p][:, c, :], d_par[:, c:c + 1], pair(Y[c // 2])[:, c % 2, :],
                                       ALU.mult, ALU.add).then_inc(y_read.sem, 1)
                dve.wait_ge(y_read.sem, y_read.at(b, c + 1))
                v.tensor_tensor(u[p][:, c, :], u[p][:, c, :], sz[p][:, c, :], ALU.mult).then_inc(y_d.sem, 1)

            def v_(b):
                dve.wait_ge(v_f.sem, v_f.at(b, 1))
                v.tensor_tensor(vv[:, :, :], pair(QA[0]), rows[:, BV, :].unsqueeze(1).to_broadcast([P, QT, D]), ALU.add).then_inc(v_c.sem, 1)

            def moments(i, src, b):
                for q in range(QT):
                    v.bn_stats(stats[:, i, q, :], src[:, q, :]).then_inc(stat1[i].sem, 1)
                dve.wait_ge(stat1[i].sem, stat1[i].at(b, QT))
                dve.sem_inc(tick, 1)
                for q in range(QT):
                    ins = v.bn_aggr(mv[:, i, q, :], stats[:, i, q, :])
                ins.then_inc(stat2[i].sem, 1)

            def normalise(b, i, src):
                dve.wait_ge(root_d[i].sem, root_d[i].at(b, 2))
                for q in range(QT):
                    ins = v.tensor_scalar(src[:, q, :], src[:, q, :], mv[:, i, q, 0:1], rs[:, i, q:q + 1], ALU.subtract, ALU.mult)
                ins.then_inc(norm_d[i].sem, 1)

            def ln0(b, p):
                dve.wait_ge(out_f.sem, out_f.at(b, 1))
                dve.wait_ge(res_in.sem, res_in.at(b, 16))
                v.tensor_tensor(x1[p][:, :, :], pair(QA[0]), x1[p][:, :, :], ALU.add).then_inc(r0_d.sem, 1)
                dve.wait_ge(r0_d.sem, r0_d.at(b, 1))
                moments(0, x1[p], b)

            def softmax(b):
                dve.wait_ge(sco_f.sem, sco_f.at(b, 1))
                v.tensor_reduce(nmx[:, :], pair(QA[1]), AX.X, ALU.max).then_inc(max_d.sem, 1)
                dve.wait_ge(max_d.sem, max_d.at(b, 1))
                v.tensor_scalar(nmx[:, :], nmx[:, :], -SCALE, None, ALU.mult).then_inc(max_d.sem, 1)

            def ln1(b):
                dve.wait_ge(p_d.sem, p_d.at(b, 1))
                v.reciprocal(rsum[:, :], ssum[:, :]).then_inc(rsum_d.sem, 1)
                dve.wait_ge(rsum_d.sem, rsum_d.at(b, 1))
                dve.wait_ge(mg_f.sem, mg_f.at(b, 1))
                dve.wait_ge(base_d.sem, base_d.at(b, 3))
                if x2aT_f.at(b - 1, 1, True):
                    dve.wait_ge(x2aT_f.sem, x2aT_f.at(b - 1, 1))
                for q in range(QT):
                    ins = v.scalar_tensor_tensor(x2a[:, q, :], pair(QA[0])[:, q, :], rsum[:, q:q + 1], base[:, q, :], ALU.mult, ALU.add)
                ins.then_inc(mg_c.sem, 1)
                dve.wait_ge(mg_c.sem, mg_c.at(b, 1))
                moments(1, x2a, b)

            def ln2(b):
                dve.wait_ge(ff_f.sem, ff_f.at(b, 1))
                dve.wait_ge(aff1_d.sem, aff1_d.at(b, 3))
                if x2_st.at(b - 1, 16, True):
                    dve.wait_ge(x2_st.sem, x2_st.at(b - 1, 16))
                v.tensor_tensor(x2[:, :, :], pair(QF[0]), base2[:, :, :], ALU.add).then_inc(ff_c.sem, 1)
                dve.wait_ge(ff_c.sem, ff_c.at(b, 1))
                moments(2, x2, b)

            def ln3(b, p):
                dve.wait_ge(aff2_d.sem, aff2_d.at(b, 2))
                v.tensor_tensor(x2[:, :, :], x2[:, :, :], x1[p][:, :, :], ALU.add).then_inc(res_d.sem, 1)
                dve.wait_ge(res_d.sem, res_d.at(b, 1))
                moments(3, x2, b)

            def router(b):
                dve.wait_ge(lg_f.sem, lg_f.at(b, 1))
                v.tensor_tensor(key[:, :, :], QF[0][:, 0:QT * NE].rearrange("p (q e) -> p q e", q=QT),
                                b_r[:, :].unsqueeze(1).to_broadcast([P, QT, NE]), ALU.add).then_inc(lg_c.sem, 1)

            def shared(b):
                dve.wait_ge(sh_c.sem, sh_c.at(b, 2))
                v.scalar_tensor_tensor(hs[:, :], hth, 1.0, hs[:, :], ALU.add, ALU.mult).then_inc(hs_d.sem, 1)

            def shared_out(b):
                dve.wait_ge(so_f.sem, so_f.at(b, 1))
                if acc_st.at(b - 1, 16, True):
                    dve.wait_ge(acc_st.sem, acc_st.at(b - 1, 16))
                dve.wait_ge(norm_d[3].sem, norm_d[3].at(b, 1))
                v.tensor_tensor(acc[:, :, :], pair(QF[1]), x2[:, :, :], ALU.add).then_inc(acc_d.sem, 1)

            def choose(b):
                dve.wait_ge(lg_e.sem, lg_e.at(b, 1))
                v.tensor_scalar(key[:, :, :], key[:, :, :], -1.0, -1.0, ALU.mult, ALU.add).then_inc(key_d.sem, 1)
                dve.wait_ge(key_d.sem, key_d.at(b, 1))
                dve.sem_inc(tick, 1)
                for q in range(QT):
                    v.max(top[:, q, :], key[:, q, :]).then_inc(pick.sem, 1)
                for q in range(QT):
                    dve.wait_ge(pick.sem, pick.at(b, q + 1))
                    dve.sem_inc(tick, 1)
                    v.match_replace(rep[:, q, :], top[:, q, :], key[:, q, :], 1.0).then_inc(pick.sem, 1)
                dve.wait_ge(pick.sem, pick.at(b, 4))
                v.tensor_scalar(msk_b[:, :, :], rep[:, :, :], 0.0, None, ALU.is_gt).then_inc(mask_d.sem, 1)

            def weigh(b):
                for q in range(QT):
                    v.max_index(ti[:, q, :], top[:, q, :], key[:, q, :]).then_inc(pick.sem, 1)
                dve.wait_ge(pick.sem, pick.at(b, 6))
                v.tensor_copy(e_st[:, :, :], ti[:, :, :]).then_inc(pick.sem, 1)
                v.reciprocal(pr[:, :, :], top[:, :, :]).then_inc(pick.sem, 1)
                dve.wait_ge(pick.sem, pick.at(b, 8))
                v.tensor_reduce(psm[:, :], pr[:, :, :], AX.X, ALU.add).then_inc(pick.sem, 1)
                dve.wait_ge(pick.sem, pick.at(b, 9))
                v.tensor_scalar(psm[:, :], psm[:, :], -1.0, 1e-9, ALU.mult, ALU.add).then_inc(pick.sem, 1)
                dve.wait_ge(pick.sem, pick.at(b, 10))
                v.reciprocal(psm[:, :], psm[:, :]).then_inc(pick.sem, 1)
                v.tensor_scalar(pr[:, :, :], pr[:, :, :], -2.5, None, ALU.mult).then_inc(pick.sem, 1)
                dve.wait_ge(pick.sem, pick.at(b, 12))
                w8 = QT * TOPK
                v.tensor_tensor(gate[:, bass.ds(b * w8, w8)].rearrange("p (q k) -> p q k", q=QT), pr[:, :, :],
                                psm[:, :].unsqueeze(2).to_broadcast([P, QT, TOPK]), ALU.mult).then_inc(pick.sem, 1)
                v.tensor_copy(sel_e[:, bass.ds(b * w8, w8)], e_st[:, :, :].rearrange("p q k -> p (q k)")).then_inc(pick.sem, 1)

            def rank(b, choices):
                for c in choices:
                    q, k = c // TOPK, c % TOPK
                    if c == 0:
                        dve.wait_ge(cum_c.sem, cum_c.at(b, 1))
                    if c >= 2:
                        dve.wait_ge(rank_s.sem, rank_s.at(b, c - 1))
                    v.scalar_tensor_tensor(junk[k % 2][:, :], iota_e[:, :], e_st[:, q, k:k + 1], cum[:, q, :],
                                           ALU.is_equal, ALU.mult, accum_out=r_st[:, q, k:k + 1]).then_inc(rank_s.sem, 1)

            def address(b):
                dve.wait_ge(rank_s.sem, rank_s.at(b, QT * TOPK))
                dve.sem_inc(ranked.sem, 1)
                v.tensor_tensor(m_sum[:, :], m_sum[:, :], msk_b[:, 0, :], ALU.add).then_inc(addr.sem, 1)
                v.scalar_tensor_tensor(ad_f[:, :, :], e_st[:, :, :], float(CAP), r_st[:, :, :], ALU.mult, ALU.add).then_inc(addr.sem, 1)
                dve.wait_ge(addr.sem, addr.at(b, 2))
                v.tensor_tensor(m_sum[:, :], m_sum[:, :], msk_b[:, 1, :], ALU.add).then_inc(msum_d.sem, 1)
                w8 = QT * TOPK
                v.tensor_copy(sel_r[:, bass.ds(b * w8, w8)], r_st[:, :, :].rearrange("p q k -> p (q k)")).then_inc(selr_d.sem, 1)
                dve.wait_ge(settled.sem, settled.at(b, 1))
                v.tensor_copy(id_st[:, :], ids_all[:, bass.ds(b * QT, QT)])
                v.tensor_copy(ad_i[:, :, :], ad_f[:, :, :]).then_inc(addr_d.sem, 1)

            def turn(s, p):
                for t in range(NTAU):
                    if exists(s - 1) and t == 8:
                        softmax(s - 1)
                    if exists(s):
                        scan(s, t)
                    b, bp, tl = tile_at(s, p, t - 1)
                    if exists(b):
                        outflow(b, tl)
                        if tl in FOLD_DVE:
                            fold(b, tl)
                    if exists(s - 1) and t < 2:
                        y(s - 1, 1 - p, 2 * t)
                        y(s - 1, 1 - p, 2 * t + 1)
                    if exists(s + 1):
                        if t == 2:
                            conv_(s + 1, 1)
                        elif t in (5, 6):
                            conv_(s + 1, t - 3)
                        elif t == 12:
                            softplus(s + 1, 1 - p)
                            softplus_max(s + 1, 1 - p)
                        elif t == 13:
                            delta(s + 1, 1 - p)
                            delta_u(s + 1, 1 - p)
                    if exists(s - 1):
                        if t == 3:
                            ln0(s - 1, 1 - p)
                        elif t == 4:
                            normalise(s - 1, 0, x1[1 - p])
                        elif t == 12:
                            ln1(s - 1)
                        elif t == 13:
                            normalise(s - 1, 1, x2a)
                    if exists(s - 2):
                        if t == 9:
                            ln2(s - 2)
                        elif t == 10:
                            normalise(s - 2, 2, x2)
                        elif t == 11:
                            ln3(s - 2, p)
                        elif t == 12:
                            normalise(s - 2, 3, x2)
                        elif t == 14:
                            router(s - 2)
                            shared(s - 2)
                        elif t == 15:
                            choose(s - 2)
                            shared_out(s - 2)
                    if exists(s) and t == 15:
                        v_(s)
                    if exists(s - 3):
                        if t == 0:
                            weigh(s - 3)
                        elif t < 4:
                            rank(s - 3, (range(0, 5), range(5, 10), range(10, 16))[t - 1])
                        if t == 3:
                            address(s - 3)

            all_turns(dve, turn)
            dve.wait_ge(selr_d.sem, selr_d.at(NB - 1, 1))

        front.close()

        cnt_f, cnt_c = sig("cnt_f"), sig("cnt_c")
        tab_s = sig("tab_s")
        tab_w, tab_in = sig("tab_w"), sig("tab_in")
        idr_in, idr_c, idT_f, ids_c = sig("idr_in"), sig("idr_c"), sig("idT_f"), sig("ids_c")
        idb_d = sig("idb_d", UNROLL)
        wt_in = [sig(f"wt_in{i}", 16) for i in range(UNROLL)]
        xg_in = [sig(f"xg_in{i}", 16) for i in range(UNROLL)]
        y_st = [sig(f"y_st{i}", 16) for i in range(UNROLL // YG)]
        xgT_f, xgT_c = sig("xgT_f", UNROLL), sig("xgT_c", UNROLL)
        up_f, up_c = sig("up_f", UNROLL), sig("up_c", UNROLL)
        dn_f, dn_c = sig("dn_f", UNROLL), sig("dn_c", UNROLL)
        slot_d = sig("slot_d", UNROLL)
        slot_i = sig("slot_i")

        slot = sb("slot", [P, NSEL])
        slot_n = sb("slot_n", [P, NSEL], I32)
        mid = ExitStack()

        def sm(name, shape, dt=FP32):
            return mid.enter_context(nc.sbuf_tensor(name, shape, dt))

        cnt_i = sm("cnt_i", [P, NE], I32)
        nblk = sm("nblk", [P, NE])
        incl = sm("incl", [P, NE])
        first = sm("first", [P, NE])
        one_f = sm("one_f", [P, NE])
        jn_i = sm("jn_i", [BJ, 3], I32)
        jn = sm("jn", [BJ, 3])
        blk_e = sm("blk_e", [BJ, 3])
        blk_b = sm("blk_b", [BJ, 3])
        blk_o = sm("blk_o", [BJ, 3])
        blk_p = sm("blk_p", [BJ, 3])
        blk_w = sm("blk_w", [BJ, 3])
        blk_i = sm("blk_i", [BJ, 2, 3], I32)
        blk_r = sm("blk_r", [BJ, 3], I32)
        last_turn = sm("last_turn", [1, 1], I32)
        idr = sm("idr", [BJ, 3, P], I32)
        idr_f = sm("idr_f", [BJ, 3, P])
        ids = sm("ids", [P, NBLK + UNROLL], I32)
        slot_j = sm("slot_j", [P, NSEL], I32)
        blk_j = sm("blk_j", [P, NSEL])
        col = sm("col", [P, NSEL])
        n_i = sm("n_i", [P, 1], I32)
        n_f = sm("n_f", [P, 3])
        junk2 = sm("junk2", [P, 3, NE])
        junk3 = sm("junk3", [P, 2, NE])
        tab = sm("tab", [1, NBLK * 2], I32)
        wt = [sm(f"wt{i}", [P, KD * INTER + D]) for i in range(UNROLL)]
        idb = [sm(f"idb{i}", [P, 1], I32) for i in range(UNROLL)]
        xg = [sm(f"xg{i}", [P, D]) for i in range(UNROLL)]
        xgT = [sm(f"xgT{i}", [P, KD, P]) for i in range(2)]
        h1 = [sm(f"h1{i}", [P, P]) for i in range(2)]
        ys = [sm(f"ys{i}", [P, YG, D]) for i in range(UNROLL // YG)]
        XT = [PB[0], PB[1]]
        UP = [Y[0], Y[1]]
        DN = [QA[0], QA[1]]
        CN = QF[0]
        TAB_DONE = 21

        def last_filled(eng):
            eng.wait_ge(tab_s.sem, TAB_DONE)
            return eng.value_load(last_turn[0:1, 0:1], min_val=SURE - 1, max_val=TURNS - 1)

        def further_turns(eng, last, body, between=None):
            with eng.Fori(1, SURE) as i:
                body(i, True)
            if between is not None:
                between()
            with eng.Fori(SURE // 4, TURNS // 4) as four:
                with eng.If(last >= four * 4):
                    with eng.Fori(0, 4) as k:
                        with eng.If(last >= four * 4 + k):
                            body(four * 4 + k, False)

        def back(i, s, lag):
            return (i, s - lag) if s >= lag else (i - 1, s - lag + UNROLL)

        block = mid.enter_context(nc.Block())

        @block.sync
        def _(sp):
            last = last_filled(sp)
            sp.dma_start(blk_dram.rearrange("f (p c) -> p f c", p=BJ), blk_i[:, :, :]).then_inc(tab_w.sem, 16)
            sp.wait_ge(tab_w.sem, 16)
            sp.dma_start(tab[0:1, :], blk_dram.rearrange("f j -> (f j)").unsqueeze(0)).then_inc(tab_in.sem, 16)
            sp.wait_ge(tab_in.sem, 16)

            column = [sp.snap(last * s_ + s_) for s_ in range(UNROLL)]

            def first_weights(s_):
                e = sp.value_load(tab[0:1, bass.ds(column[s_], 1)], min_val=0, max_val=NE - 1)
                sp.dma_start(wt[s_][:, :], a["w_moe"][bass.ds(e * P, P), :]).then_inc(wt_in[s_].sem, 16)

            def weights(i, s_):
                j = column[s_] + i
                w = nc.values_load(tab[0:1, bass.ds(j + NBLK, 1)], engines=[mybir.EngineType.SP], min_val=0, max_val=2 * NE - 1,
                                   skip_runtime_bounds_check_because="the table holds experts, and those plus NE")
                e = nc.s_assert_within(w, 0, NE - 1, skip_runtime_bounds_check_because="the copy is left out from NE on")
                sp.wait_ge(dn_f.sem, dn_f.at(i - 1, s_ + 1))
                sp.sem_inc(tick, 1)
                sp.dma_start(wt[s_][:, :], a["w_moe"][bass.ds(e * P, P), :], cond=w < NE).then_inc(wt_in[s_].sem, 16)

            def store(i, h):
                sp.wait_ge(dn_c.sem, dn_c.at(i, (h + 1) * YG))
                sp.sem_inc(tick, 1)
                rows_ = y_dram[bass.ds((i * UNROLL + h * YG) * P, YG * P), :]
                sp.dma_start(rows_.rearrange("(j p) d -> p j d", p=P), ys[h][:, :, :]).then_inc(y_st[h].sem, 16)

            def body(i, sure):
                for s_ in range(UNROLL):
                    weights(i, s_)
                    if s_ % YG == YG - 1:
                        store(i - 1, s_ // YG)

            for s_ in range(UNROLL):
                first_weights(s_)
            further_turns(sp, last, body)
            for h in range(UNROLL // YG):
                store(last, h)
            for h in range(UNROLL // YG):
                sp.wait_ge(y_st[h].sem, y_st[h].at(last, 16))
                sp.sem_inc(tick, 1)

        @block.gpsimd
        def _(pool):
            g = nc.gpsimd
            g.iota(jn_i[:, :], pattern=[[1, 3]], base=0, channel_multiplier=3).then_inc(cnt_c.sem, 1)
            last = last_filled(pool)
            by_block = tok_dram.rearrange("(r p) o -> r (p o)", p=P)
            for c in range(3):
                g.indirect_dma_start(idr[:, c, :], None, by_block,
                                     bass.IndirectOffsetOnAxis(ap=blk_r[:, c:c + 1], axis=0)).then_inc(idr_in.sem, 16)

            def gather(i, s_):
                pool.wait_ge(idb_d.sem, idb_d.at(i, s_ + 1))
                if xgT_f.at(i - 1, s_ + 1, True):
                    pool.wait_ge(xgT_f.sem, xgT_f.at(i - 1, s_ + 1))
                pool.sem_inc(tick, 1)
                g.indirect_dma_start(xg[s_][:, :], None, x2_dram,
                                     bass.IndirectOffsetOnAxis(ap=idb[s_][:, 0:1], axis=0)).then_inc(xg_in[s_].sem, 16)

            def body(i, sure):
                for s_ in range(UNROLL):
                    gather(i, s_)

            body(0, True)
            further_turns(pool, last, body)

        @block.tensor
        def _(pe):
            mm = nc.tensor.matmul
            mm(CN[:, 0:NE], ones[:, :], m_sum[:, :], start=True, stop=True).then_inc(cnt_f.sem, 1)
            last = last_filled(pe)
            pe.wait_ge(idr_c.sem, 1)
            for c in range(3):
                ins = nc.tensor.transpose(QF[1][:, c * BJ:(c + 1) * BJ], idr_f[:, c, :], ident[0:BJ, 0:BJ])
            ins.then_inc(idT_f.sem, 1)

            def turned(i, s_):
                pe.wait_ge(xg_in[s_].sem, xg_in[s_].at(i, 16))
                if xgT_c.at(i, s_ - 1, True):
                    pe.wait_ge(xgT_c.sem, xgT_c.at(i, s_ - 1))
                for k in range(KD):
                    ins = nc.tensor.transpose(XT[s_ % 2][:, k * P:(k + 1) * P], xg[s_][:, k * P:(k + 1) * P], ident[:, :])
                ins.then_inc(xgT_f.sem, 1)

            def up(i, s_):
                pe.wait_ge(xgT_c.sem, xgT_c.at(i, s_ + 1))
                pe.wait_ge(wt_in[s_].sem, wt_in[s_].at(i, 16))
                if up_c.at(i, s_ - 1, True):
                    pe.wait_ge(up_c.sem, up_c.at(i, s_ - 1))
                for k in range(KD):
                    ins = mm(UP[s_ % 2][:, 0:P], wt[s_][:, k * INTER:(k + 1) * INTER], xgT[s_ % 2][:, k, :], start=k == 0, stop=k == KD - 1)
                ins.then_inc(up_f.sem, 1)

            def down(i, s_):
                pe.wait_ge(up_c.sem, up_c.at(i, s_ + 1))
                if dn_c.at(i, s_ - 1, True):
                    pe.wait_ge(dn_c.sem, dn_c.at(i, s_ - 1))
                mm(DN[s_ % 2][:, 0:D], h1[s_ % 2][:, :], wt[s_][:, KD * INTER:], start=True, stop=True).then_inc(dn_f.sem, 1)

            def body(i, sure):
                first_turn = isinstance(i, int)
                for s_ in range(UNROLL):
                    turned(i, s_)
                    if not (first_turn and s_ < 1):
                        up(*back(i, s_, 1))
                    if not (first_turn and s_ < 2):
                        down(*back(i, s_, 2))

            body(0, True)
            further_turns(pe, last, body)
            up(last, UNROLL - 1)
            down(last, UNROLL - 2)
            down(last, UNROLL - 1)

        @block.scalar
        def _(act):
            s = nc.scalar
            last = last_filled(act)

            def silu(i, s_):
                act.wait_ge(up_f.sem, up_f.at(i, s_ + 1))
                if dn_f.at(i, s_ - 1, True):
                    act.wait_ge(dn_f.sem, dn_f.at(i, s_ - 1))
                s.activation(h1[s_ % 2][:, :], UP[s_ % 2][:, 0:P], ACT.Silu).then_inc(up_c.sem, 1)

            def copy_y(i, s_):
                h = s_ // YG
                act.wait_ge(dn_f.sem, dn_f.at(i, s_ + 1))
                if s_ % YG == 0:
                    if y_st[h].at(i - 1, 16, True):
                        act.wait_ge(y_st[h].sem, y_st[h].at(i - 1, 16))
                s.activation(ys[h][:, s_ % YG, :], DN[s_ % 2][:, 0:D], ACT.Copy).then_inc(dn_c.sem, 1)

            def body(i, sure):
                first_turn = isinstance(i, int)
                for s_ in range(UNROLL):
                    if not (first_turn and s_ < 1):
                        silu(*back(i, s_, 1))
                    if not (first_turn and s_ < 2):
                        copy_y(*back(i, s_, 2))

            body(0, True)
            further_turns(act, last, body)
            silu(last, UNROLL - 1)
            copy_y(last, UNROLL - 2)
            copy_y(last, UNROLL - 1)

        @block.vector
        def _(dve):
            v = nc.vector
            steps = [0]

            def link(ins):
                steps[0] += 1
                ins.then_inc(tab_s.sem, 1)
                dve.wait_ge(tab_s.sem, steps[0])

            dve.wait_ge(cnt_f.sem, 1)
            dve.wait_ge(cnt_c.sem, 1)
            link(v.tensor_scalar(cnt_i[:, :], CN[:, 0:NE], float(P - 1), None, ALU.add))
            link(v.tensor_scalar(cnt_i[:, :], cnt_i[:, :], 7, None, ALU.arith_shift_right))
            link(v.tensor_copy(nblk[:, :], cnt_i[:, :]))
            link(v.memset(one_f[:, :], 1.0))
            link(v.tensor_copy(jn[:, :], jn_i[:, :]))
            link(v.tensor_tensor_scan(incl[:, :], one_f[:, :], nblk[:, :], 0.0, ALU.mult, ALU.add))
            link(v.tensor_tensor(first[:, :], incl[:, :], nblk[:, :], ALU.subtract))
            for c in range(3):
                v.scalar_tensor_tensor(junk2[0:BJ, c, :], incl[0:BJ, :], jn[:, c:c + 1], one_f[0:BJ, :], ALU.is_le, ALU.mult,
                                       accum_out=blk_e[:, c:c + 1])
            link(v.tensor_scalar(first[:, :], first[:, :], float(P), None, ALU.mult))
            for c in range(3):
                ins = v.scalar_tensor_tensor(junk2[0:BJ, c, :], incl[0:BJ, :], jn[:, c:c + 1], nblk[0:BJ, :], ALU.is_le, ALU.mult,
                                             accum_out=blk_b[:, c:c + 1])
            link(ins)
            link(v.tensor_tensor(blk_b[:, :], jn[:, :], blk_b[:, :], ALU.subtract))
            link(v.scalar_tensor_tensor(blk_o[:, :], blk_e[:, :], float(CAP // P), blk_b[:, :], ALU.mult, ALU.add))
            link(v.tensor_scalar(blk_r[:, :], blk_o[:, :], float(NE * CAP // P - 1), None, ALU.min))
            link(v.tensor_scalar(jn[:, :], jn[:, :], -1.0, None, ALU.add))
            for c in range(3):
                ins = v.scalar_tensor_tensor(junk2[0:BJ, c, :], incl[0:BJ, :], jn[:, c:c + 1], one_f[0:BJ, :], ALU.is_le, ALU.mult,
                                             accum_out=blk_p[:, c:c + 1])
            link(ins)
            link(v.tensor_scalar(blk_e[:, :], blk_e[:, :], float(NE - 1), None, ALU.min))
            link(v.tensor_tensor(blk_w[:, :], blk_p[:, :], blk_e[:, :], ALU.is_ge))
            link(v.scalar_tensor_tensor(blk_w[:, :], blk_w[:, :], float(NE), blk_e[:, :], ALU.mult, ALU.add))
            link(v.tensor_copy(blk_i[:, 0, :], blk_e[:, :]))
            link(v.tensor_copy(blk_i[:, 1, :], blk_w[:, :]))
            link(v.tensor_scalar(last_turn[:, :], incl[0:1, NE - 1:NE], -1.0, None, ALU.add))
            link(v.tensor_scalar(last_turn[:, :], last_turn[:, :], 3, None, ALU.arith_shift_right))
            assert steps[0] == TAB_DONE and UNROLL == 1 << 3 and P == 1 << 7
            last = last_filled(dve)
            dve.wait_ge(idr_in.sem, 16 * 3)
            v.tensor_copy(idr_f[:, :, :], idr[:, :, :]).then_inc(idr_c.sem, 1)
            v.memset(ids[:, NBLK:], 0).then_inc(ids_c.sem, 1)
            dve.wait_ge(idT_f.sem, 1)
            v.tensor_copy(ids[:, 0:NBLK].rearrange("p (j c) -> p c j", c=3),
                          QF[1][:, 0:NBLK].rearrange("p (c j) -> p c j", c=3)).then_inc(ids_c.sem, 1)
            dve.wait_ge(ids_c.sem, 2)
            for s_ in range(UNROLL):
                v.tensor_copy(idb[s_][:, :], ids[:, bass.ds(last * s_ + s_, 1)]).then_inc(idb_d.sem, 1)

            def body(i, sure):
                for s_ in range(UNROLL):
                    dve.wait_ge(xgT_f.sem, xgT_f.at(i, s_ + 1))
                    if up_f.at(i, s_ - 1, True):
                        dve.wait_ge(up_f.sem, up_f.at(i, s_ - 1))
                    v.tensor_copy(xgT[s_ % 2][:, :, :], XT[s_ % 2][:, 0:KD * P].rearrange("p (k t) -> p k t", k=KD)).then_inc(xgT_c.sem, 1)
                    dve.wait_ge(xg_in[s_].sem, xg_in[s_].at(i, 16))
                    v.tensor_copy(idb[s_][:, :], ids[:, bass.ds(last * s_ + (i + (s_ + 1)), 1)]).then_inc(idb_d.sem, 1)
                    if sure:
                        f = i * UNROLL + s_
                        if slot_d.at(i, s_ - 1, True):
                            dve.wait_ge(slot_d.sem, slot_d.at(i, s_ - 1))
                        v.scalar_tensor_tensor(junk3[:, s_ % 2, :], iota_e[:, :], sel_e[:, bass.ds(f, 1)], first[:, :],
                                               ALU.is_equal, ALU.mult, accum_out=slot[:, bass.ds(f, 1)]).then_inc(slot_d.sem, 1)

            def places():
                dve.wait_ge(slot_d.sem, slot_d.at(SURE - 1, UNROLL))
                v.tensor_tensor(slot[:, :], slot[:, :], sel_r[:, :], ALU.add).then_inc(slot_i.sem, 1)
                v.tensor_scalar(n_f[:, 0:1], incl[:, NE - 1:NE], -1.0, None, ALU.add).then_inc(slot_i.sem, 1)
                dve.wait_ge(slot_i.sem, 2)
                v.tensor_copy(slot_n[:, :], slot[:, :]).then_inc(slot_i.sem, 1)
                v.tensor_copy(n_i[:, :], n_f[:, 0:1]).then_inc(slot_i.sem, 1)
                dve.wait_ge(slot_i.sem, 4)
                v.tensor_scalar(slot_j[:, :], slot_n[:, :], 7, None, ALU.arith_shift_right).then_inc(slot_i.sem, 1)
                v.tensor_scalar(n_i[:, :], n_i[:, :], 3, None, ALU.arith_shift_right).then_inc(slot_i.sem, 1)
                dve.wait_ge(slot_i.sem, 6)
                v.tensor_copy(blk_j[:, :], slot_j[:, :]).then_inc(slot_i.sem, 1)
                v.tensor_copy(n_f[:, 0:1], n_i[:, :]).then_inc(slot_i.sem, 1)
                dve.wait_ge(slot_i.sem, 8)
                v.tensor_scalar(n_f[:, 0:1], n_f[:, 0:1], 1.0, None, ALU.add).then_inc(slot_i.sem, 1)
                v.scalar_tensor_tensor(slot[:, :], blk_j[:, :], -float(P), slot[:, :], ALU.mult, ALU.add).then_inc(slot_i.sem, 1)
                dve.wait_ge(slot_i.sem, 10)
                v.tensor_scalar(n_f[:, 1:2], n_f[:, 0:1], float(UNROLL), -1.0, ALU.mult, ALU.add).then_inc(slot_i.sem, 1)
                v.tensor_scalar(col[:, :], blk_j[:, :], n_f[:, 0:1], None, ALU.is_ge).then_inc(slot_i.sem, 1)
                dve.wait_ge(slot_i.sem, 12)
                for m in range(2, UNROLL):
                    v.tensor_scalar(n_f[:, 2:3], n_f[:, 0:1], float(m), None, ALU.mult).then_inc(slot_i.sem, 1)
                    dve.wait_ge(slot_i.sem, 12 + 2 * (m - 2) + 1)
                    v.scalar_tensor_tensor(col[:, :], blk_j[:, :], n_f[:, 2:3], col[:, :], ALU.is_ge, ALU.add).then_inc(slot_i.sem, 1)
                    dve.wait_ge(slot_i.sem, 12 + 2 * (m - 2) + 2)
                n0 = 12 + 2 * (UNROLL - 2)
                v.tensor_scalar(col[:, :], col[:, :], n_f[:, 1:2], None, ALU.mult).then_inc(slot_i.sem, 1)
                dve.wait_ge(slot_i.sem, n0 + 1)
                v.scalar_tensor_tensor(blk_j[:, :], blk_j[:, :], float(UNROLL), col[:, :], ALU.mult, ALU.subtract).then_inc(slot_i.sem, 1)
                dve.wait_ge(slot_i.sem, n0 + 2)
                v.scalar_tensor_tensor(slot[:, :], blk_j[:, :], float(P), slot[:, :], ALU.mult, ALU.add).then_inc(slot_i.sem, 1)
                dve.wait_ge(slot_i.sem, n0 + 3)
                v.tensor_copy(slot_n[:, :], slot[:, :]).then_inc(slot_i.sem, 1)
                dve.wait_ge(slot_i.sem, n0 + 4)

            body(0, True)
            further_turns(dve, last, body, places)
            dve.wait_ge(idb_d.sem, UNROLL * (SURE + 1))

        mid.close()

        gat_in = [sig(f"gat_in{i}", 8 * TOPK) for i in range(2)]
        acc_in = [sig(f"acc_in{i}", 8) for i in range(2)]
        out_st = [sig(f"out_st{i}", 8) for i in range(2)]
        add_s = sig("add_s", TOPK)
        sidx = sig("sidx")
        bst, bag = sig("bst"), sig("bag")
        var_d, std_d, rstd_d, fin_d = sig("var_d"), sig("std_d"), sig("rstd_d"), sig("fin_d")
        end = ExitStack()

        def se(name, shape, dt=FP32):
            return end.enter_context(nc.sbuf_tensor(name, shape, dt))

        G = [se(f"G{i}", [P, TOPK, D]) for i in range(2)]
        si = [se(f"si{i}", [P, TOPK], I32) for i in range(2)]
        ac = [se(f"ac{i}", [P, D]) for i in range(2)]
        bs = se("bs", [P, 6])
        bm = se("bm", [P, 2])
        vr = se("vr", [P, 1])
        sd = se("sd", [P, 1])
        rd = se("rd", [P, 1])

        def tiles(eng, body):
            for t in range(2):
                body(t, t)
            with eng.Fori(1, NTILE // 2) as i:
                for p in range(2):
                    body(i * 2 + p, p)

        block = end.enter_context(nc.Block())

        @block.sync
        def _(sp):
            def body(t, p):
                if out_st[p].at(t - p - 2, 16, True):
                    sp.wait_ge(out_st[p].sem, out_st[p].at(t - p - 2, 16))
                sp.dma_start(ac[p][:, :], acc_dram[bass.ds(t * P, P), :]).then_inc(acc_in[p].sem, 16)
                if isinstance(t, int) and t == 0:
                    return
                if fin_d.at(t - 1, 1, True):
                    sp.wait_ge(fin_d.sem, fin_d.at(t - 1, 1))
                sp.dma_start(out[bass.ds((t - 1) * P, P), :], ac[1 - p][:, :]).then_inc(out_st[1 - p].sem, 16)

            tiles(sp, body)
            sp.wait_ge(fin_d.sem, fin_d.at(NTILE - 1, 1))
            sp.dma_start(out[(NTILE - 1) * P:, :], ac[(NTILE - 1) % 2][:, :]).then_inc(out_st[1].sem, 16)
            for p in range(2):
                sp.wait_ge(out_st[p].sem, out_st[p].at(NTILE - 2, 16))

        @block.gpsimd
        def _(pool):
            def body(t, p):
                pool.wait_ge(sidx.sem, sidx.at(t, 1))
                if add_s.at(t - 2, TOPK, True):
                    pool.wait_ge(add_s.sem, add_s.at(t - 2, TOPK))
                pool.sem_inc(tick, 1)
                for k in range(TOPK):
                    nc.gpsimd.indirect_dma_start(G[p][:, k, :], None, y_dram,
                                                 bass.IndirectOffsetOnAxis(ap=si[p][:, k:k + 1], axis=0)).then_inc(gat_in[p].sem, 16)

            tiles(pool, body)

        @block.scalar
        def _(act):
            def body(t, p):
                act.wait_ge(var_d.sem, var_d.at(t, 1))
                nc.scalar.activation(sd[:, :], vr[:, :], ACT.Sqrt).then_inc(std_d.sem, 1)

            tiles(act, body)

        @block.vector
        def _(dve):
            v = nc.vector

            def body(t, p):
                if gat_in[p].at(t - p - 2, 16 * TOPK, True):
                    dve.wait_ge(gat_in[p].sem, gat_in[p].at(t - p - 2, 16 * TOPK))
                v.tensor_copy(si[p][:, :], slot_n[:, bass.ds(t * TOPK, TOPK)]).then_inc(sidx.sem, 1)

            def add(t, p):
                dve.wait_ge(acc_in[p].sem, acc_in[p].at(t - p, 16))
                dve.wait_ge(gat_in[p].sem, gat_in[p].at(t - p, 16 * TOPK))
                for k in range(TOPK):
                    dve.wait_ge(add_s.sem, add_s.at(t, k))
                    v.scalar_tensor_tensor(ac[p][:, :], G[p][:, k, :], gate[:, bass.ds(t * TOPK + k, 1)], ac[p][:, :],
                                           ALU.mult, ALU.add).then_inc(add_s.sem, 1)
                dve.wait_ge(add_s.sem, add_s.at(t, TOPK))
                v.bn_stats(bs[:, :], ac[p][:, :]).then_inc(bst.sem, 1)
                dve.wait_ge(bst.sem, bst.at(t, 1))
                dve.sem_inc(tick, 1)
                v.bn_aggr(bm[:, :], bs[:, :]).then_inc(bag.sem, 1)
                dve.wait_ge(bag.sem, bag.at(t, 1))
                v.tensor_scalar(vr[:, :], bm[:, 1:2], LN_EPS, None, ALU.add).then_inc(var_d.sem, 1)
                dve.wait_ge(std_d.sem, std_d.at(t, 1))
                v.reciprocal(rd[:, :], sd[:, :]).then_inc(rstd_d.sem, 1)
                dve.wait_ge(rstd_d.sem, rstd_d.at(t, 1))
                v.tensor_scalar(ac[p][:, :], ac[p][:, :], bm[:, 0:1], rd[:, 0:1], ALU.subtract, ALU.mult).then_inc(fin_d.sem, 1)

            body(0, 0)
            body(1, 1)
            add(0, 0)
            body(2, 0)
            add(1, 1)
            body(3, 1)
            with dve.Fori(1, NTILE // 2 - 1) as i:
                for p in range(2):
                    add(i * 2 + p, p)
                    body(i * 2 + (p + 2), p)
            for p in range(2):
                add(NTILE - 2 + p, p)

        end.close()


def chunked(w, p=128):
    n = w.shape[0] // p
    return np.ascontiguousarray(w.reshape(n, p, *w.shape[1:]).swapaxes(0, 1))


def kernel(**inputs):
    import concourse.bacc as _bacc
    from concourse import mybir as _mybir
    from concourse.bass_utils import run_bass_kernel_spmd as _run

    g = {k: np.asarray(v) for k, v in inputs.items()}
    m = {k[len("L0_attn_h_"):]: v for k, v in g.items() if k.startswith("L0_attn_h_")}
    x = {k[len("L0_xattn_"):]: v for k, v in g.items() if k.startswith("L0_xattn_")}
    f = {k[len("L0_ffn_"):]: v for k, v in g.items() if k.startswith("L0_ffn_")}
    xs, cs = g["x"].reshape(NT, D), g["ctx_1024"].reshape(NT, D)
    xp = m["x_proj_w"]
    xp = np.concatenate([xp[:R], np.zeros((R, DI), xp.dtype), xp[R:]], 0)
    moe = np.concatenate([f["w_gate"].reshape(NE, INTER, KD, P).transpose(0, 3, 2, 1).reshape(NE, P, KD * INTER),
                          f["w_down"].transpose(0, 2, 1)], 2).reshape(NE * P, KD * INTER + D)
    arrays = {
        "x": xs, "xT": chunked(xs.T), "c": cs, "cT": chunked(cs.T),
        "w_in": chunked(m["in_proj_w"].T), "conv_w": chunked(m["conv_w"]), "conv_b": chunked(m["conv_b"]),
        "w_xp": chunked(xp.T), "w_dt": m["dt_proj_w"].T, "dt_b": chunked(m["dt_proj_b"]),
        "A_log": chunked(m["A_log"]), "D": chunked(m["D_param"]), "w_out": chunked(m["out_proj_w"].T),
        "w_q": chunked(x["Wq"]), "w_k": chunked(x["Wk"]), "w_v": chunked(x["Wv"]), "w_o": chunked(x["Wo"]),
        "b_q": chunked(x["bq"]), "b_k": chunked(x["bk"]), "w_1": chunked(x["W1"]), "b_1": chunked(x["b1"]),
        "w_2": chunked(x["W2"]), "w_r": chunked(f["router_w"].T), "b_r": f["expert_bias"],
        "ws_g": chunked(f["w_gate_shared"].T), "ws_d": f["w_down_shared"].T, "w_moe": moe,
    } | {n: x[n] for n in ROWS}
    arrays = {k: np.ascontiguousarray(v) for k, v in arrays.items()}
    nc = _bacc.Bacc("TRN2", target_bir_lowering=False, num_devices=1)
    aps = {k: nc.dram_tensor(f"in_{k}", v.shape, _mybir.dt.from_np(v.dtype), kind="ExternalInput").ap()
           for k, v in arrays.items()}
    out = nc.dram_tensor("out", (NT, D), FP32, kind="ExternalOutput").ap()
    decoder_kernel(nc, aps, out)
    r = _run(nc, [{f"in_{k}": v for k, v in arrays.items()}], core_ids=[0])
    return r.results[0]["out"].reshape(NB, T, D)
```
